# Optimizing a Trainium2 kernel written in Bass

```python
import numpy as np
import jax
import jax.numpy as jnp

def _softmax(x, axis=-1):
    return jax.nn.softmax(x, axis=axis)

def _gelu(x):
    return jax.nn.gelu(x, approximate=True)

def _silu(x):
    return jax.nn.silu(x)

def _sigmoid(x):
    return jax.nn.sigmoid(x)

def _layernorm(x, axis=-1, eps=1e-05):
    m = jnp.mean(x, axis=axis, keepdims=True)
    v = jnp.var(x, axis=axis, keepdims=True)
    return (x - m) / jnp.sqrt(v + eps)

def _scatter_add(tgt, idx, src, axis=0):
    return tgt.at[idx].add(src)

def _segment_sum(src, seg, n):
    return jax.ops.segment_sum(src, seg, n)
kernel_name = 'mk_xattn_seq_d2_seqx_r8_72f5ce'

def setup_inputs(seed: int=0):
    np.random.seed(seed)
    _w = jnp.asarray

    def _rec_inputs():
        import jax
        import jax.numpy as jnp
        _rk = jax.random.key(seed)
        x = -0.0001233 + 1 * jax.random.normal(jax.random.fold_in(_rk, 1), (64, 128, 160), jnp.float32)
        _lenS = 128 - jax.random.randint(jax.random.fold_in(_rk, 7), (64,), 0, max(1, 128 // 4) + 1, jnp.int32)
        _lenS2 = 120 - jax.random.randint(jax.random.fold_in(_rk, 8), (64,), 0, max(1, 120 // 4) + 1, jnp.int32)
        _ctx_768P = jax.random.normal(jax.random.fold_in(_rk, 11), (64, 16, 96), jnp.float32)
        _ctx_768c = jax.random.dirichlet(jax.random.fold_in(_rk, 511), 0.3 * jnp.ones((16,), jnp.float32), (64, 120))
        _ctx_768t = jnp.einsum('bsk,bkd->bsd', _ctx_768c, _ctx_768P)
        _ctx_768t = _ctx_768t * jax.lax.rsqrt(jnp.mean(jnp.square(_ctx_768t)) + 1e-12) * 0.953939
        ctx_768 = 0.00272024 + 0.999456 * (_ctx_768t + 0.3 * jax.random.normal(jax.random.fold_in(_rk, 611), (64, 120, 96), jnp.float32))
        return (x, ctx_768)
    x, ctx_768 = _rec_inputs()

    def _L0_xattn_setup():
        import jax, jax.numpy as jnp
        import numpy as np
        D = 160
        H = 20
        DH = D // H
        CTX = 96
        FF_IN = 4 * D
        EPS = 1e-05

        def _ln(x, g, b):
            m = jnp.mean(x, axis=-1, keepdims=True)
            v = jnp.mean(jnp.square(x - m), axis=-1, keepdims=True)
            return (x - m) * jax.lax.rsqrt(v + EPS) * g + b

        def _attn(x, ctx, wq, wk, wv, wo, bo, heads):
            b, n, _ = x.shape
            j = ctx.shape[1]
            dh = wq.shape[1] // heads
            scale = dh ** (-0.5)
            q = (x @ wq).reshape(b, n, heads, dh).transpose(0, 2, 1, 3)
            k = (ctx @ wk).reshape(b, j, heads, dh).transpose(0, 2, 1, 3)
            v = (ctx @ wv).reshape(b, j, heads, dh).transpose(0, 2, 1, 3)
            sim = jnp.einsum('bhid,bhjd->bhij', q, k) * scale
            a = jax.nn.softmax(sim, axis=-1)
            out = jnp.einsum('bhij,bhjd->bhid', a, v)
            out = out.transpose(0, 2, 1, 3).reshape(b, n, heads * dh)
            return out @ wo + bo
        key = jax.random.key(seed)
        ks = jax.random.split(key, 24)
        r = lambda k, shp, s: jax.random.normal(k, shp, dtype=jnp.float32) * s
        d = {'x': r(ks[0], (8, 128, D), 1.0), 'context': r(ks[1], (8, 77, CTX), 1.0), 'heads': H, 'n1_g': jnp.ones((D,), jnp.float32), 'n1_b': jnp.zeros((D,), jnp.float32), 'q1': r(ks[2], (D, D), D ** (-0.5)), 'k1': r(ks[3], (D, D), D ** (-0.5)), 'v1': r(ks[4], (D, D), D ** (-0.5)), 'o1_w': r(ks[5], (D, D), D ** (-0.5)), 'o1_b': jnp.zeros((D,), jnp.float32), 'n2_g': jnp.ones((D,), jnp.float32), 'n2_b': jnp.zeros((D,), jnp.float32), 'q2': r(ks[6], (D, D), D ** (-0.5)), 'k2': r(ks[7], (CTX, D), CTX ** (-0.5)), 'v2': r(ks[8], (CTX, D), CTX ** (-0.5)), 'o2_w': r(ks[9], (D, D), D ** (-0.5)), 'o2_b': jnp.zeros((D,), jnp.float32), 'n3_g': jnp.ones((D,), jnp.float32), 'n3_b': jnp.zeros((D,), jnp.float32), 'ff_w1': r(ks[10], (D, 2 * FF_IN), D ** (-0.5)), 'ff_b1': jnp.zeros((2 * FF_IN,), jnp.float32), 'ff_w2': r(ks[11], (FF_IN, D), FF_IN ** (-0.5)), 'ff_b2': jnp.zeros((D,), jnp.float32)}
        return d
    _L0_xattn_all = _L0_xattn_setup()
    _L0_xattn_in = {k: v for k, v in _L0_xattn_all.items() if k in ('n1_g', 'n1_b', 'q1', 'k1', 'v1', 'o1_w', 'o1_b', 'n2_g', 'n2_b', 'q2', 'k2', 'v2', 'o2_w', 'o2_b', 'n3_g', 'n3_b', 'ff_w1', 'ff_b1', 'ff_w2', 'ff_b2')}
    del _L0_xattn_all

    def _L1_xattn_setup():
        import jax, jax.numpy as jnp
        import numpy as np
        HEADS = 8
        NUM_TOKENS = 4
        CROSS_ATTENTION_DIM = 96

        def _mha(q, k, v, heads=HEADS):
            B, Sq, H = q.shape
            Sk = k.shape[1]
            d = H // heads
            qh = q.reshape(B, Sq, heads, d).transpose(0, 2, 1, 3)
            kh = k.reshape(B, Sk, heads, d).transpose(0, 2, 1, 3)
            vh = v.reshape(B, Sk, heads, d).transpose(0, 2, 1, 3)
            scores = jnp.einsum('bhqd,bhkd->bhqk', qh, kh) * jnp.asarray(d, q.dtype) ** (-0.5)
            probs = jax.nn.softmax(scores, axis=-1)
            out = jnp.einsum('bhqk,bhkd->bhqd', probs, vh)
            return out.transpose(0, 2, 1, 3).reshape(B, Sq, H)
        key = jax.random.key(seed)
        ks = jax.random.split(key, 10)
        B, S, H, CAD, T = (4, 128, 160, CROSS_ATTENTION_DIM, NUM_TOKENS)
        sc = 0.02
        return {'hidden_states': jax.random.normal(ks[0], (B, S, H), jnp.float32), 'encoder_hidden_states': jax.random.normal(ks[1], (B, 77 + T, CAD), jnp.float32), 'Wq': jax.random.normal(ks[2], (H, H), jnp.float32) * sc, 'Wk': jax.random.normal(ks[3], (CAD, H), jnp.float32) * sc, 'Wv': jax.random.normal(ks[4], (CAD, H), jnp.float32) * sc, 'Wq_ca': jax.random.normal(ks[5], (T, H), jnp.float32) * sc, 'Wk_ca': jax.random.normal(ks[6], (CAD, H), jnp.float32) * sc, 'Wv_ca': jax.random.normal(ks[7], (CAD, H), jnp.float32) * sc, 'Wout': jax.random.normal(ks[8], (H, H), jnp.float32) * sc, 'b_out': jnp.zeros((H,), jnp.float32)}
    _L1_xattn_all = _L1_xattn_setup()
    _L1_xattn_in = {k: v for k, v in _L1_xattn_all.items() if k in ('Wq', 'Wk', 'Wv', 'Wq_ca', 'Wk_ca', 'Wv_ca', 'Wout', 'b_out')}
    del _L1_xattn_all
    return {'x': x, 'ctx_768': ctx_768, 'L0_xattn_n1_g': _L0_xattn_in['n1_g'], 'L0_xattn_n1_b': _L0_xattn_in['n1_b'], 'L0_xattn_q1': _L0_xattn_in['q1'], 'L0_xattn_k1': _L0_xattn_in['k1'], 'L0_xattn_v1': _L0_xattn_in['v1'], 'L0_xattn_o1_w': _L0_xattn_in['o1_w'], 'L0_xattn_o1_b': _L0_xattn_in['o1_b'], 'L0_xattn_n2_g': _L0_xattn_in['n2_g'], 'L0_xattn_n2_b': _L0_xattn_in['n2_b'], 'L0_xattn_q2': _L0_xattn_in['q2'], 'L0_xattn_k2': _L0_xattn_in['k2'], 'L0_xattn_v2': _L0_xattn_in['v2'], 'L0_xattn_o2_w': _L0_xattn_in['o2_w'], 'L0_xattn_o2_b': _L0_xattn_in['o2_b'], 'L0_xattn_n3_g': _L0_xattn_in['n3_g'], 'L0_xattn_n3_b': _L0_xattn_in['n3_b'], 'L0_xattn_ff_w1': _L0_xattn_in['ff_w1'], 'L0_xattn_ff_b1': _L0_xattn_in['ff_b1'], 'L0_xattn_ff_w2': _L0_xattn_in['ff_w2'], 'L0_xattn_ff_b2': _L0_xattn_in['ff_b2'], 'L1_xattn_Wq': _L1_xattn_in['Wq'], 'L1_xattn_Wk': _L1_xattn_in['Wk'], 'L1_xattn_Wv': _L1_xattn_in['Wv'], 'L1_xattn_Wq_ca': _L1_xattn_in['Wq_ca'], 'L1_xattn_Wk_ca': _L1_xattn_in['Wk_ca'], 'L1_xattn_Wv_ca': _L1_xattn_in['Wv_ca'], 'L1_xattn_Wout': _L1_xattn_in['Wout'], 'L1_xattn_b_out': _L1_xattn_in['b_out']}

def reference(x, ctx_768, L0_xattn_n1_g, L0_xattn_n1_b, L0_xattn_q1, L0_xattn_k1, L0_xattn_v1, L0_xattn_o1_w, L0_xattn_o1_b, L0_xattn_n2_g, L0_xattn_n2_b, L0_xattn_q2, L0_xattn_k2, L0_xattn_v2, L0_xattn_o2_w, L0_xattn_o2_b, L0_xattn_n3_g, L0_xattn_n3_b, L0_xattn_ff_w1, L0_xattn_ff_b1, L0_xattn_ff_w2, L0_xattn_ff_b2, L1_xattn_Wq, L1_xattn_Wk, L1_xattn_Wv, L1_xattn_Wq_ca, L1_xattn_Wk_ca, L1_xattn_Wv_ca, L1_xattn_Wout, L1_xattn_b_out):
    import jax
    import jax.numpy as jnp

    def _L0_xattn_ref(x, context, heads, n1_g, n1_b, q1, k1, v1, o1_w, o1_b, n2_g, n2_b, q2, k2, v2, o2_w, o2_b, n3_g, n3_b, ff_w1, ff_b1, ff_w2, ff_b2):
        import jax, jax.numpy as jnp
        import numpy as np
        D = 160
        H = 20
        DH = D // H
        CTX = 96
        FF_IN = 4 * D
        EPS = 1e-05

        def _ln(x, g, b):
            m = jnp.mean(x, axis=-1, keepdims=True)
            v = jnp.mean(jnp.square(x - m), axis=-1, keepdims=True)
            return (x - m) * jax.lax.rsqrt(v + EPS) * g + b

        def _attn(x, ctx, wq, wk, wv, wo, bo, heads):
            b, n, _ = x.shape
            j = ctx.shape[1]
            dh = wq.shape[1] // heads
            scale = dh ** (-0.5)
            q = (x @ wq).reshape(b, n, heads, dh).transpose(0, 2, 1, 3)
            k = (ctx @ wk).reshape(b, j, heads, dh).transpose(0, 2, 1, 3)
            v = (ctx @ wv).reshape(b, j, heads, dh).transpose(0, 2, 1, 3)
            sim = jnp.einsum('bhid,bhjd->bhij', q, k) * scale
            a = jax.nn.softmax(sim, axis=-1)
            out = jnp.einsum('bhij,bhjd->bhid', a, v)
            out = out.transpose(0, 2, 1, 3).reshape(b, n, heads * dh)
            return out @ wo + bo
        h1 = _ln(x, n1_g, n1_b)
        x = _attn(h1, h1, q1, k1, v1, o1_w, o1_b, heads) + x
        h2 = _ln(x, n2_g, n2_b)
        x = _attn(h2, context, q2, k2, v2, o2_w, o2_b, heads) + x
        h3 = _ln(x, n3_g, n3_b)
        proj = h3 @ ff_w1 + ff_b1
        a, g = jnp.split(proj, 2, axis=-1)
        ff = a * jax.nn.gelu(g, approximate=False) @ ff_w2 + ff_b2
        return ff + x

    def _L1_xattn_ref(hidden_states, encoder_hidden_states, Wq, Wk, Wv, Wq_ca, Wk_ca, Wv_ca, Wout, b_out):
        import jax, jax.numpy as jnp
        import numpy as np
        HEADS = 8
        NUM_TOKENS = 4
        CROSS_ATTENTION_DIM = 96

        def _mha(q, k, v, heads=HEADS):
            B, Sq, H = q.shape
            Sk = k.shape[1]
            d = H // heads
            qh = q.reshape(B, Sq, heads, d).transpose(0, 2, 1, 3)
            kh = k.reshape(B, Sk, heads, d).transpose(0, 2, 1, 3)
            vh = v.reshape(B, Sk, heads, d).transpose(0, 2, 1, 3)
            scores = jnp.einsum('bhqd,bhkd->bhqk', qh, kh) * jnp.asarray(d, q.dtype) ** (-0.5)
            probs = jax.nn.softmax(scores, axis=-1)
            out = jnp.einsum('bhqk,bhkd->bhqd', probs, vh)
            return out.transpose(0, 2, 1, 3).reshape(B, Sq, H)
        residual = hidden_states
        unet_size = residual.shape[1]
        end_pos = encoder_hidden_states.shape[1] - NUM_TOKENS
        enc = encoder_hidden_states[:, :end_pos, :]
        ca = encoder_hidden_states[:, end_pos:, :]
        query = hidden_states @ Wq
        keyt = enc @ Wk
        valt = enc @ Wv
        hs = _mha(query, keyt, valt)
        ca_q1 = jnp.einsum('btc,th->bch', ca, Wq_ca)
        indices = np.linspace(0, CROSS_ATTENTION_DIM - 1, unet_size).astype(np.int64)
        ca_q1 = ca_q1[:, indices, :]
        ca_hs1 = _mha(ca_q1, residual, residual)
        ca_q2 = ca_hs1 @ Wq
        ca_k2 = ca @ Wk_ca
        ca_v2 = ca @ Wv_ca
        ca_hs2 = _mha(ca_q2, ca_k2, ca_v2)
        out = hs + ca_hs2
        out = out @ Wout + b_out
        out = out + residual
        return out
    x = _L0_xattn_ref(x, ctx_768, 20, L0_xattn_n1_g, L0_xattn_n1_b, L0_xattn_q1, L0_xattn_k1, L0_xattn_v1, L0_xattn_o1_w, L0_xattn_o1_b, L0_xattn_n2_g, L0_xattn_n2_b, L0_xattn_q2, L0_xattn_k2, L0_xattn_v2, L0_xattn_o2_w, L0_xattn_o2_b, L0_xattn_n3_g, L0_xattn_n3_b, L0_xattn_ff_w1, L0_xattn_ff_b1, L0_xattn_ff_w2, L0_xattn_ff_b2)
    x = _L1_xattn_ref(x, ctx_768, L1_xattn_Wq, L1_xattn_Wk, L1_xattn_Wv, L1_xattn_Wq_ca, L1_xattn_Wk_ca, L1_xattn_Wv_ca, L1_xattn_Wout, L1_xattn_b_out)
    return x

_drawn_inputs = setup_inputs


def setup_inputs(seed=0):
    import zlib

    import numpy as np

    out = dict(_drawn_inputs(seed))
    spreads = {'L0_xattn_n1_g': (1.0, 0.2),
     'L0_xattn_n1_b': (0.0, 0.1),
     'L0_xattn_o1_b': (0.0, 0.1),
     'L0_xattn_n2_g': (1.0, 0.2),
     'L0_xattn_n2_b': (0.0, 0.372),
     'L0_xattn_o2_b': (0.0, 0.1),
     'L0_xattn_n3_g': (1.0, 0.2),
     'L0_xattn_n3_b': (0.0, 0.1),
     'L0_xattn_ff_b1': (0.0, 0.1),
     'L0_xattn_ff_b2': (0.0, 0.1),
     'L1_xattn_b_out': (0.0, 0.1)}
    factors = {'L1_xattn_Wq': 8.0,
     'L1_xattn_Wk': 8.0,
     'L1_xattn_Wv': 3.065,
     'L1_xattn_Wq_ca': 64.0,
     'L1_xattn_Wk_ca': 26.262}
    for name, (base, spread) in spreads.items():
        noise = np.random.default_rng([zlib.crc32(name.encode()), seed]).standard_normal(out[name].shape)
        drawn = base * np.exp(spread * noise) if base else spread * noise
        out[name] = jnp.asarray(drawn.astype(out[name].dtype))
    for name, factor in factors.items():
        out[name] = (out[name] * factor).astype(out[name].dtype)
    return out
```

```python
import concourse.bass as bass
from concourse import mybir
from contextlib import ExitStack

F32 = mybir.dt.float32
F32R = mybir.dt.float32r
BF16 = mybir.dt.bfloat16
ALU = mybir.AluOpType
ACT = mybir.ActivationFunctionType
AX = mybir.AxisListType

B, N, D = 64, 128, 160
NC_, C = 120, 96
H, DH = 20, 8
D0, D1 = 128, 32
GROUPS = H // 4
FF = 4 * D
FT = FF // 128
EPS = 1e-5
HL, DL = 8, 20
CA = 4
NE = NC_ - CA
LA, LB = 100, 60
LO = 32


def hold(eng, M):
    eng.sem_inc(M.held, 1)


def split_stack(ap, slots):
    v = ap.rearrange("p (n k d) -> p n k d", k=4, d=DH)
    return v[:, :, slots, :]


class Memory:

    def __init__(self, nc, ctx):
        def sb(name, shape, dt=F32):
            return ctx.enter_context(nc.sbuf_tensor(name, shape, dt))

        self.held = ctx.enter_context(nc.semaphore("held"))
        self.X = sb("X", [N, B, D])
        self.MV = sb("MV", [N, B, 2])
        self.RSTD = sb("RSTD", [N, B])
        self.VEPS = sb("VEPS", [N, B])
        self.HALF = sb("HALF", [N, B])
        self.LN = sb("LN", [N, 6, D])
        self.BIAS = sb("BIAS", [N, 4, D])
        self.ident = sb("ident", [128, 128])
        self.identb = sb("identb", [128, 128], BF16)
        self.sel = sb("sel", [128, H, 128], BF16)
        self.quad = sb("quad", [128, 4])
        self.ones = sb("ones", [128, 4, 32])
        self.one32 = sb("one32", [128, 32])
        self.NM = sb("NM", [128, 128], BF16)
        self.NMT = sb("NMT", [128, 128], BF16)
        self.negmax = sb("negmax", [128, H])
        self.stats = sb("stats", [N, 6])
        self.mv1 = sb("mv1", [N, 2])
        self.h = sb("h", [N, 2, D])
        self.hs = sb("hs", [N, 2, 4, D1], F32R)
        self.hT = sb("hT", [128, N])
        self.hsT = sb("hsT", [128, N], F32R)
        self.xc = sb("xc", [N, D])
        self.p = sb("p", [128, 5, 512])
        self.rec = sb("rec", [128, 2, 256])
        self.aT = sb("aT", [128, 256])
        self.ctxT = sb("ctxT", [C, 2, NC_])
        self.ps = [ctx.enter_context(nc.psum_tensor(f"bank{i}", [128, 512], F32)) for i in range(8)]


def setup(nc, ctx, M, d):
    sem = lambda n: ctx.enter_context(nc.semaphore(n))
    x_loaded = [sem(f"x_loaded{k}") for k in range(8)]
    vectors_loaded, zeroed, placed, stats_done, means_done = (
        sem(n) for n in ("vectors_loaded", "zeroed", "placed", "stats_done0", "means_done0"))
    block = ctx.enter_context(nc.Block())

    @block.sync
    def _(sp):
        for k in range(8):
            sp.dma_start(M.X[:, 8 * k:8 * k + 8, :], d["x"][8 * k:8 * k + 8].rearrange("b n d -> n b d"))\
              .then_inc(x_loaded[k], 16)

    @block.scalar
    def _(act):
        names = ["n1_g", "n1_b", "n2_g", "n2_b", "n3_g", "n3_b"]
        for k, n in enumerate(names):
            act.dma_start(M.LN[:, k, :], d["L0_xattn_" + n].partition_broadcast(N)).then_inc(vectors_loaded, 16)
        names = ["L0_xattn_o1_b", "L0_xattn_o2_b", "L0_xattn_ff_b2", "L1_xattn_b_out"]
        for k, n in enumerate(names):
            act.dma_start(M.BIAS[:, k, :], d[n].partition_broadcast(N)).then_inc(vectors_loaded, 16)
        act.wait_ge(vectors_loaded, 160)

    @block.gpsimd
    def _(pool):
        pool.memset(M.ident[:, :], 0.0).then_inc(zeroed, 1)
        pool.memset(M.sel[:, :, :], 0.0).then_inc(zeroed, 1)
        pool.memset(M.ones[:, :, :], 0.0).then_inc(zeroed, 1)
        pool.memset(M.one32[:, :], 1.0).then_inc(zeroed, 1)
        pool.memset(M.quad[:, :], 1.0).then_inc(zeroed, 1)
        pool.memset(M.NM[:, :], 0.0).then_inc(zeroed, 1)
        pool.memset(M.HALF[:, :], -0.5).then_inc(zeroed, 1)
        pool.wait_ge(zeroed, 7)
        pool.affine_select(out=M.ident[:, :], in_=M.ident[:, :], compare_op=ALU.not_equal, fill=1.0, base=0,
                           pattern=[[-1, 128]], channel_multiplier=1).then_inc(placed, 1)
        pool.affine_select(out=M.sel[:, :, :], in_=M.sel[:, :, :], compare_op=ALU.not_equal, fill=1.0, base=0,
                           pattern=[[-1, H], [0, 128]], channel_multiplier=1).then_inc(placed, 1)
        pool.wait_ge(placed, 2)
        pool.affine_select(out=M.sel[:, :, :], in_=M.sel[:, :, :], compare_op=ALU.not_equal, fill=1.0, base=-LO,
                           pattern=[[-1, H], [0, 128]], channel_multiplier=1).then_inc(placed, 1)
        pool.affine_select(out=M.quad[:, :], in_=M.quad[:, :], compare_op=ALU.is_ge, fill=0.0, base=0,
                           pattern=[[-32, 4]], channel_multiplier=1).then_inc(placed, 1)
        pool.wait_ge(placed, 4)
        pool.affine_select(out=M.quad[:, :], in_=M.quad[:, :], compare_op=ALU.is_ge, fill=0.0, base=31,
                           pattern=[[32, 4]], channel_multiplier=-1).then_inc(placed, 1)
        for i in range(4):
            pool.memset(M.ones[:, i, DH * i:DH * i + DH], 1.0).then_inc(placed, 1)
        pool.tensor_copy(M.identb[:, :], M.ident[:, :]).then_inc(placed, 1)
        pool.wait_ge(placed, 10)

    @block.vector
    def _(dve):
        for k in range(8):
            dve.wait_ge(x_loaded[k], 16)
            with dve.Fori(8 * k, 8 * k + 8) as b:
                row_statistics(dve, M, b, b, stats_done, means_done)


def row_statistics(dve, M, b, done, stats_done, means_done):
    hold(dve, M)
    dve.bn_stats(M.stats[:, :], M.X[:, b, :]).then_inc(stats_done, 1)
    dve.wait_ge(stats_done, done + 1)
    hold(dve, M)
    dve.bn_aggr(M.mv1[:, :], M.stats[:, :]).then_inc(means_done, 1)
    dve.wait_ge(means_done, 2 * done + 1)
    dve.tensor_copy(M.MV[:, b, :], M.mv1[:, :]).then_inc(means_done, 1)
    dve.wait_ge(means_done, 2 * done + 2)


def reciprocal_deviation(pool, M, step):
    pool.memset(M.VEPS[:, :], EPS).then_inc(step, 1)
    pool.wait_ge(step, 1)
    pool.tensor_tensor(M.VEPS[:, :], M.MV[:, :, 1], M.VEPS[:, :], ALU.add).then_inc(step, 1)
    pool.wait_ge(step, 2)
    pool.tensor_tensor(M.RSTD[:, :], M.VEPS[:, :], M.HALF[:, :], ALU.pow).then_inc(step, 1)
    pool.wait_ge(step, 3)


NORM_STEPS = 6


def normalise(pool, M, j, u, ln, step, h_free):
    base = NORM_STEPS * j + 3
    h, hs, X = M.h[:, u, :], M.hs[:, u], M.X[:, j, :]
    h_free(pool, j)
    hold(pool, M)
    pool.tensor_tensor(M.xc[:, :], X, M.MV[:, j, 0:1].broadcast_to([N, D]), ALU.subtract).then_inc(step, 1)
    pool.wait_ge(step, base + 1)
    hold(pool, M)
    pool.tensor_tensor(h, M.xc[:, :], M.RSTD[:, bass.ds(j, 1)].broadcast_to([N, D]), ALU.mult).then_inc(step, 1)
    pool.wait_ge(step, base + 2)
    pool.tensor_tensor(M.xc[:, :], h, M.LN[:, ln, :], ALU.mult).then_inc(step, 1)
    pool.wait_ge(step, base + 3)
    pool.tensor_tensor(h, M.xc[:, :], M.LN[:, ln + 1, :], ALU.add).then_inc(step, 1)
    pool.wait_ge(step, base + 4)
    hold(pool, M)
    tail = h[:, D0:D].unsqueeze(1).broadcast_to([N, 2, D1])
    pool.tensor_copy(hs[:, 0::2, :], tail).then_inc(step, 1)
    pool.wait_ge(step, base + 5)
    high = hs[:, 0:1, :].bitcast(F32).broadcast_to([N, 2, D1])
    pool.tensor_tensor(hs[:, 1::2, :], tail, high, ALU.subtract).then_inc(step, 1)


def stack_weight(dve, raw, out, n, done, base):
    dve.tensor_copy(out[:, :], raw[:, :]).then_inc(done, 1)
    dve.wait_ge(done, base + 1)
    dve.tensor_tensor(out[64:128, :], raw[64:128, :], out[64:128, :].bitcast(F32), ALU.subtract).then_inc(done, 1)
    dve.wait_ge(done, base + 2)


def attention(nc, ctx, M, d, cross):
    tag = "c" if cross else "s"
    nk = NC_ if cross else N
    wname = "2" if cross else "1"
    ctx = ctx.enter_context(ExitStack())

    def sb(name, shape, dt=F32):
        return ctx.enter_context(nc.sbuf_tensor(f"{name}_{tag}", shape, dt))

    def sem(name):
        return ctx.enter_context(nc.semaphore(f"{name}_{tag}"))

    nq = D if cross else 3 * D
    wq0, wq_raw, wqs = sb("wq0", [D0, nq]), sb("wq_raw", [128, nq]), sb("wqs", [128, nq], F32R)
    wkv = sb("wkv", [C, 2 * D])
    wo0, wo1 = sb("wo0", [D0, D]), sb("wo1", [D1, D])
    qs, ks = sb("qs", [N, H * 32], F32R), sb("ks", [N, H * 32], F32R)
    qT, kT = sb("qT", [128, 2, GROUPS, N], F32R), sb("kT", [128, 2, GROUPS, N], F32R)
    kB = sb("kB", [128, 2, 4, N], F32R)
    p, pT = sb("p", [N, 2, 5, 512]), sb("pT", [128, 5, 512])
    sums = sb("sums", [N, 2, H])
    rec, rec8 = sb("rec", [N, H]), sb("rec8", [N, D])
    recT = sb("recT", [128, 256])
    v = sb("v", [128, D])
    vpad = sb("vpad", [128, 2, H, 32])

    w_loaded, w_split, vpad_zero = sem("w_loaded"), sem("w_split"), sem("vpad_zero")
    blocks_ready = sem("blocks_ready")
    ctx_loaded = [sem("ctx_loaded0"), sem("ctx_loaded1")]
    norm_step, h_used = sem("norm_step"), sem("h_used")
    hT_ready, qkv_done, high_ready, v_copied, low_ready, v_ready = (
        sem(n) for n in ("hT_ready", "qkv_done", "high_ready", "v_copied", "low_ready", "v_ready"))
    turned, turned_copied, s_done, s_reduced = (sem(n) for n in ("turned", "turned_copied", "s_done", "s_reduced"))
    p_ready, p_turned, pT_even, pT_odd, pv_done = (
        sem(n) for n in ("p_ready", "p_turned", "pT_even", "pT_odd", "pv_done"))
    rec_ready, rec_turned, recT_ready = (sem(n) for n in ("rec_ready", "rec_turned", "recT_ready"))
    aT_ready, o_done, x_ready = (sem(n) for n in ("aT_ready", "o_done", "x_ready"))
    bias_added, stats_done, means_done = (sem(n) for n in ("bias_added", "stats_done", "means_done"))

    S, PT = M.ps[0:2], M.ps[2:4]
    PV, TR, QKV, TURN = M.ps[4:8]
    numA, numB = PV[:, 0:128], PV[0:32, 256:384]
    scale = DH ** -0.5

    def heads(c):
        return [4 * g + c for g in range(4)] if c < 4 else [16 + j for j in range(4)]

    def wait_pT(eng, i, c):
        if c % 2:
            eng.wait_ge(pT_odd, 2 * i + c // 2 + 1)
        else:
            eng.wait_ge(pT_even, 3 * i + c // 2 + 1)

    def pipeline(eng, stage):
        stage(0, 0, True, True)
        stage(1, 1, True, True)
        with eng.Fori(1, (B - 2) // 2) as half:
            for u in range(2):
                stage(2 * half + u, u, True, True)
        stage(B - 2, 0, False, True)
        stage(B - 1, 1, False, False)

    block = ctx.enter_context(nc.Block())

    @block.sync
    def _(sp):
        q, o = d[f"L0_xattn_q{wname}"], d[f"L0_xattn_o{wname}_w"]
        k, vv = d[f"L0_xattn_k{wname}"], d[f"L0_xattn_v{wname}"]
        loads = [(wo0[:, :], o[0:D0]), (wo1[:, :], o[D0:D])]
        for n, w in enumerate([q] if cross else [q, k, vv]):
            loads.append((wq0[:, n * D:n * D + D], w[0:D0]))
            loads += [(wq_raw[32 * r:32 * r + 32, n * D:n * D + D], w[D0:D]) for r in range(4)]
        if cross:
            loads += [(wkv[:, 0:D], k), (wkv[:, D:2 * D], vv)]
        for to, src in loads:
            sp.dma_start(to, src).then_inc(w_loaded, 16)
        if cross:
            for u in range(2):
                sp.dma_start(M.ctxT[:, u, :], d["ctxT"][u]).then_inc(ctx_loaded[u], 16)
            with sp.Fori(0, (B - 2) // 2) as half:
                for u in range(2):
                    sp.wait_ge(qkv_done, 2 * half + u + 1)
                    sp.dma_start(M.ctxT[:, u, :], d["ctxT"][2 * half + u + 2]).then_inc(ctx_loaded[u], 16)
    n_loads = 2 + 5 * (1 if cross else 3) + (2 if cross else 0)

    @block.gpsimd
    def _(pool):
        pool.memset(vpad[:, :, :, :], 0.0).then_inc(vpad_zero, 1)
        pool.memset(kB[:, :, :, :].bitcast(F32), 0.0).then_inc(vpad_zero, 1)
        reciprocal_deviation(pool, M, norm_step)

        def h_free(pool, j):
            if isinstance(j, int) and j < 2:
                return
            pool.wait_ge(h_used, j - 1)

        def place_blocks(j, u):
            pool.wait_ge(turned_copied, 3 * (j + 1))
            if not (isinstance(j, int) and j < 2):
                pool.wait_ge(s_done, 5 * (j - 1))
            hold(pool, M)
            pool.tensor_tensor(kB[:, u, :, 0:nk], kT[:, u, 4:5, 0:nk].bitcast(F32).broadcast_to([128, 4, nk]),
                               M.quad[:, :].unsqueeze(2).broadcast_to([128, 4, nk]), ALU.mult).then_inc(blocks_ready, 1)

        def place_v(j, u):
            pool.wait_ge(v_copied, j + 1)
            if not (isinstance(j, int) and j < 2):
                pool.wait_ge(pv_done, 5 * (j - 1))
            hold(pool, M)
            to = bass.AP(vpad, u * H * 32, [[2 * H * 32, nk], [128, GROUPS], [32 + DH, 4], [1, DH]])
            pool.tensor_copy(to, v[0:nk, :].rearrange("p (g i e) -> p g i e", g=GROUPS, e=DH)).then_inc(v_ready, 1)

        def add_bias(j):
            pool.wait_ge(norm_step, NORM_STEPS * (j + 1) + 3)
            hold(pool, M)
            pool.tensor_tensor(M.X[:, j, :], M.X[:, j, :], M.BIAS[:, int(cross), :], ALU.add)\
                .then_inc(bias_added, 1)

        def ahead(j, u):
            normalise(pool, M, j, u, 2 * int(cross), norm_step, h_free)
            add_bias(j)

        pool.wait_ge(vpad_zero, 2)
        ahead(0, 0)
        ahead(1, 1)
        place_v(0, 0)
        place_blocks(0, 0)
        ahead(2, 0)
        place_v(1, 1)
        place_blocks(1, 1)
        ahead(3, 1)
        with pool.Fori(1, (B - 2) // 2) as half:
            for u in range(2):
                place_v(2 * half + u, u)
                place_blocks(2 * half + u, u)
                ahead(2 * half + u + 2, u)
        place_v(B - 2, 0)
        place_blocks(B - 2, 0)
        place_v(B - 1, 1)
        place_blocks(B - 1, 1)

    @block.scalar
    def _(act):
        def copy_hT(j):
            act.wait_ge(h_used, j + 1)
            if not (isinstance(j, int) and j < 1):
                act.wait_ge(qkv_done, j)
            act.activation(M.hT[:, :], TR[:, 0:128], ACT.Copy).then_inc(hT_ready, 1)
            act.activation(M.hsT[:, :], TR[:, 128:256], ACT.Copy).then_inc(hT_ready, 1)

        def high_halves(j):
            act.wait_ge(qkv_done, j + 1)
            if not (isinstance(j, int) and j < 1):
                act.wait_ge(turned, 3 * j)
                act.wait_ge(v_ready, j)
            q4 = QKV[:, 0:D].rearrange("p (n d) -> p n d", d=DH).unsqueeze(2).broadcast_to([N, H, 2, DH])
            k4 = QKV[0:nk, D:2 * D].rearrange("p (n d) -> p n d", d=DH).unsqueeze(2).broadcast_to([nk, H, 2, DH])
            act.activation(split_stack(qs[:, :], slice(0, None, 2)), q4, ACT.Copy).then_inc(high_ready, 1)
            act.activation(split_stack(ks[0:nk, :], slice(0, 2)), k4, ACT.Copy).then_inc(high_ready, 1)
            act.activation(v[0:nk, :], QKV[0:nk, 2 * D:3 * D], ACT.Copy).then_inc(v_copied, 1)

        def exps(j, u, c):
            act.wait_ge(s_reduced, 5 * j + c + 1)
            if not (isinstance(j, int) and j < 2):
                act.wait_ge(p_turned, 5 * (j - 2) + c + 1)
            if c == 0 and not (isinstance(j, int) and j < 2):
                act.wait_ge(rec_ready, 2 * (j - 1))
            for k, n in enumerate(heads(c)):
                last = act.activation(p[:, u, c, 128 * k:128 * k + nk], S[(u + c) % 2][:, 128 * k:128 * k + nk], ACT.Exp,
                                      bias=M.negmax[:, 4 * c + k:4 * c + k + 1], accum_out=sums[:, u, n:n + 1])
            last.then_inc(p_ready, 1)

        def copy_even(i, u, c):
            act.wait_ge(p_turned, 5 * i + c + 1)
            if not (isinstance(i, int) and i < 1):
                act.wait_ge(pv_done, 5 * (i - 1) + c + 1)
            act.activation(pT[0:nk, c, :], PT[(u + c) % 2][0:nk, :], ACT.Copy).then_inc(pT_even, 1)

        def copy_recT(i):
            act.wait_ge(rec_turned, i + 1)
            if not (isinstance(i, int) and i < 1):
                act.wait_ge(aT_ready, 2 * i)
            act.activation(recT[:, 0:128], TR[:, 256:384], ACT.Copy).then_inc(recT_ready, 1)
            act.activation(recT[0:32, 128:256], TR[0:32, 384:512], ACT.Copy).then_inc(recT_ready, 1)

        copy_hT(0)
        high_halves(0)
        copy_hT(1)
        high_halves(1)
        for c in range(5):
            exps(0, 0, c)

        def stage(i, u, a, b):
            for c in range(5):
                if c % 2 == 0:
                    copy_even(i, u, c)
                if a and c == 0:
                    copy_hT(i + 2)
                if b:
                    exps(i + 1, 1 - u, c)
                if a and c == 2:
                    high_halves(i + 2)
                if c == 2:
                    copy_recT(i)

        pipeline(act, stage)

    @block.vector
    def _(dve):
        dve.wait_ge(w_loaded, 16 * n_loads)
        for w in (wq0, wq_raw):
            dve.tensor_scalar(w[:, 0:D], w[:, 0:D], scale, None, op0=ALU.mult).then_inc(w_split, 1)
        dve.wait_ge(w_split, 2)
        stack_weight(dve, wq_raw, wqs, nq, w_split, 2)

        def low_halves(j):
            dve.wait_ge(high_ready, 2 * (j + 1))
            dve.wait_ge(v_copied, j + 1)
            q4 = QKV[:, 0:D].rearrange("p (n d) -> p n d", d=DH).unsqueeze(2).broadcast_to([N, H, 2, DH])
            k4 = QKV[0:nk, D:2 * D].rearrange("p (n d) -> p n d", d=DH).unsqueeze(2).broadcast_to([nk, H, 2, DH])
            qh = split_stack(qs[:, :], slice(0, 1)).bitcast(F32).broadcast_to([N, H, 2, DH])
            kh = split_stack(ks[0:nk, :], slice(0, 1)).bitcast(F32).broadcast_to([nk, H, 2, DH])
            dve.tensor_tensor(split_stack(qs[:, :], slice(1, None, 2)), q4, qh, ALU.subtract).then_inc(low_ready, 1)
            dve.tensor_tensor(split_stack(ks[0:nk, :], slice(2, 4)), k4, kh, ALU.subtract).then_inc(low_ready, 1)

        def copy_turned(j, u, part):
            dve.wait_ge(turned, 3 * j + part + 1)
            if part == 0 and not (isinstance(j, int) and j < 2):
                dve.wait_ge(s_done, 5 * (j - 1))
            if part == 0:
                out, src = qT[:, u, 0:4, :], TURN[:, :].rearrange("p (g n) -> p g n", g=4)
                dve.tensor_copy(out, src).then_inc(turned_copied, 1)
            elif part == 1:
                src = TURN[:, :].rearrange("p (g n) -> p g n", g=4)[:, :, 0:nk]
                dve.tensor_copy(kT[:, u, 0:4, 0:nk], src).then_inc(turned_copied, 1)
            else:
                dve.tensor_copy(qT[:, u, 4, :], TURN[:, 0:128])
                dve.tensor_copy(kT[:, u, 4, 0:nk], TURN[:, 128:128 + nk]).then_inc(turned_copied, 1)

        def reduce_max(j, u, c):
            dve.wait_ge(s_done, 5 * j + c + 1)
            src = S[(u + c) % 2][:, :].rearrange("p (g n) -> p g n", g=4)[:, :, 0:nk]
            dve.tensor_reduce(M.negmax[:, 4 * c:4 * c + 4], src, AX.X, ALU.max, negate=True).then_inc(s_reduced, 1)

        def copy_odd(i, u, c):
            dve.wait_ge(p_turned, 5 * i + c + 1)
            if not (isinstance(i, int) and i < 1):
                dve.wait_ge(pv_done, 5 * (i - 1) + c + 1)
            dve.tensor_copy(pT[0:nk, c, :], PT[(u + c) % 2][0:nk, :]).then_inc(pT_odd, 1)

        def reciprocals(i, u):
            dve.wait_ge(p_ready, 5 * (i + 1))
            if not (isinstance(i, int) and i < 1):
                dve.wait_ge(rec_turned, i)
            dve.reciprocal(rec[:, :], sums[:, u, :]).then_inc(rec_ready, 1)
            dve.wait_ge(rec_ready, 2 * i + 1)
            dve.tensor_copy(rec8[:, :].rearrange("p (n d) -> p n d", d=DH),
                            rec[:, :].unsqueeze(2).broadcast_to([N, H, DH])).then_inc(rec_ready, 1)

        def divide(i):
            dve.wait_ge(pv_done, 5 * (i + 1))
            dve.wait_ge(recT_ready, 2 * (i + 1))
            if not (isinstance(i, int) and i < 1):
                dve.wait_ge(o_done, i)
            dve.tensor_tensor(M.aT[:, 0:128], numA, recT[:, 0:128], ALU.mult).then_inc(aT_ready, 1)
            dve.tensor_tensor(M.aT[0:32, 128:256], numB, recT[0:32, 128:256], ALU.mult).then_inc(aT_ready, 1)

        def residual(i):
            dve.wait_ge(o_done, i + 1)
            dve.wait_ge(bias_added, i + 1)
            dve.tensor_tensor(M.X[:, i, :], QKV[:, 0:D], M.X[:, i, :], ALU.add).then_inc(x_ready, 1)
            dve.wait_ge(x_ready, i + 1)
            row_statistics(dve, M, i, i, stats_done, means_done)

        low_halves(0)
        for part in range(3):
            copy_turned(0, 0, part)
        low_halves(1)
        for part in range(3):
            copy_turned(1, 1, part)
        for c in range(5):
            reduce_max(0, 0, c)

        def stage(i, u, a, b):
            for c in range(5):
                if c % 2:
                    copy_odd(i, u, c)
                if b:
                    reduce_max(i + 1, 1 - u, c)
                if c == 0:
                    reciprocals(i, u)
                if c == 1 and not (isinstance(i, int) and i < 1):
                    residual(i - 1)
                if a and c == 3:
                    low_halves(i + 2)
            if a:
                for part in range(3):
                    copy_turned(i + 2, u, part)
            divide(i)

        pipeline(dve, stage)
        residual(B - 1)

    @block.tensor
    def _(pe):
        def turn_h(j, u):
            pe.wait_ge(norm_step, NORM_STEPS * (j + 1) + 3)
            if not (isinstance(j, int) and j < 1):
                pe.wait_ge(hT_ready, 2 * j)
            if not (isinstance(j, int) and j < 3):
                pe.wait_ge(recT_ready, 2 * (j - 2))
            pe.transpose(TR[:, 0:128], M.h[:, u, 0:D0], M.ident[:, :])
            pe.transpose(TR[:, 128:256], M.hs[:, u].rearrange("p k d -> p (k d)").bitcast(F32), M.ident[:, :])\
              .then_inc(h_used, 1)

        def project(j, u):
            pe.wait_ge(hT_ready, 2 * (j + 1))
            if cross:
                pe.wait_ge(ctx_loaded[u], 16 * ((j - u) // 2 + 1) if isinstance(j, int) else ctx_count(j, u))
            if not (isinstance(j, int) and j < 1):
                pe.wait_ge(low_ready, 2 * j)
            if not (isinstance(j, int) and j < 3):
                pe.wait_ge(x_ready, j - 2)
            pe.matmul(QKV[:, 0:nq], M.hT[:, :], wq0[:, :], start=True, stop=False)
            last = pe.matmul(QKV[:, 0:nq], M.hsT[:, :], wqs[:, :], start=False, stop=True)
            if cross:
                last = pe.matmul(QKV[0:NC_, D:3 * D], M.ctxT[:, u, :], wkv[:, :], start=True, stop=True)
            last.then_inc(qkv_done, 1)

        def ctx_count(j, u):
            return 8 * j + (16 - 8 * u)

        def turn_stack(j, part):
            pe.wait_ge(low_ready, 2 * (j + 1))
            if part > 0 or not (isinstance(j, int) and j < 1):
                pe.wait_ge(turned_copied, 3 * j + part)
            blocks = [[(qs, g, g) for g in range(4)], [(ks, g, g) for g in range(4)], [(qs, 4, 0), (ks, 4, 1)]][part]
            for src, g, at in blocks:
                rows = N if src is qs else nk
                last = pe.transpose(TURN[:, 128 * at:128 * at + rows], src[0:rows, 128 * g:128 * g + 128].bitcast(F32),
                                    M.ident[0:rows, 0:rows])
            last.then_inc(turned, 1)

        def scores(j, u, c):
            if not (isinstance(j, int) and 5 * j + c < 2):
                pe.wait_ge(p_ready, 5 * j + c - 1)
            bank = S[(u + c) % 2]
            if c == 4:
                pe.wait_ge(blocks_ready, j + 1)
                last = pe.matmul(bank[:, :], qT[:, u, 4, :], kB[:, u].rearrange("p k n -> p (k n)"),
                                 start=True, stop=True)
            else:
                for g in range(4):
                    r = 32 * c
                    last = pe.matmul(bank[:, 128 * g:128 * g + nk], qT[r:r + 32, u, g, :], kT[r:r + 32, u, g, 0:nk],
                                     start=True, stop=True, tile_position=(r, 0))
            last.then_inc(s_done, 1)

        def turn_p(i, u, c):
            pe.wait_ge(p_ready, 5 * i + c + 1)
            if c >= 2:
                wait_pT(pe, i, c - 2)
            elif not (isinstance(i, int) and i < 1):
                wait_pT(pe, i - 1, c + 3)
            for k in range(4):
                last = pe.transpose(PT[(u + c) % 2][0:nk, 128 * k:128 * k + N], p[:, u, c, 128 * k:128 * k + nk],
                                    M.ident[:, :])
            last.then_inc(p_turned, 1)

        def turn_rec(i, j):
            pe.wait_ge(rec_ready, 2 * (i + 1))
            pe.wait_ge(hT_ready, 2 * j)
            pe.transpose(TR[:, 256:384], rec8[:, 0:D0], M.ident[:, :])
            pe.transpose(TR[0:32, 384:512], rec8[:, D0:D], M.ident[:, :]).then_inc(rec_turned, 1)

        def weighted(i, u, c):
            wait_pT(pe, i, c)
            if c == 0:
                pe.wait_ge(v_ready, i + 1)
                if not (isinstance(i, int) and i < 1):
                    pe.wait_ge(aT_ready, 2 * i)
            for k, n in enumerate(heads(c)):
                out = numA[32 * k:32 * k + 32, :] if c < 4 else numB
                last = pe.matmul(out, vpad[0:nk, u, n, :], pT[0:nk, c, 128 * k:128 * k + 128], start=(c == 0),
                                 stop=(c == 3 or (c == 4 and k == 3)), skip_group_check=True)
            last.then_inc(pv_done, 1)

        def project_out(i, j):
            pe.wait_ge(aT_ready, 2 * (i + 1))
            pe.wait_ge(low_ready, 2 * j)
            pe.matmul(QKV[:, 0:D], M.aT[:, 0:128], wo0[:, :], start=True, stop=False)
            pe.matmul(QKV[:, 0:D], M.aT[0:32, 128:256], wo1[:, :], start=False, stop=True).then_inc(o_done, 1)

        pe.wait_ge(w_split, 4)
        pe.wait_ge(w_loaded, 16 * n_loads)
        for j in range(2):
            turn_h(j, j)
            project(j, j)
            for part in range(3):
                turn_stack(j, part)
        pe.wait_ge(turned_copied, 3)
        for c in range(5):
            scores(0, 0, c)

        def stage(i, u, a, b):
            for c in range(5):
                turn_p(i, u, c)
                if b and c == 0:
                    pe.wait_ge(turned_copied, 3 * (i + 2))
                if b:
                    scores(i + 1, 1 - u, c)
                if a and c == 0:
                    turn_h(i + 2, u)
                if c:
                    weighted(i, u, c - 1)
                if c == 1 and not (isinstance(i, int) and i < 1):
                    project_out(i - 1, min(i + 2, B) if isinstance(i, int) else i + 2)
                if a and c == 2:
                    project(i + 2, u)
                if c == 2:
                    turn_rec(i, min(i + 3, B) if isinstance(i, int) else i + 3)
            if a:
                turn_stack(i + 2, 0)
            weighted(i, u, 4)
            if a:
                turn_stack(i + 2, 1)
                turn_stack(i + 2, 2)

        pipeline(pe, stage)
        project_out(B - 1, B)

    ctx.close()


def feed_forward(nc, ctx, M, d):
    ctx = ctx.enter_context(ExitStack())
    G, Q = B // 4, 4

    def sb(name, shape, dt=F32):
        return ctx.enter_context(nc.sbuf_tensor(f"{name}_f", shape, dt))

    def sem(name):
        return ctx.enter_context(nc.semaphore(f"{name}_f"))

    w1, w1_raw, w1s = sb("w1", [D0, 2 * FF]), sb("w1_raw", [128, 2 * FF]), sb("w1s", [128, 2 * FF], F32R)
    w2, b1 = sb("w2", [128, FT, D]), sb("b1", [128, 2 * FT])
    hT, hsT = sb("hT4", [128, 2, Q * N]), sb("hsT4", [128, 2, Q * N], F32R)
    gate, f = sb("gate", [128, 2, Q * N]), sb("f", [128, 2, FT, Q * N])
    w_loaded, w_split, norm_step, h_used, hT_ready, bias_added = (
        sem(n) for n in ("w_loaded", "w_split", "norm_step", "h_used", "hT_ready", "bias_added"))
    up_done, gate_ready, f_ready, down_done, x_ready = (
        sem(n) for n in ("up_done", "gate_ready", "f_ready", "down_done", "x_ready"))
    A, GP, DOWN = M.ps[0:2], M.ps[2:4], M.ps[4:6]
    TR = M.ps[6]
    block = ctx.enter_context(nc.Block())

    def pipeline(eng, stage, last):
        stage(0, 0, True, True, False)
        stage(1, 1, True, True, True)
        with eng.Fori(1, G // 2 - 1) as half:
            for u in range(2):
                stage(2 * half + u, u, True, True, True)
        stage(G - 2, 0, True, True, True)
        stage(G - 1, 1, True, False, True)
        if last:
            stage(G, 0, False, False, True)

    @block.sync
    def _(sp):
        sp.dma_start(w1[:, :], d["L0_xattn_ff_w1"][0:D0]).then_inc(w_loaded, 16)
        for r in range(4):
            sp.dma_start(w1_raw[32 * r:32 * r + 32, :], d["L0_xattn_ff_w1"][D0:D]).then_inc(w_loaded, 16)
        sp.dma_start(w2[:, :, :], d["L0_xattn_ff_w2"].rearrange("(t p) n -> p t n", p=128)).then_inc(w_loaded, 16)
        sp.dma_start(b1[:, :], d["ff_b1T"]).then_inc(w_loaded, 16)

    @block.gpsimd
    def _(pool):
        reciprocal_deviation(pool, M, norm_step)

        def h_free(pool, j):
            if isinstance(j, int) and j < 2:
                return
            pool.wait_ge(h_used, j - 1)

        def ahead(j, u):
            normalise(pool, M, j, u, 4, norm_step, h_free)
            pool.wait_ge(norm_step, NORM_STEPS * (j + 1) + 3)
            hold(pool, M)
            pool.tensor_tensor(M.X[:, j, :], M.X[:, j, :], M.BIAS[:, 2, :], ALU.add).then_inc(bias_added, 1)

        ahead(0, 0)
        ahead(1, 1)
        with pool.Fori(1, B // 2) as half:
            for u in range(2):
                ahead(2 * half + u, u)

    @block.scalar
    def _(act):
        def copy_hT(k, u, q):
            act.wait_ge(h_used, Q * k + q + 1)
            if q == 0 and not (isinstance(k, int) and k < 2):
                act.wait_ge(up_done, FT * (k - 1))
            act.activation(hT[:, u, N * q:N * q + N], TR[:, 0:128], ACT.Copy).then_inc(hT_ready, 1)
            act.activation(hsT[:, u, N * q:N * q + N], TR[:, 128:256], ACT.Copy).then_inc(hT_ready, 1)

        def gelu(k, u, t):
            act.wait_ge(up_done, FT * k + t + 1)
            if not (isinstance(k, int) and FT * k + t < 2):
                act.wait_ge(f_ready, FT * k + t - 1)
            act.activation(gate[:, (u + t) % 2, :], GP[(u + t) % 2][:, :], ACT.Gelu, bias=b1[:, FT + t:FT + t + 1])\
               .then_inc(gate_ready, 1)

        act.wait_ge(w_loaded, 16 * 7)
        for q in range(Q):
            copy_hT(0, 0, q)

        def stage(k, u, up, ahead, down):
            for t in range(FT):
                gelu(k, u, t)
                if ahead and t < Q:
                    copy_hT(k + 1, 1 - u, t)

        pipeline(act, stage, False)

    @block.vector
    def _(dve):
        dve.wait_ge(w_loaded, 16 * 7)
        stack_weight(dve, w1_raw, w1s, 2 * FF, w_split, 0)

        def gated(k, u, t):
            dve.wait_ge(gate_ready, FT * k + t + 1)
            if t == 0 and not (isinstance(k, int) and k < 2):
                dve.wait_ge(down_done, Q * (k - 1))
            dve.scalar_tensor_tensor(f[:, u, t, :], A[(u + t) % 2][:, :], b1[:, t:t + 1], gate[:, (u + t) % 2, :],
                                     ALU.add, ALU.mult).then_inc(f_ready, 1)

        def residual(k, q):
            j = Q * k + q
            dve.wait_ge(down_done, j + 1)
            dve.wait_ge(bias_added, j + 1)
            dve.tensor_tensor(M.X[:, j, :], DOWN[q % 2][:, 0:D], M.X[:, j, :], ALU.add).then_inc(x_ready, 1)

        def stage(k, u, up, ahead, down):
            for t in range(FT):
                if up:
                    gated(k, u, t)
                if down and t < Q:
                    residual(k - 1, t)

        pipeline(dve, stage, True)

    @block.tensor
    def _(pe):
        def turn_h(k, q):
            j = Q * k + q
            pe.wait_ge(norm_step, NORM_STEPS * (j + 1) + 3)
            if not (isinstance(j, int) and j < 1):
                pe.wait_ge(hT_ready, 2 * j)
            pe.transpose(TR[:, 0:128], M.h[:, q % 2, 0:D0], M.ident[:, :])
            pe.transpose(TR[:, 128:256], M.hs[:, q % 2].rearrange("p k d -> p (k d)").bitcast(F32), M.ident[:, :])\
              .then_inc(h_used, 1)

        def up_tile(k, u, t):
            if t == 0:
                pe.wait_ge(hT_ready, 2 * Q * (k + 1))
            if not (isinstance(k, int) and FT * k + t < 2):
                pe.wait_ge(f_ready, FT * k + t - 1)
            for bank, at in ((GP, FF), (A, 0)):
                out, cols = bank[(u + t) % 2][:, :], slice(at + 128 * t, at + 128 * t + 128)
                pe.matmul(out, w1[:, cols], hT[:, u, :], start=True, stop=False)
                last = pe.matmul(out, w1s[:, cols], hsT[:, u, :], start=False, stop=True)
            last.then_inc(up_done, 1)

        def down(k, u, q):
            j = Q * k + q
            pe.wait_ge(f_ready, FT * (k + 1))
            if not (isinstance(j, int) and j < 2):
                pe.wait_ge(x_ready, j - 1)
            for t in range(FT):
                last = pe.matmul(DOWN[q % 2][:, 0:D], f[:, u, t, N * q:N * q + N], w2[:, t, :], start=(t == 0),
                                 stop=(t == FT - 1))
            last.then_inc(down_done, 1)

        pe.wait_ge(w_loaded, 16 * 7)
        pe.wait_ge(w_split, 2)
        for q in range(Q):
            turn_h(0, q)

        def stage(k, u, up, ahead, down_):
            for t in range(FT):
                if up:
                    up_tile(k, u, t)
                if ahead and t < Q:
                    turn_h(k + 1, t)
                if down_ and t < Q:
                    down(k - 1, 1 - u, t)

        pipeline(pe, stage, True)

    ctx.close()


def second_block(nc, ctx, M, d, out):
    ctx = ctx.enter_context(ExitStack())

    def sb(name, shape, dt=F32):
        return ctx.enter_context(nc.sbuf_tensor(f"{name}_l", shape, dt))

    def sem(name):
        return ctx.enter_context(nc.semaphore(f"{name}_l"))

    S2, T2 = 2, 128
    NCH = 8
    wqa_a, wqa_b = sb("wqa_a", [LA, S2 * T2]), sb("wqa_b", [LB, S2 * T2])
    wk, wv, wvca = sb("wk", [C, S2 * T2]), sb("wv", [C, S2 * T2]), sb("wvca", [C, S2 * T2])
    wkca = sb("wkca", [C, D])
    wqT_a, wqT_b = sb("wqT_a", [LA, S2 * T2]), sb("wqT_b", [LB, S2 * T2])
    wout, E = sb("wout", [128, S2, D]), sb("E", [C, N])
    kmask, vmask = sb("kmask", [LA, 2, 32]), sb("vmask", [32, S2 * T2])
    caq = sb("caq", [128, 2, C])
    ca32 = sb("ca32", [C, 32])
    x1, xpad = sb("x1", [N, 2, D]), sb("xpad", [N, 2, HL, 32])
    xT, k2 = sb("xT", [LA, 2 * N]), sb("k2", [LA, 2, CA])
    k2b = sb("k2b", [LA, 2, 32])
    wk2 = sb("wk2", [128, 2, S2 * 32])
    qk = sb("qk", [128, 2, S2 * T2 + S2 * NE])
    v, v2 = sb("v", [NE, 2, S2 * T2]), sb("v2", [32, 2, S2 * T2])
    p2, sum2, max2 = sb("p2", [C, 3, 32]), sb("sum2", [C, 2, HL]), sb("max2", [C, HL])
    p2T, hs1, hs, yt = sb("p2T", [32, N]), sb("hs1", [128, S2 * C]), sb("hs", [128, S2 * T2]), sb("yt", [N, 2, D])
    res = sb("res", [128, S2 * T2])

    w_loaded, zeroed = sem("w_loaded"), sem("zeroed")
    ctx_loaded = [sem("ctx_loaded0"), sem("ctx_loaded1")]
    x1_copied, xpad_copied, bias_added, k2b_ready, ca32_ready = (
        sem(n) for n in ("x1_copied", "xpad_copied", "bias_added", "k2b_ready", "ca32_ready"))
    turned, xT_ready, qk_done, qk_ready, v_done, v_ready, v2_ready, wk2_done, wk2_ready = (
        sem(n) for n in ("turned", "xT_ready", "qk_done", "qk_ready", "v_done", "v_ready", "v2_ready", "wk2_done",
                         "wk2_ready"))
    s_done, s_reduced, nm_ready, nm_turned, nmT_ready = (
        sem(n) for n in ("s_done", "s_reduced", "nm_ready", "nm_turned", "nmT_ready"))
    st_done, p_ready, pv_done, rec_ready, hs1_ready, hs_ready = (
        sem(n) for n in ("st_done", "p_ready", "pv_done", "rec_ready", "hs1_ready", "hs_ready"))
    s2_done, max2_ready, e2_ready, sum2_ready, p2_ready, p2_turned, p2T_ready, ca2_done = (
        sem(n) for n in ("s2_done", "max2_ready", "e2_ready", "sum2_ready", "p2_ready", "p2_turned", "p2T_ready",
                         "ca2_done"))
    aT_ready, out_done, y_ready = sem("aT_ready"), sem("out_done"), sem("y_ready")
    stored = [sem("stored0"), sem("stored1")]

    S, ST = M.ps[0:2], M.ps[2:4]
    PV, PV1, TR, PRJ = M.ps[4:8]
    num, den = PV[:, 0:S2 * T2], PV[:, S2 * T2:2 * S2 * T2]
    num1, den1 = PV1[:, 0:S2 * C], PV1[:, S2 * C:2 * S2 * C]
    s2_ps, p2T_ps, ca2_ps = PV1[0:C, 0:32], PV1[0:32, 128:256], PV1[:, 256:512]
    xT_ps, k2_ps, wk2_ps = TR[:, 0:2 * N], TR[0:LA, 256:264], TR[:, 320:320 + S2 * 32]
    scale = DL ** -0.5

    def pipeline(eng, stage):
        stage(0, 0, True, True)
        stage(1, 1, True, True)
        with eng.Fori(1, (B - 2) // 2) as half:
            for u in range(2):
                stage(2 * half + u, u, True, True)
        stage(B - 2, 0, False, True)
        stage(B - 1, 1, False, False)

    def first(j, n=1):
        return isinstance(j, int) and j < n

    def loads_until(j, u):
        return 80 * ((j - u) // 2 + 1) if isinstance(j, int) else 40 * j + 80 - 40 * u

    block = ctx.enter_context(nc.Block())

    @block.sync
    def _(sp):
        loads = [(wqa_a, "wqa", 0, LA), (wqa_b, "wqa", LA, D), (wk, "l_wk", 0, C), (wv, "l_wv", 0, C),
                 (wvca, "l_wvca", 0, C), (wkca, "L1_xattn_Wk_ca", 0, C), (wqT_a, "l_wqT", 0, LA),
                 (wqT_b, "l_wqT", LA, D), (E, "spread", 0, C), (vmask, "vmask", 0, 32)]
        for to, name, r0, r1 in loads:
            sp.dma_start(to[:, :], d[name][r0:r1]).then_inc(w_loaded, 16)
        sp.dma_start(wout[:, :, :], d["l_wout"]).then_inc(w_loaded, 16)
        sp.dma_start(kmask[:, 0, :], d["kmask"][0:LA]).then_inc(w_loaded, 16)
        sp.dma_start(kmask[0:LB, 1, :], d["kmask"][LA:D]).then_inc(w_loaded, 16)

        def load_context(j, u):
            sp.dma_start(M.ctxT[:, u, :], d["ctxT"][j]).then_inc(ctx_loaded[u], 16)
            for r in range(4):
                sp.dma_start(caq[32 * r + DL:32 * r + DL + CA, u, :], d["ctx_768"][j, NE:NC_, :])\
                  .then_inc(ctx_loaded[u], 16)

        def write(i, u):
            sp.wait_ge(y_ready, i + 1)
            sp.dma_start(out[i], yt[:, u, :]).then_inc(stored[u], 16)

        sp.wait_ge(zeroed, 2)
        load_context(0, 0)
        load_context(1, 1)
        with sp.Fori(0, (B - 2) // 2) as half:
            for u in range(2):
                i = 2 * half + u
                sp.wait_ge(v_done, i + 1)
                sp.wait_ge(st_done, NCH * i + 4)
                load_context(i + 2, u)
                write(i, u)
        write(B - 2, 0)
        write(B - 1, 1)
        for u in range(2):
            sp.wait_ge(stored[u], 8 * B)

    @block.gpsimd
    def _(pool):
        pool.memset(caq[:, :, :], 0.0).then_inc(zeroed, 1)
        pool.memset(xpad[:, :, :, :], 0.0).then_inc(zeroed, 1)
        pool.memset(k2b[:, :, :], 0.0).then_inc(zeroed, 1)
        pool.wait_ge(zeroed, 3)
        pool.wait_ge(w_loaded, 16 * 13)

        def copy_x1(j, u):
            if not first(j, 2):
                pool.wait_ge(turned, j - 1)
            hold(pool, M)
            pool.tensor_copy(x1[:, u, :], M.X[:, j, :]).then_inc(x1_copied, 1)

        def copy_xpad(j, u):
            if not first(j, 2):
                pool.wait_ge(pv_done, 4 * (j - 2) + 2)
            hold(pool, M)
            pool.tensor_copy(xpad[:, u, :, 0:DL], M.X[:, j, :].rearrange("p (n d) -> p n d", d=DL))\
                .then_inc(xpad_copied, 1)
            pool.wait_ge(x1_copied, j + 1)
            pool.wait_ge(xpad_copied, j + 1)
            hold(pool, M)
            pool.tensor_tensor(M.X[:, j, :], M.X[:, j, :], M.BIAS[:, 3, :], ALU.add).then_inc(bias_added, 1)

        def repeat_ca(j, u):
            pool.wait_ge(ctx_loaded[u], loads_until(j, u))
            if not first(j):
                pool.wait_ge(v_done, j)
            hold(pool, M)
            pool.tensor_copy(ca32[:, :].rearrange("p (n t) -> p n t", t=CA),
                             M.ctxT[:, u, NE:NC_].unsqueeze(1).broadcast_to([C, HL, CA])).then_inc(ca32_ready, 1)

        def block_keys(j):
            pool.wait_ge(xT_ready, 4 * (j + 1))
            if not first(j):
                pool.wait_ge(wk2_done, j)
            for s, rows in ((0, LA), (1, LB)):
                pool.tensor_tensor(k2b[0:rows, s, :].rearrange("p (n t) -> p n t", t=CA),
                                   k2[0:rows, s, :].unsqueeze(1).broadcast_to([rows, HL, CA]),
                                   kmask[0:rows, s, :].rearrange("p (n t) -> p n t", t=CA), ALU.mult)\
                    .then_inc(k2b_ready, 1)

        def ahead(j, u, more=True):
            copy_xpad(j, u)
            repeat_ca(j, u)
            block_keys(j)
            if more:
                copy_x1(j + 1, 1 - u)

        copy_x1(0, 0)
        ahead(0, 0)
        ahead(1, 1)
        with pool.Fori(1, B // 2 - 1) as half:
            for u in range(2):
                ahead(2 * half + u, u)
        ahead(B - 2, 0)
        ahead(B - 1, 1, False)

    @block.scalar
    def _(act):
        def copy_xT(j):
            act.wait_ge(turned, j + 1)
            if not first(j):
                act.wait_ge(qk_done, j)
                act.wait_ge(k2b_ready, 2 * j)
            act.activation(xT[:, 0:N], xT_ps[0:LA, 0:N], ACT.Copy).then_inc(xT_ready, 1)
            act.activation(xT[0:LB, N:2 * N], xT_ps[0:LB, N:2 * N], ACT.Copy).then_inc(xT_ready, 1)
            act.activation(k2[:, 0, :], k2_ps[:, 0:CA], ACT.Copy).then_inc(xT_ready, 1)
            act.activation(k2[0:LB, 1, :], k2_ps[0:LB, CA:2 * CA], ACT.Copy).then_inc(xT_ready, 1)

        def copy_qk(j, u):
            act.wait_ge(qk_done, j + 1)
            if not first(j, 2):
                act.wait_ge(st_done, NCH * (j - 1))
            act.activation(qk[:, u, :], PRJ[:, 0:S2 * T2 + S2 * NE], ACT.Copy).then_inc(qk_ready, 1)

        def copy_v(j, u):
            act.wait_ge(v_done, j + 1)
            if not first(j, 2):
                act.wait_ge(pv_done, 4 * (j - 1))
            act.activation(v[:, u, :], PRJ[0:NE, 0:S2 * T2], ACT.Copy).then_inc(v_ready, 1)

        def copy_wk2(j, u):
            act.wait_ge(wk2_done, j + 1)
            if not first(j, 2):
                act.wait_ge(s2_done, j - 1)
            act.activation(wk2[:, u, :], wk2_ps, ACT.Copy).then_inc(wk2_ready, 1)

        def copy_nmT(j):
            act.wait_ge(nm_turned, j + 1)
            if not first(j):
                act.wait_ge(st_done, NCH * j)
            act.activation(M.NMT[:, :], TR[:, 0:64].bitcast(BF16), ACT.Copy).then_inc(nmT_ready, 1)

        def exps(i, c):
            act.wait_ge(st_done, NCH * i + c + 1)
            if not first(i):
                act.wait_ge(pv_done, 4 * (i - 1) + c // 2 + 1)
            rows, cols = (N, C) if c < 4 else (NE, N)
            to = M.p[0:rows, c // 2, 256 * (c % 2):256 * (c % 2) + 256]
            act.activation(to.rearrange("p (k n) -> p k n", k=2)[:, :, 0:cols],
                           ST[c % 2][0:rows, 0:256].rearrange("p (k n) -> p k n", k=2)[:, :, 0:cols], ACT.Exp,
                           scale=scale).then_inc(p_ready, 1)

        def exp2(i):
            act.wait_ge(max2_ready, 2 * (i + 1))
            act.activation(p2[:, 1, :], p2[:, 0, :], ACT.Exp, scale=scale).then_inc(e2_ready, 1)

        def copy_p2T(i):
            act.wait_ge(p2_turned, i + 1)
            if not first(i):
                act.wait_ge(ca2_done, i)
            act.activation(p2T[:, :], p2T_ps, ACT.Copy).then_inc(p2T_ready, 1)

        for j in range(2):
            copy_xT(j)
            copy_qk(j, j)
            copy_v(j, j)
            copy_wk2(j, j)
        copy_nmT(0)

        def stage(i, u, a, b):
            for c in range(4):
                exps(i, c)
            if a:
                copy_xT(i + 2)
            exps(i, 4)
            exps(i, 5)
            exp2(i)
            exps(i, 6)
            exps(i, 7)
            if a:
                copy_qk(i + 2, u)
            copy_p2T(i)
            if a:
                copy_v(i + 2, u)
                copy_wk2(i + 2, u)
            if b:
                copy_nmT(i + 1)

        pipeline(act, stage)

    @block.vector
    def _(dve):
        dve.wait_ge(w_loaded, 16 * 13)

        def block_values(j, u):
            dve.wait_ge(v_ready, j + 1)
            if not first(j, 2):
                dve.wait_ge(ca2_done, j - 1)
            dve.tensor_tensor(v2[:, u, :], PRJ[0:32, S2 * T2:2 * S2 * T2], vmask[:, :], ALU.mult).then_inc(v2_ready, 1)

        def reduce_max(j, c):
            dve.wait_ge(s_done, NCH * j + c + 1)
            if c == 0 and not first(j):
                dve.wait_ge(nm_ready, 4 * j)
            rows, cols = (C, N) if c < 4 else (N, NE)
            src = S[c % 2][0:rows, 0:256].rearrange("p (k n) -> p k n", k=2)[:, :, 0:cols]
            dve.tensor_reduce(M.negmax[0:rows, 2 * c:2 * c + 2], src, AX.X, ALU.max, negate=True).then_inc(s_reduced, 1)

        def split_max(j):
            dve.wait_ge(s_reduced, NCH * (j + 1))
            if not first(j):
                dve.wait_ge(nm_turned, j)
            parts = ((C, 0, 8), (N, 8, 16))
            for rows, a, b in parts:
                dve.tensor_copy(M.NM[0:rows, a:b], M.negmax[0:rows, a:b]).then_inc(nm_ready, 1)
            dve.wait_ge(nm_ready, 4 * j + 2)
            for rows, a, b in parts:
                dve.tensor_tensor(M.NM[0:rows, LO + a:LO + b], M.negmax[0:rows, a:b], M.NM[0:rows, a:b],
                                  ALU.subtract).then_inc(nm_ready, 1)

        def divide1(i):
            dve.wait_ge(pv_done, 4 * i + 2)
            if not first(i):
                dve.wait_ge(s2_done, i)
                dve.wait_ge(hs1_ready, i)
                dve.wait_ge(hs_ready, 2 * i)
            dve.reciprocal(M.rec[:, 0, 0:S2 * C], den1).then_inc(rec_ready, 1)
            dve.wait_ge(rec_ready, 2 * i + 1)
            dve.tensor_tensor(hs1[:, :], num1, M.rec[:, 0, 0:S2 * C], ALU.mult).then_inc(hs1_ready, 1)

        def divide(i):
            dve.wait_ge(pv_done, 4 * (i + 1))
            dve.reciprocal(M.rec[:, 1, :], den).then_inc(rec_ready, 1)
            dve.wait_ge(rec_ready, 2 * i + 2)
            dve.tensor_tensor(hs[:, :], num, M.rec[:, 1, :], ALU.mult).then_inc(hs_ready, 1)

        def less_max2(i):
            dve.wait_ge(s2_done, i + 1)
            if not first(i):
                dve.wait_ge(max2_ready, 2 * i)
            s2 = s2_ps.rearrange("p (n t) -> p n t", t=CA)
            dve.tensor_reduce(max2[:, :], s2, AX.X, ALU.max).then_inc(max2_ready, 1)
            dve.wait_ge(max2_ready, 2 * i + 1)
            dve.tensor_tensor(p2[:, 0, :].rearrange("p (n t) -> p n t", t=CA), s2,
                              max2[:, :].unsqueeze(2).broadcast_to([C, HL, CA]), ALU.subtract).then_inc(max2_ready, 1)

        def divide2(i):
            dve.wait_ge(e2_ready, i + 1)
            if not first(i):
                dve.wait_ge(p2_ready, i)
                dve.wait_ge(p2_turned, i)
            e2 = p2[:, 1, :].rearrange("p (n t) -> p n t", t=CA)
            dve.tensor_reduce(sum2[:, 0, :], e2, AX.X, ALU.add).then_inc(sum2_ready, 1)
            dve.wait_ge(sum2_ready, 2 * i + 1)
            dve.reciprocal(sum2[:, 1, :], sum2[:, 0, :]).then_inc(sum2_ready, 1)
            dve.wait_ge(sum2_ready, 2 * i + 2)
            dve.tensor_tensor(p2[:, 2, :].rearrange("p (n t) -> p n t", t=CA), e2,
                              sum2[:, 1, :].unsqueeze(2).broadcast_to([C, HL, CA]), ALU.mult).then_inc(p2_ready, 1)

        def add_branch(i):
            dve.wait_ge(ca2_done, i + 1)
            dve.wait_ge(hs_ready, 2 * i + 1)
            if not first(i):
                dve.wait_ge(out_done, i)
            dve.tensor_tensor(res[:, :], ca2_ps, hs[:, :], ALU.add).then_inc(hs_ready, 1)

        def result(i, u):
            dve.wait_ge(out_done, i + 1)
            dve.wait_ge(bias_added, i + 1)
            if not first(i, 2):
                dve.wait_ge(stored[u], 16 * ((i - u) // 2) if isinstance(i, int) else 8 * i - 8 * u)
            dve.tensor_tensor(yt[:, u, :], PRJ[:, 0:D], M.X[:, i, :], ALU.add).then_inc(y_ready, 1)

        for j in range(2):
            block_values(j, j)
        for c in range(NCH):
            reduce_max(0, c)
        split_max(0)

        def stage(i, u, a, b):
            def reduce_next(*chunks):
                for c in chunks if b else ():
                    reduce_max(i + 1, c)

            reduce_next(0, 1)
            divide1(i)
            less_max2(i)
            reduce_next(2)
            divide2(i)
            reduce_next(3)
            divide(i)
            reduce_next(4)
            add_branch(i)
            reduce_next(5)
            if a:
                block_values(i + 2, u)
            reduce_next(6)
            result(i, u)
            reduce_next(7)
            if b:
                split_max(i + 1)

        pipeline(dve, stage)

    @block.tensor
    def _(pe):
        def q_of(u, s, j):
            return qk[32 * j:32 * j + 32, u, T2 * s:T2 * s + N]

        def k_of(u, s, j):
            return qk[32 * j:32 * j + 32, u, S2 * T2 + NE * s:S2 * T2 + NE * s + NE]

        def turn(j, u):
            pe.wait_ge(x1_copied, j + 1)
            pe.wait_ge(ctx_loaded[u], loads_until(j, u))
            if not first(j):
                pe.wait_ge(wk2_ready, j)
            pe.transpose(TR[0:LA, 0:N], x1[:, u, 0:LA], M.ident[:, :])
            pe.transpose(TR[0:LB, N:2 * N], x1[:, u, LA:D], M.ident[:, :])
            ca = M.ctxT[:, u, NE:NC_]
            pe.matmul(k2_ps[:, 0:CA], wkca[:, 0:LA], ca, start=True, stop=True)
            pe.matmul(k2_ps[0:LB, CA:2 * CA], wkca[:, LA:D], ca, start=True, stop=True).then_inc(turned, 1)

        def project_qk(j, u):
            pe.wait_ge(xT_ready, 4 * (j + 1))
            if not first(j):
                pe.wait_ge(v2_ready, j)
            if not first(j, 3):
                pe.wait_ge(y_ready, j - 2)
            for s in range(S2):
                cols = slice(T2 * s, T2 * s + T2)
                pe.matmul(PRJ[:, cols], wqa_a[:, cols], xT[:, 0:N], start=True, stop=False)
                pe.matmul(PRJ[:, cols], wqa_b[:, cols], xT[0:LB, N:2 * N], start=False, stop=True)
            for s in range(S2):
                last = pe.matmul(PRJ[:, S2 * T2 + NE * s:S2 * T2 + NE * s + NE], wk[:, T2 * s:T2 * s + T2],
                                 M.ctxT[:, u, 0:NE], start=True, stop=True)
            last.then_inc(qk_done, 1)

        def project_v(j, u):
            pe.wait_ge(qk_ready, j + 1)
            pe.wait_ge(ca32_ready, j + 1)
            pe.matmul(PRJ[0:NE, 0:S2 * T2], M.ctxT[:, u, 0:NE], wv[:, :], start=True, stop=True)
            pe.matmul(PRJ[0:32, S2 * T2:2 * S2 * T2], ca32[:, :], wvca[:, :], start=True, stop=True).then_inc(v_done, 1)

        def fold_keys(j, u):
            pe.wait_ge(k2b_ready, 2 * (j + 1))
            for s in range(S2):
                out = wk2_ps[:, 32 * s:32 * s + 32]
                pe.matmul(out, wqT_a[:, T2 * s:T2 * s + T2], k2b[:, 0, :], start=True, stop=False)
                last = pe.matmul(out, wqT_b[:, T2 * s:T2 * s + T2], k2b[0:LB, 1, :], start=False, stop=True)
            last.then_inc(wk2_done, 1)

        def scores(j, u, c):
            if not (isinstance(j, int) and NCH * j + c < 2):
                pe.wait_ge(s_reduced, NCH * j + c - 1)
            bank, r = S[c % 2], c % 4
            if c < 4:
                last = pe.matmul(bank[0:C, 0:256], caq[32 * r:32 * r + 32, u, :], qk[32 * r:32 * r + 32, u, 0:256],
                                 start=True, stop=True, tile_position=(32 * r, 0))
            else:
                for s in range(S2):
                    last = pe.matmul(bank[:, 128 * s:128 * s + NE], q_of(u, s, r), k_of(u, s, r),
                                     start=True, stop=True, tile_position=(32 * r, 0))
            last.then_inc(s_done, 1)

        def turn_max(j):
            pe.wait_ge(nm_ready, 4 * (j + 1))
            pe.wait_ge(wk2_ready, min(j + 2, B) if isinstance(j, int) else j + 2)
            pe.transpose(TR[:, 0:64].bitcast(BF16), M.NM[:, :], M.identb[:, :]).then_inc(nm_turned, 1)

        def scores_T(i, u, c):
            if c == 0:
                pe.wait_ge(nmT_ready, i + 1)
            if not (isinstance(i, int) and NCH * i + c < 2):
                pe.wait_ge(p_ready, NCH * i + c - 1)
            bank, r = ST[c % 2], c % 4
            rows, cols = (N, C) if c < 4 else (NE, N)
            for s in range(S2):
                at = bank[0:rows, 128 * s:128 * s + cols]
                if c < 4:
                    pe.matmul(at, q_of(u, s, r), caq[32 * r:32 * r + 32, u, :], start=True, stop=False,
                              tile_position=(32 * r, 0))
                else:
                    pe.matmul(at, k_of(u, s, r), q_of(u, s, r), start=True, stop=False, tile_position=(32 * r, 0))
                last = pe.matmul(at, M.sel[:, 2 * c + s, 0:rows], M.NMT[:, 0:cols], start=False, stop=True)
            last.then_inc(st_done, 1)

        def weighted(i, u, pair):
            pe.wait_ge(p_ready, NCH * i + 2 * pair + 2)
            if pair == 0:
                pe.wait_ge(xpad_copied, i + 1)
                if not first(i):
                    pe.wait_ge(hs_ready, 2 * i)
            branch, t = pair < 2, pair % 2
            rows, cols = (N, C) if branch else (NE, N)
            sums = (num1, den1) if branch else (num, den)
            for k in range(4):
                values = xpad[:, u, 4 * t + k, :] if branch else v[:, u, T2 * t + 32 * k:T2 * t + 32 * k + 32]
                pe.matmul(sums[0][32 * k:32 * k + 32, cols * t:cols * t + cols], values,
                          M.p[0:rows, pair, 128 * k:128 * k + cols], start=True, stop=True)
            for k in range(4):
                last = pe.matmul(sums[1][32 * k:32 * k + 32, cols * t:cols * t + cols], M.one32[0:rows, :],
                                 M.p[0:rows, pair, 128 * k:128 * k + cols], start=True, stop=True)
            last.then_inc(pv_done, 1)

        def scores2(i, u):
            pe.wait_ge(hs1_ready, i + 1)
            for t in range(S2):
                last = pe.matmul(s2_ps, hs1[:, C * t:C * t + C], wk2[:, u, 32 * t:32 * t + 32], start=(t == 0),
                                 stop=(t == 1))
            last.then_inc(s2_done, 1)

        def turn_p2(i):
            pe.wait_ge(p2_ready, i + 1)
            pe.matmul(p2T_ps, p2[:, 2, :], E[:, :], start=True, stop=True).then_inc(p2_turned, 1)

        def weighted2(i, u):
            pe.wait_ge(p2T_ready, i + 1)
            for t in range(S2):
                last = pe.matmul(ca2_ps[:, T2 * t:T2 * t + T2], v2[:, u, T2 * t:T2 * t + T2], p2T[:, :], start=True,
                                 stop=True)
            last.then_inc(ca2_done, 1)

        def project_out(i, j):
            pe.wait_ge(hs_ready, 2 * (i + 1))
            pe.wait_ge(v2_ready, j)
            for t in range(S2):
                last = pe.matmul(PRJ[:, 0:D], res[:, T2 * t:T2 * t + T2], wout[:, t, :], start=(t == 0), stop=(t == 1))
            last.then_inc(out_done, 1)

        pe.wait_ge(w_loaded, 16 * 13)
        for j in range(2):
            turn(j, j)
            project_qk(j, j)
            project_v(j, j)
            fold_keys(j, j)
        for c in range(NCH):
            scores(0, 0, c)
        turn_max(0)

        def stage(i, u, a, b):
            def scores_next(c):
                if b:
                    scores(i + 1, 1 - u, c)

            scores_T(i, u, 0)
            scores_T(i, u, 1)
            scores_next(0)
            scores_T(i, u, 2)
            weighted(i, u, 0)
            scores_T(i, u, 3)
            scores_next(1)
            weighted(i, u, 1)
            if a:
                turn(i + 2, u)
            scores_T(i, u, 4)
            scores_T(i, u, 5)
            scores2(i, u)
            scores_next(2)
            scores_T(i, u, 6)
            weighted(i, u, 2)
            scores_T(i, u, 7)
            scores_next(3)
            weighted(i, u, 3)
            if a:
                project_qk(i + 2, u)
            turn_p2(i)
            scores_next(4)
            weighted2(i, u)
            if a:
                project_v(i + 2, u)
            scores_next(5)
            if a:
                fold_keys(i + 2, u)
            scores_next(6)
            project_out(i, i + 3 if a else B)
            scores_next(7)
            if b:
                turn_max(i + 1)

        pipeline(pe, stage)

    ctx.close()


def layouts(given):
    import numpy as np

    def pairs(n):
        return 128 * (n % 2) + 32 * (n // 2)

    def fours(n):
        return 128 * (n // 4) + 32 * (n % 4)

    def padded(w, place):
        to = np.zeros((w.shape[0], 256), w.dtype)
        for n in range(HL):
            to[:, place(n):place(n) + DL] = w[:, DL * n:DL * n + DL]
        return to

    wqa = padded(given["L1_xattn_Wq"], pairs)
    spread = np.zeros((C, N), np.float32)
    kmask = np.zeros((D, HL * CA), np.float32)
    vmask = np.zeros((HL * CA, 256), np.float32)
    for n in range(HL):
        mine = slice(DL * n, DL * n + DL)
        wqa[mine, pairs(n) + DL:pairs(n) + DL + CA] = given["L1_xattn_Wq_ca"][:, mine].T
        kmask[mine, CA * n:CA * n + CA] = 1
        vmask[CA * n:CA * n + CA, fours(n):fours(n) + DL] = 1
    spread[np.linspace(0, C - 1, N).astype(np.int64), np.arange(N)] = 1
    return {
        "ctxT": given["ctx_768"].transpose(0, 2, 1),
        "ff_b1T": given["L0_xattn_ff_b1"].reshape(2 * FT, 128).T,
        "wqa": wqa,
        "l_wk": padded(given["L1_xattn_Wk"], pairs),
        "l_wv": padded(given["L1_xattn_Wv"], fours),
        "l_wvca": padded(given["L1_xattn_Wv_ca"], fours),
        "l_wqT": padded(given["L1_xattn_Wq"].T, fours),
        "l_wout": padded(given["L1_xattn_Wout"].T, fours).T.reshape(2, 128, D).transpose(1, 0, 2),
        "spread": spread, "kmask": kmask, "vmask": vmask,
    }


def build(nc, d, out):
    ctx = ExitStack()
    with ctx:
        M = Memory(nc, ctx)
        with ExitStack() as scope:
            setup(nc, scope, M, d)
        attention(nc, ctx, M, d, False)
        attention(nc, ctx, M, d, True)
        feed_forward(nc, ctx, M, d)
        second_block(nc, ctx, M, d, out)


def kernel(**inputs):
    import numpy as np
    import concourse.bacc as bacc
    from concourse.bass_utils import run_bass_kernel_spmd

    nc = bacc.Bacc("TRN2", target_bir_lowering=False, num_devices=1)
    given = {name: np.ascontiguousarray(a) for name, a in inputs.items()}
    laid = layouts(given)
    arrays = {"in_" + name: np.ascontiguousarray(a) for name, a in {**given, **laid}.items()}
    d = {name[3:]: nc.dram_tensor(name, a.shape, mybir.dt.from_np(a.dtype), kind="ExternalInput").ap()
         for name, a in arrays.items()}
    out = nc.dram_tensor("out_0", (B, N, D), F32, kind="ExternalOutput").ap()
    build(nc, d, out)
    return run_bass_kernel_spmd(nc, [arrays], core_ids=[0]).results[0]["out_0"]
```

```python
import concourse.bass as bass
from concourse import mybir
from contextlib import ExitStack

F32 = mybir.dt.float32
F32R = mybir.dt.float32r
ALU = mybir.AluOpType
ACT = mybir.ActivationFunctionType
AX = mybir.AxisListType

B, N, D = 64, 128, 160
NC_, C = 120, 96
H, DH = 20, 8
D0, D1 = 128, 32
GROUPS = H // 4
FF = 4 * D
FT = FF // 128
EPS = 1e-5
HL, DL = 8, 20
CA = 4
NE = NC_ - CA
LA, LB = 100, 60


def hold(eng, M):
    eng.sem_inc(M.held, 1)


def split_stack(ap, slots):
    v = ap.rearrange("p (n k d) -> p n k d", k=4, d=DH)
    return v[:, :, slots, :]


class Memory:

    def __init__(self, nc, ctx):
        def sb(name, shape, dt=F32):
            return ctx.enter_context(nc.sbuf_tensor(name, shape, dt))

        self.held = ctx.enter_context(nc.semaphore("held"))
        self.X = sb("X", [N, B, D])
        self.MV = sb("MV", [N, B, 2])
        self.veps, self.rstd = sb("veps", [N, 1]), sb("rstd", [N, 1])
        self.eps, self.half = sb("eps", [N, 1]), sb("half", [N, 1])
        self.LN = sb("LN", [N, 6, D])
        self.BIAS = sb("BIAS", [N, 4, D])
        self.ident = sb("ident", [128, 128])
        self.quad = sb("quad", [128, 4])
        self.negmax = sb("negmax", [128, H])
        self.stats = sb("stats", [N, 4, 6])
        self.mv1 = sb("mv1", [N, 4, 2])
        self.h = sb("h", [N, 2, D])
        self.hs = sb("hs", [N, 2, 4, D1], F32R)
        self.hT = sb("hT", [128, N])
        self.hsT = sb("hsT", [128, N], F32R)
        self.xc = sb("xc", [N, D])
        self.aT = sb("aT", [128, 256])
        self.ctxT = sb("ctxT", [C, 2, NC_])
        self.ps = [ctx.enter_context(nc.psum_tensor(f"bank{i}", [128, 512], F32)) for i in range(8)]


def setup(nc, ctx, M, d):
    sem = lambda n: ctx.enter_context(nc.semaphore(n))
    x_loaded = [sem(f"x_loaded{k}") for k in range(8)]
    vectors_loaded, zeroed, placed, stats_done, means_done = (
        sem(n) for n in ("vectors_loaded", "zeroed", "placed", "stats_done0", "means_done0"))
    block = ctx.enter_context(nc.Block())

    @block.sync
    def _(sp):
        for k in range(8):
            sp.dma_start(M.X[:, 8 * k:8 * k + 8, :], d["x"][8 * k:8 * k + 8].rearrange("b n d -> n b d"))\
              .then_inc(x_loaded[k], 16)

    @block.scalar
    def _(act):
        names = ["n1_g", "n1_b", "n2_g", "n2_b", "n3_g", "n3_b"]
        for k, n in enumerate(names):
            act.dma_start(M.LN[:, k, :], d["L0_xattn_" + n].partition_broadcast(N)).then_inc(vectors_loaded, 16)
        names = ["L0_xattn_o1_b", "L0_xattn_o2_b", "L0_xattn_ff_b2", "L1_xattn_b_out"]
        for k, n in enumerate(names):
            act.dma_start(M.BIAS[:, k, :], d[n].partition_broadcast(N)).then_inc(vectors_loaded, 16)
        act.wait_ge(vectors_loaded, 160)

    @block.gpsimd
    def _(pool):
        pool.memset(M.ident[:, :], 0.0).then_inc(zeroed, 1)
        pool.memset(M.quad[:, :], 1.0).then_inc(zeroed, 1)
        pool.memset(M.half[:, :], -0.5).then_inc(zeroed, 1)
        pool.memset(M.eps[:, :], EPS).then_inc(zeroed, 1)
        pool.wait_ge(zeroed, 4)
        pool.affine_select(out=M.ident[:, :], in_=M.ident[:, :], compare_op=ALU.not_equal, fill=1.0, base=0,
                           pattern=[[-1, 128]], channel_multiplier=1).then_inc(placed, 1)
        pool.affine_select(out=M.quad[:, :], in_=M.quad[:, :], compare_op=ALU.is_ge, fill=0.0, base=0,
                           pattern=[[-32, 4]], channel_multiplier=1).then_inc(placed, 1)
        pool.wait_ge(placed, 2)
        pool.affine_select(out=M.quad[:, :], in_=M.quad[:, :], compare_op=ALU.is_ge, fill=0.0, base=31,
                           pattern=[[32, 4]], channel_multiplier=-1).then_inc(placed, 1)
        pool.wait_ge(placed, 3)

    @block.vector
    def _(dve):
        for k in range(8):
            dve.wait_ge(x_loaded[k], 16)
            with dve.Fori(2 * k, 2 * k + 2) as four:
                for e in range(4):
                    hold(dve, M)
                    dve.bn_stats(M.stats[:, e, :], M.X[:, 4 * four + e, :]).then_inc(stats_done, 1)
                dve.wait_ge(stats_done, 4 * (four + 1))
                hold(dve, M)
                for e in range(4):
                    dve.bn_aggr(M.mv1[:, e, :], M.stats[:, e, :]).then_inc(means_done, 1)
                dve.wait_ge(means_done, 5 * four + 4)
                dve.tensor_copy(M.MV[:, bass.ds(4 * four, 4), :], M.mv1[:, :, :]).then_inc(means_done, 1)
                dve.wait_ge(means_done, 5 * four + 5)


def row_statistics(dve, M, b, done, stats_done, means_done):
    hold(dve, M)
    dve.bn_stats(M.stats[:, 0, :], M.X[:, b, :]).then_inc(stats_done, 1)
    dve.wait_ge(stats_done, done + 1)
    hold(dve, M)
    dve.bn_aggr(M.mv1[:, 0, :], M.stats[:, 0, :]).then_inc(means_done, 1)
    dve.wait_ge(means_done, 2 * done + 1)
    dve.tensor_copy(M.MV[:, b, :], M.mv1[:, 0, :]).then_inc(means_done, 1)
    dve.wait_ge(means_done, 2 * done + 2)


NORM_STEPS = 8


def normalise(pool, M, j, u, ln, step, h_free):
    base = NORM_STEPS * j
    h, hs, X = M.h[:, u, :], M.hs[:, u], M.X[:, j, :]
    h_free(pool, j)
    hold(pool, M)
    pool.tensor_tensor(M.veps[:, :], M.MV[:, j, 1:2], M.eps[:, :], ALU.add).then_inc(step, 1)
    hold(pool, M)
    pool.tensor_tensor(M.xc[:, :], X, M.MV[:, j, 0:1].broadcast_to([N, D]), ALU.subtract).then_inc(step, 1)
    pool.wait_ge(step, base + 2)
    hold(pool, M)
    pool.tensor_tensor(M.rstd[:, :], M.veps[:, :], M.half[:, :], ALU.pow).then_inc(step, 1)
    pool.wait_ge(step, base + 3)
    hold(pool, M)
    pool.tensor_tensor(h, M.xc[:, :], M.rstd[:, :].broadcast_to([N, D]), ALU.mult).then_inc(step, 1)
    pool.wait_ge(step, base + 4)
    pool.tensor_tensor(M.xc[:, :], h, M.LN[:, ln, :], ALU.mult).then_inc(step, 1)
    pool.wait_ge(step, base + 5)
    pool.tensor_tensor(h, M.xc[:, :], M.LN[:, ln + 1, :], ALU.add).then_inc(step, 1)
    pool.wait_ge(step, base + 6)
    hold(pool, M)
    tail = h[:, D0:D].unsqueeze(1).broadcast_to([N, 2, D1])
    pool.tensor_copy(hs[:, 0::2, :], tail).then_inc(step, 1)
    pool.wait_ge(step, base + 7)
    high = hs[:, 0:1, :].bitcast(F32).broadcast_to([N, 2, D1])
    pool.tensor_tensor(hs[:, 1::2, :], tail, high, ALU.subtract).then_inc(step, 1)


def stack_weight(dve, raw, out, n, done, base):
    dve.tensor_copy(out[:, :], raw[:, :]).then_inc(done, 1)
    dve.wait_ge(done, base + 1)
    dve.tensor_tensor(out[64:128, :], raw[64:128, :], out[64:128, :].bitcast(F32), ALU.subtract).then_inc(done, 1)
    dve.wait_ge(done, base + 2)


def attention(nc, ctx, M, d, cross):
    tag = "c" if cross else "s"
    nk = NC_ if cross else N
    wname = "2" if cross else "1"
    ctx = ctx.enter_context(ExitStack())

    def sb(name, shape, dt=F32):
        return ctx.enter_context(nc.sbuf_tensor(f"{name}_{tag}", shape, dt))

    def sem(name):
        return ctx.enter_context(nc.semaphore(f"{name}_{tag}"))

    nq = D if cross else 3 * D
    wq0, wq_raw, wqs = sb("wq0", [D0, nq]), sb("wq_raw", [128, nq]), sb("wqs", [128, nq], F32R)
    wkv = sb("wkv", [C, 2 * D])
    wo0, wo1 = sb("wo0", [D0, D]), sb("wo1", [D1, D])
    qs, ks = sb("qs", [N, H * 32], F32R), sb("ks", [N, H * 32], F32R)
    qT, kT = sb("qT", [128, 2, GROUPS, N], F32R), sb("kT", [128, 2, GROUPS, N], F32R)
    kB = sb("kB", [128, 2, 4, N], F32R)
    p, pT = sb("p", [N, 2, 5, 512]), sb("pT", [128, 5, 512])
    sums = sb("sums", [N, 2, H])
    rec, rec8 = sb("rec", [N, H]), sb("rec8", [N, D])
    recT = sb("recT", [128, 256])
    v = sb("v", [128, 2, D])
    vpad = sb("vpad", [128, 2, H, 32])

    w_loaded, w_split, vpad_zero = sem("w_loaded"), sem("w_split"), sem("vpad_zero")
    blocks_ready = sem("blocks_ready")
    ctx_loaded = [sem("ctx_loaded0"), sem("ctx_loaded1")]
    norm_step, h_used = sem("norm_step"), sem("h_used")
    hT_ready, qkv_done, high_ready, v_copied, low_ready, v_ready = (
        sem(n) for n in ("hT_ready", "qkv_done", "high_ready", "v_copied", "low_ready", "v_ready"))
    turned, turned_copied, s_done, s_reduced = (sem(n) for n in ("turned", "turned_copied", "s_done", "s_reduced"))
    p_ready, p_turned, pT_even, pT_odd, pv_done = (
        sem(n) for n in ("p_ready", "p_turned", "pT_even", "pT_odd", "pv_done"))
    rec_ready, rec_turned, recT_ready = (sem(n) for n in ("rec_ready", "rec_turned", "recT_ready"))
    aT_ready, o_done, x_ready = (sem(n) for n in ("aT_ready", "o_done", "x_ready"))
    bias_added, stats_done, means_done = (sem(n) for n in ("bias_added", "stats_done", "means_done"))

    S, PT = M.ps[0:2], M.ps[2:4]
    PV, TR, QKV, TURN = M.ps[4:8]
    numA, numB = PV[:, 0:128], PV[0:32, 256:384]
    scale = DH ** -0.5

    def heads(c):
        return [4 * g + c for g in range(4)] if c < 4 else [16 + j for j in range(4)]

    def wait_pT(eng, i, c):
        if c % 2:
            eng.wait_ge(pT_odd, 2 * i + c // 2 + 1)
        else:
            eng.wait_ge(pT_even, 3 * i + c // 2 + 1)

    def pipeline(eng, stage):
        stage(0, 0, True, True, True)
        stage(1, 1, True, True, True)
        with eng.Fori(1, B // 2 - 2) as half:
            for u in range(2):
                stage(2 * half + u, u, True, True, True)
        stage(B - 4, 0, True, True, True)
        stage(B - 3, 1, False, True, True)
        stage(B - 2, 0, False, False, True)
        stage(B - 1, 1, False, False, False)

    block = ctx.enter_context(nc.Block())

    @block.sync
    def _(sp):
        q, o = d[f"L0_xattn_q{wname}"], d[f"L0_xattn_o{wname}_w"]
        k, vv = d[f"L0_xattn_k{wname}"], d[f"L0_xattn_v{wname}"]
        loads = [(wo0[:, :], o[0:D0]), (wo1[:, :], o[D0:D])]
        for n, w in enumerate([q] if cross else [q, k, vv]):
            loads.append((wq0[:, n * D:n * D + D], w[0:D0]))
            loads += [(wq_raw[32 * r:32 * r + 32, n * D:n * D + D], w[D0:D]) for r in range(4)]
        if cross:
            loads += [(wkv[:, 0:D], k), (wkv[:, D:2 * D], vv)]
        for to, src in loads:
            sp.dma_start(to, src).then_inc(w_loaded, 16)
        if cross:
            for u in range(2):
                sp.dma_start(M.ctxT[:, u, :], d["ctxT"][u]).then_inc(ctx_loaded[u], 16)
            with sp.Fori(0, (B - 2) // 2) as half:
                for u in range(2):
                    sp.wait_ge(qkv_done, 2 * half + u + 1)
                    sp.dma_start(M.ctxT[:, u, :], d["ctxT"][2 * half + u + 2]).then_inc(ctx_loaded[u], 16)
    n_loads = 2 + 5 * (1 if cross else 3) + (2 if cross else 0)

    @block.gpsimd
    def _(pool):
        pool.memset(vpad[:, :, :, :], 0.0).then_inc(vpad_zero, 1)
        pool.memset(kB[:, :, :, :].bitcast(F32), 0.0).then_inc(vpad_zero, 1)

        def h_free(pool, j):
            if isinstance(j, int) and j < 2:
                return
            pool.wait_ge(h_used, j - 1)

        def place_blocks(j, u):
            pool.wait_ge(turned_copied, 3 * (j + 1))
            if not (isinstance(j, int) and j < 2):
                pool.wait_ge(s_done, 5 * (j - 1))
            hold(pool, M)
            pool.tensor_tensor(kB[:, u, :, 0:nk], kT[:, u, 4:5, 0:nk].bitcast(F32).broadcast_to([128, 4, nk]),
                               M.quad[:, :].unsqueeze(2).broadcast_to([128, 4, nk]), ALU.mult).then_inc(blocks_ready, 1)

        def place_v(j, u):
            pool.wait_ge(v_copied, j + 1)
            if not (isinstance(j, int) and j < 2):
                pool.wait_ge(pv_done, 5 * (j - 1))
            hold(pool, M)
            to = bass.AP(vpad, u * H * 32, [[2 * H * 32, nk], [128, GROUPS], [32 + DH, 4], [1, DH]])
            pool.tensor_copy(to, v[0:nk, u, :].rearrange("p (g i e) -> p g i e", g=GROUPS, e=DH)).then_inc(v_ready, 1)

        def add_bias(j):
            pool.wait_ge(norm_step, NORM_STEPS * (j + 1))
            hold(pool, M)
            pool.tensor_tensor(M.X[:, j, :], M.X[:, j, :], M.BIAS[:, int(cross), :], ALU.add)\
                .then_inc(bias_added, 1)

        def ahead(j, u):
            normalise(pool, M, j, u, 2 * int(cross), norm_step, h_free)
            add_bias(j)

        pool.wait_ge(vpad_zero, 2)
        for j in range(3):
            ahead(j, j % 2)
        place_v(0, 0)
        place_blocks(0, 0)
        ahead(3, 1)
        place_v(1, 1)
        place_blocks(1, 1)
        with pool.Fori(1, (B - 2) // 2) as half:
            for u in range(2):
                j = 2 * half + u
                ahead(j + 2, u)
                place_v(j, u)
                place_blocks(j, u)
        place_v(B - 2, 0)
        place_blocks(B - 2, 0)
        place_v(B - 1, 1)
        place_blocks(B - 1, 1)

    @block.scalar
    def _(act):
        def copy_hT(j):
            act.wait_ge(h_used, j + 1)
            if not (isinstance(j, int) and j < 1):
                act.wait_ge(qkv_done, j)
            act.activation(M.hT[:, :], TR[:, 0:128], ACT.Copy).then_inc(hT_ready, 1)
            act.activation(M.hsT[:, :], TR[:, 128:256], ACT.Copy).then_inc(hT_ready, 1)

        def high_halves(j, u):
            act.wait_ge(qkv_done, j + 1)
            if not (isinstance(j, int) and j < 1):
                act.wait_ge(turned, 3 * j)
            if not (isinstance(j, int) and j < 2):
                act.wait_ge(v_ready, j - 1)
            q4 = QKV[:, 0:D].rearrange("p (n d) -> p n d", d=DH).unsqueeze(2).broadcast_to([N, H, 2, DH])
            k4 = QKV[0:nk, D:2 * D].rearrange("p (n d) -> p n d", d=DH).unsqueeze(2).broadcast_to([nk, H, 2, DH])
            act.activation(split_stack(qs[:, :], slice(0, None, 2)), q4, ACT.Copy).then_inc(high_ready, 1)
            act.activation(split_stack(ks[0:nk, :], slice(0, 2)), k4, ACT.Copy).then_inc(high_ready, 1)
            act.activation(v[0:nk, u, :], QKV[0:nk, 2 * D:3 * D], ACT.Copy).then_inc(v_copied, 1)

        def exps(j, u, c):
            act.wait_ge(s_reduced, 5 * j + c + 1)
            if not (isinstance(j, int) and j < 2):
                act.wait_ge(p_turned, 5 * (j - 2) + c + 1)
            if c == 0 and not (isinstance(j, int) and j < 2):
                act.wait_ge(rec_ready, 2 * (j - 1))
            for k, n in enumerate(heads(c)):
                last = act.activation(p[:, u, c, 128 * k:128 * k + nk], S[(u + c) % 2][:, 128 * k:128 * k + nk], ACT.Exp,
                                      bias=M.negmax[:, 4 * c + k:4 * c + k + 1], accum_out=sums[:, u, n:n + 1])
            last.then_inc(p_ready, 1)

        def copy_even(i, u, c):
            act.wait_ge(p_turned, 5 * i + c + 1)
            if not (isinstance(i, int) and i < 1):
                act.wait_ge(pv_done, 5 * (i - 1) + c + 1)
            act.activation(pT[0:nk, c, :], PT[(u + c) % 2][0:nk, :], ACT.Copy).then_inc(pT_even, 1)

        def copy_recT(i):
            act.wait_ge(rec_turned, i + 1)
            if not (isinstance(i, int) and i < 1):
                act.wait_ge(aT_ready, 2 * i)
            act.activation(recT[:, 0:128], TR[:, 256:384], ACT.Copy).then_inc(recT_ready, 1)
            act.activation(recT[0:32, 128:256], TR[0:32, 384:512], ACT.Copy).then_inc(recT_ready, 1)

        copy_hT(0)
        high_halves(0, 0)
        copy_hT(1)
        high_halves(1, 1)
        copy_hT(2)
        for c in range(5):
            exps(0, 0, c)

        def stage(i, u, h, a, b):
            for c in range(5):
                if c % 2 == 0:
                    copy_even(i, u, c)
                if b:
                    exps(i + 1, 1 - u, c)
                if a and c == 0:
                    high_halves(i + 2, u)
                if c == 1:
                    copy_recT(i)
                if h and c == 3:
                    copy_hT(i + 3)

        pipeline(act, stage)

    @block.vector
    def _(dve):
        dve.wait_ge(w_loaded, 16 * n_loads)
        for w in (wq0, wq_raw):
            dve.tensor_scalar(w[:, 0:D], w[:, 0:D], scale, None, op0=ALU.mult).then_inc(w_split, 1)
        dve.wait_ge(w_split, 2)
        stack_weight(dve, wq_raw, wqs, nq, w_split, 2)

        def low_halves(j):
            dve.wait_ge(high_ready, 2 * (j + 1))
            dve.wait_ge(v_copied, j + 1)
            q4 = QKV[:, 0:D].rearrange("p (n d) -> p n d", d=DH).unsqueeze(2).broadcast_to([N, H, 2, DH])
            k4 = QKV[0:nk, D:2 * D].rearrange("p (n d) -> p n d", d=DH).unsqueeze(2).broadcast_to([nk, H, 2, DH])
            qh = split_stack(qs[:, :], slice(0, 1)).bitcast(F32).broadcast_to([N, H, 2, DH])
            kh = split_stack(ks[0:nk, :], slice(0, 1)).bitcast(F32).broadcast_to([nk, H, 2, DH])
            dve.tensor_tensor(split_stack(qs[:, :], slice(1, None, 2)), q4, qh, ALU.subtract).then_inc(low_ready, 1)
            dve.tensor_tensor(split_stack(ks[0:nk, :], slice(2, 4)), k4, kh, ALU.subtract).then_inc(low_ready, 1)

        def copy_turned(j, u, part):
            dve.wait_ge(turned, 3 * j + part + 1)
            if part == 0 and not (isinstance(j, int) and j < 2):
                dve.wait_ge(s_done, 5 * (j - 1))
            if part == 0:
                out, src = qT[:, u, 0:4, :], TURN[:, :].rearrange("p (g n) -> p g n", g=4)
                dve.tensor_copy(out, src).then_inc(turned_copied, 1)
            elif part == 1:
                src = TURN[:, :].rearrange("p (g n) -> p g n", g=4)[:, :, 0:nk]
                dve.tensor_copy(kT[:, u, 0:4, 0:nk], src).then_inc(turned_copied, 1)
            else:
                dve.tensor_copy(qT[:, u, 4, :], TURN[:, 0:128])
                dve.tensor_copy(kT[:, u, 4, 0:nk], TURN[:, 128:128 + nk]).then_inc(turned_copied, 1)

        def reduce_max(j, u, c):
            dve.wait_ge(s_done, 5 * j + c + 1)
            src = S[(u + c) % 2][:, :].rearrange("p (g n) -> p g n", g=4)[:, :, 0:nk]
            dve.tensor_reduce(M.negmax[:, 4 * c:4 * c + 4], src, AX.X, ALU.max, negate=True).then_inc(s_reduced, 1)

        def copy_odd(i, u, c):
            dve.wait_ge(p_turned, 5 * i + c + 1)
            if not (isinstance(i, int) and i < 1):
                dve.wait_ge(pv_done, 5 * (i - 1) + c + 1)
            dve.tensor_copy(pT[0:nk, c, :], PT[(u + c) % 2][0:nk, :]).then_inc(pT_odd, 1)

        def reciprocals(i, u):
            dve.wait_ge(p_ready, 5 * (i + 1))
            if not (isinstance(i, int) and i < 1):
                dve.wait_ge(rec_turned, i)
            dve.reciprocal(rec[:, :], sums[:, u, :]).then_inc(rec_ready, 1)
            dve.wait_ge(rec_ready, 2 * i + 1)
            dve.tensor_copy(rec8[:, :].rearrange("p (n d) -> p n d", d=DH),
                            rec[:, :].unsqueeze(2).broadcast_to([N, H, DH])).then_inc(rec_ready, 1)

        def divide(i):
            dve.wait_ge(pv_done, 5 * (i + 1))
            dve.wait_ge(recT_ready, 2 * (i + 1))
            if not (isinstance(i, int) and i < 1):
                dve.wait_ge(o_done, i)
            dve.tensor_tensor(M.aT[:, 0:128], numA, recT[:, 0:128], ALU.mult).then_inc(aT_ready, 1)
            dve.tensor_tensor(M.aT[0:32, 128:256], numB, recT[0:32, 128:256], ALU.mult).then_inc(aT_ready, 1)

        def residual(i):
            dve.wait_ge(o_done, i + 1)
            dve.wait_ge(bias_added, i + 1)
            dve.tensor_tensor(M.X[:, i, :], QKV[:, 0:D], M.X[:, i, :], ALU.add).then_inc(x_ready, 1)
            dve.wait_ge(x_ready, i + 1)
            row_statistics(dve, M, i, i, stats_done, means_done)

        low_halves(0)
        for part in range(3):
            copy_turned(0, 0, part)
        low_halves(1)
        for part in range(3):
            copy_turned(1, 1, part)
        for c in range(5):
            reduce_max(0, 0, c)

        def stage(i, u, h, a, b):
            for c in range(5):
                if c % 2:
                    copy_odd(i, u, c)
                if b:
                    reduce_max(i + 1, 1 - u, c)
                if c == 0:
                    reciprocals(i, u)
                if a:
                    if c == 1:
                        low_halves(i + 2)
                    if c >= 2:
                        copy_turned(i + 2, u, c - 2)
                if c == 3 and not (isinstance(i, int) and i < 1):
                    residual(i - 1)
            divide(i)

        pipeline(dve, stage)
        residual(B - 1)

    @block.tensor
    def _(pe):
        def turn_h(j, u):
            pe.wait_ge(norm_step, NORM_STEPS * (j + 1))
            if not (isinstance(j, int) and j < 1):
                pe.wait_ge(hT_ready, 2 * j)
            if not (isinstance(j, int) and j < 3):
                pe.wait_ge(recT_ready, 2 * (j - 2))
            pe.transpose(TR[:, 0:128], M.h[:, u, 0:D0], M.ident[:, :])
            pe.transpose(TR[:, 128:256], M.hs[:, u].rearrange("p k d -> p (k d)").bitcast(F32), M.ident[:, :])\
              .then_inc(h_used, 1)

        def project(j, u):
            pe.wait_ge(hT_ready, 2 * (j + 1))
            if cross:
                pe.wait_ge(ctx_loaded[u], 16 * ((j - u) // 2 + 1) if isinstance(j, int) else ctx_count(j, u))
            if not (isinstance(j, int) and j < 1):
                pe.wait_ge(low_ready, 2 * j)
            if not (isinstance(j, int) and j < 4):
                pe.wait_ge(x_ready, j - 3)
            pe.matmul(QKV[:, 0:nq], M.hT[:, :], wq0[:, :], start=True, stop=False)
            last = pe.matmul(QKV[:, 0:nq], M.hsT[:, :], wqs[:, :], start=False, stop=True)
            if cross:
                last = pe.matmul(QKV[0:NC_, D:3 * D], M.ctxT[:, u, :], wkv[:, :], start=True, stop=True)
            last.then_inc(qkv_done, 1)

        def ctx_count(j, u):
            return 8 * j + (16 - 8 * u)

        def turn_stack(j, part):
            pe.wait_ge(low_ready, 2 * (j + 1))
            if part > 0 or not (isinstance(j, int) and j < 1):
                pe.wait_ge(turned_copied, 3 * j + part)
            blocks = [[(qs, g, g) for g in range(4)], [(ks, g, g) for g in range(4)], [(qs, 4, 0), (ks, 4, 1)]][part]
            for src, g, at in blocks:
                rows = N if src is qs else nk
                last = pe.transpose(TURN[:, 128 * at:128 * at + rows], src[0:rows, 128 * g:128 * g + 128].bitcast(F32),
                                    M.ident[0:rows, 0:rows])
            last.then_inc(turned, 1)

        def scores(j, u, c):
            if not (isinstance(j, int) and 5 * j + c < 2):
                pe.wait_ge(p_ready, 5 * j + c - 1)
            bank = S[(u + c) % 2]
            if c == 4:
                pe.wait_ge(blocks_ready, j + 1)
                last = pe.matmul(bank[:, :], qT[:, u, 4, :], kB[:, u].rearrange("p k n -> p (k n)"),
                                 start=True, stop=True)
            else:
                for g in range(4):
                    r = 32 * c
                    last = pe.matmul(bank[:, 128 * g:128 * g + nk], qT[r:r + 32, u, g, :], kT[r:r + 32, u, g, 0:nk],
                                     start=True, stop=True, tile_position=(r, 0))
            last.then_inc(s_done, 1)

        def turn_p(i, u, c):
            pe.wait_ge(p_ready, 5 * i + c + 1)
            if c >= 2:
                wait_pT(pe, i, c - 2)
            elif not (isinstance(i, int) and i < 1):
                wait_pT(pe, i - 1, c + 3)
            for k in range(4):
                last = pe.transpose(PT[(u + c) % 2][0:nk, 128 * k:128 * k + N], p[:, u, c, 128 * k:128 * k + nk],
                                    M.ident[:, :])
            last.then_inc(p_turned, 1)

        def turn_rec(i, j):
            pe.wait_ge(rec_ready, 2 * (i + 1))
            pe.wait_ge(hT_ready, 2 * j)
            pe.transpose(TR[:, 256:384], rec8[:, 0:D0], M.ident[:, :])
            pe.transpose(TR[0:32, 384:512], rec8[:, D0:D], M.ident[:, :]).then_inc(rec_turned, 1)

        def weighted(i, u, c):
            wait_pT(pe, i, c)
            if c == 0:
                pe.wait_ge(v_ready, i + 1)
                if not (isinstance(i, int) and i < 1):
                    pe.wait_ge(aT_ready, 2 * i)
            for k, n in enumerate(heads(c)):
                out = numA[32 * k:32 * k + 32, :] if c < 4 else numB
                last = pe.matmul(out, vpad[0:nk, u, n, :], pT[0:nk, c, 128 * k:128 * k + 128], start=(c == 0),
                                 stop=(c == 3 or (c == 4 and k == 3)), skip_group_check=True)
            last.then_inc(pv_done, 1)

        def project_out(i, j):
            pe.wait_ge(aT_ready, 2 * (i + 1))
            pe.wait_ge(low_ready, 2 * j)
            pe.matmul(QKV[:, 0:D], M.aT[:, 0:128], wo0[:, :], start=True, stop=False)
            pe.matmul(QKV[:, 0:D], M.aT[0:32, 128:256], wo1[:, :], start=False, stop=True).then_inc(o_done, 1)

        pe.wait_ge(w_split, 4)
        pe.wait_ge(w_loaded, 16 * n_loads)
        for j in range(2):
            turn_h(j, j)
            project(j, j)
            for part in range(3):
                turn_stack(j, part)
        turn_h(2, 0)
        pe.wait_ge(turned_copied, 3)
        for c in range(5):
            scores(0, 0, c)

        def stage(i, u, h, a, b):
            for c in range(5):
                turn_p(i, u, c)
                if b and c == 0:
                    pe.wait_ge(turned_copied, 3 * (i + 2))
                if b:
                    scores(i + 1, 1 - u, c)
                if a and c == 0:
                    project(i + 2, u)
                if c == 1:
                    turn_rec(i, min(i + 3, B) if isinstance(i, int) else i + 3)
                if a and c >= 2:
                    turn_stack(i + 2, c - 2)
                if c:
                    weighted(i, u, c - 1)
                if c == 3 and not (isinstance(i, int) and i < 1):
                    project_out(i - 1, min(i + 3, B) if isinstance(i, int) else i + 3)
                if h and c == 3:
                    turn_h(i + 3, 1 - u)
            weighted(i, u, 4)

        pipeline(pe, stage)
        project_out(B - 1, B)

    ctx.close()


def feed_forward(nc, ctx, M, d):
    ctx = ctx.enter_context(ExitStack())
    G, Q = B // 4, 4

    def sb(name, shape, dt=F32):
        return ctx.enter_context(nc.sbuf_tensor(f"{name}_f", shape, dt))

    def sem(name):
        return ctx.enter_context(nc.semaphore(f"{name}_f"))

    w1, w1_raw, w1s = sb("w1", [D0, 2 * FF]), sb("w1_raw", [128, 2 * FF]), sb("w1s", [128, 2 * FF], F32R)
    w2, b1 = sb("w2", [128, FT, D]), sb("b1", [128, 2 * FT])
    hT, hsT = sb("hT4", [128, 2, Q * N]), sb("hsT4", [128, 2, Q * N], F32R)
    gate, f = sb("gate", [128, 2, Q * N]), sb("f", [128, 2, FT, Q * N])
    w_loaded, w_split, norm_step, h_used, hT_ready, bias_added = (
        sem(n) for n in ("w_loaded", "w_split", "norm_step", "h_used", "hT_ready", "bias_added"))
    up_done, gate_ready, f_ready, down_done, x_ready = (
        sem(n) for n in ("up_done", "gate_ready", "f_ready", "down_done", "x_ready"))
    A, GP, DOWN = M.ps[0:2], M.ps[2:4], M.ps[4:6]
    TR = M.ps[6]
    block = ctx.enter_context(nc.Block())

    def pipeline(eng, stage, last):
        stage(0, 0, True, True, False)
        stage(1, 1, True, True, True)
        with eng.Fori(1, G // 2 - 1) as half:
            for u in range(2):
                stage(2 * half + u, u, True, True, True)
        stage(G - 2, 0, True, True, True)
        stage(G - 1, 1, True, False, True)
        if last:
            stage(G, 0, False, False, True)

    @block.sync
    def _(sp):
        sp.dma_start(w1[:, :], d["L0_xattn_ff_w1"][0:D0]).then_inc(w_loaded, 16)
        for r in range(4):
            sp.dma_start(w1_raw[32 * r:32 * r + 32, :], d["L0_xattn_ff_w1"][D0:D]).then_inc(w_loaded, 16)
        sp.dma_start(w2[:, :, :], d["L0_xattn_ff_w2"].rearrange("(t p) n -> p t n", p=128)).then_inc(w_loaded, 16)
        sp.dma_start(b1[:, :], d["ff_b1T"]).then_inc(w_loaded, 16)

    @block.gpsimd
    def _(pool):

        def h_free(pool, j):
            if isinstance(j, int) and j < 2:
                return
            pool.wait_ge(h_used, j - 1)

        def ahead(j, u):
            normalise(pool, M, j, u, 4, norm_step, h_free)
            pool.wait_ge(norm_step, NORM_STEPS * (j + 1))
            hold(pool, M)
            pool.tensor_tensor(M.X[:, j, :], M.X[:, j, :], M.BIAS[:, 2, :], ALU.add).then_inc(bias_added, 1)

        ahead(0, 0)
        ahead(1, 1)
        with pool.Fori(1, B // 2) as half:
            for u in range(2):
                ahead(2 * half + u, u)

    @block.scalar
    def _(act):
        def copy_hT(k, u, q):
            act.wait_ge(h_used, Q * k + q + 1)
            if q == 0 and not (isinstance(k, int) and k < 2):
                act.wait_ge(up_done, FT * (k - 1))
            act.activation(hT[:, u, N * q:N * q + N], TR[:, 0:128], ACT.Copy).then_inc(hT_ready, 1)
            act.activation(hsT[:, u, N * q:N * q + N], TR[:, 128:256], ACT.Copy).then_inc(hT_ready, 1)

        def gelu(k, u, t):
            act.wait_ge(up_done, FT * k + t + 1)
            if not (isinstance(k, int) and FT * k + t < 2):
                act.wait_ge(f_ready, FT * k + t - 1)
            act.activation(gate[:, (u + t) % 2, :], GP[(u + t) % 2][:, :], ACT.Gelu, bias=b1[:, FT + t:FT + t + 1])\
               .then_inc(gate_ready, 1)

        act.wait_ge(w_loaded, 16 * 7)
        for q in range(Q):
            copy_hT(0, 0, q)

        def stage(k, u, up, ahead, down):
            for t in range(FT):
                gelu(k, u, t)
                if ahead and t < Q:
                    copy_hT(k + 1, 1 - u, t)

        pipeline(act, stage, False)

    @block.vector
    def _(dve):
        dve.wait_ge(w_loaded, 16 * 7)
        stack_weight(dve, w1_raw, w1s, 2 * FF, w_split, 0)

        def gated(k, u, t):
            dve.wait_ge(gate_ready, FT * k + t + 1)
            if t == 0 and not (isinstance(k, int) and k < 2):
                dve.wait_ge(down_done, Q * (k - 1))
            dve.scalar_tensor_tensor(f[:, u, t, :], A[(u + t) % 2][:, :], b1[:, t:t + 1], gate[:, (u + t) % 2, :],
                                     ALU.add, ALU.mult).then_inc(f_ready, 1)

        def residual(k, q):
            j = Q * k + q
            dve.wait_ge(down_done, j + 1)
            dve.wait_ge(bias_added, j + 1)
            dve.tensor_tensor(M.X[:, j, :], DOWN[q % 2][:, 0:D], M.X[:, j, :], ALU.add).then_inc(x_ready, 1)

        def stage(k, u, up, ahead, down):
            for t in range(FT):
                if up:
                    gated(k, u, t)
                if down and t < Q:
                    residual(k - 1, t)

        pipeline(dve, stage, True)

    @block.tensor
    def _(pe):
        def turn_h(k, q):
            j = Q * k + q
            pe.wait_ge(norm_step, NORM_STEPS * (j + 1))
            if not (isinstance(j, int) and j < 1):
                pe.wait_ge(hT_ready, 2 * j)
            pe.transpose(TR[:, 0:128], M.h[:, q % 2, 0:D0], M.ident[:, :])
            pe.transpose(TR[:, 128:256], M.hs[:, q % 2].rearrange("p k d -> p (k d)").bitcast(F32), M.ident[:, :])\
              .then_inc(h_used, 1)

        def up_tile(k, u, t):
            if t == 0:
                pe.wait_ge(hT_ready, 2 * Q * (k + 1))
            if not (isinstance(k, int) and FT * k + t < 2):
                pe.wait_ge(f_ready, FT * k + t - 1)
            for bank, at in ((GP, FF), (A, 0)):
                out, cols = bank[(u + t) % 2][:, :], slice(at + 128 * t, at + 128 * t + 128)
                pe.matmul(out, w1[:, cols], hT[:, u, :], start=True, stop=False)
                last = pe.matmul(out, w1s[:, cols], hsT[:, u, :], start=False, stop=True)
            last.then_inc(up_done, 1)

        def down(k, u, q):
            j = Q * k + q
            pe.wait_ge(f_ready, FT * (k + 1))
            if not (isinstance(j, int) and j < 2):
                pe.wait_ge(x_ready, j - 1)
            for t in range(FT):
                last = pe.matmul(DOWN[q % 2][:, 0:D], f[:, u, t, N * q:N * q + N], w2[:, t, :], start=(t == 0),
                                 stop=(t == FT - 1))
            last.then_inc(down_done, 1)

        pe.wait_ge(w_loaded, 16 * 7)
        pe.wait_ge(w_split, 2)
        for q in range(Q):
            turn_h(0, q)

        def stage(k, u, up, ahead, down_):
            for t in range(FT):
                if up:
                    up_tile(k, u, t)
                if ahead and t < Q:
                    turn_h(k + 1, t)
                if down_ and t < Q:
                    down(k - 1, 1 - u, t)

        pipeline(pe, stage, True)

    ctx.close()


def second_block(nc, ctx, M, d, out):
    ctx = ctx.enter_context(ExitStack())

    def sb(name, shape, dt=F32):
        return ctx.enter_context(nc.sbuf_tensor(f"{name}_l", shape, dt))

    def sem(name):
        return ctx.enter_context(nc.semaphore(f"{name}_l"))

    S2, T2 = 2, 128
    NCH = 8
    wqa_a, wqa_b = sb("wqa_a", [LA, S2 * T2]), sb("wqa_b", [LB, S2 * T2])
    wk, wv, wvca = sb("wk", [C, S2 * T2]), sb("wv", [C, S2 * T2]), sb("wvca", [C, S2 * T2])
    wkca = sb("wkca", [C, D])
    wqT_a, wqT_b = sb("wqT_a", [LA, S2 * T2]), sb("wqT_b", [LB, S2 * T2])
    wout, E = sb("wout", [128, S2, D]), sb("E", [C, N])
    kmask, vmask = sb("kmask", [LA, 2, 32]), sb("vmask", [32, S2 * T2])
    caq = sb("caq", [128, 2, C])
    ca32 = sb("ca32", [C, 32])
    p, pT = sb("p", [128, 2, NCH, 256]), sb("pT", [128, 4, 512])
    sums = sb("sums", [128, 2, 2 * HL])
    rec, rec32 = sb("rec", [128, 2 * HL]), sb("rec32", [128, 2, HL * 32])
    recT1, recT = sb("recT1", [128, S2 * C]), sb("recT", [128, S2 * T2])
    x1, xpad = sb("x1", [N, 2, D]), sb("xpad", [N, 2, HL, 32])
    xT, k2 = sb("xT", [LA, 2 * N]), sb("k2", [LA, 2, CA])
    k2b = sb("k2b", [LA, 2, 32])
    wk2 = sb("wk2", [128, 2, S2 * 32])
    qk = sb("qk", [128, 2, S2 * T2 + S2 * NE])
    v, v2 = sb("v", [NE, 2, S2 * T2]), sb("v2", [32, 2, S2 * T2])
    p2, sum2, max2 = sb("p2", [C, 3, 32]), sb("sum2", [C, 2, HL]), sb("max2", [C, HL])
    p2T, hs1, hs, yt = sb("p2T", [32, N]), sb("hs1", [128, S2 * C]), sb("hs", [128, S2 * T2]), sb("yt", [N, 2, D])
    res = sb("res", [128, S2 * T2])

    w_loaded, zeroed = sem("w_loaded"), sem("zeroed")
    ctx_loaded = [sem("ctx_loaded0"), sem("ctx_loaded1")]
    x1_copied, xpad_copied, bias_added, k2b_ready, ca32_ready = (
        sem(n) for n in ("x1_copied", "xpad_copied", "bias_added", "k2b_ready", "ca32_ready"))
    turned, xT_ready, qk_done, qk_ready, v_done, v_ready, v2_ready, wk2_done, wk2_ready = (
        sem(n) for n in ("turned", "xT_ready", "qk_done", "qk_ready", "v_done", "v_ready", "v2_ready", "wk2_done",
                         "wk2_ready"))
    s_done, s_reduced, p_ready, p_turned, pT_even, pT_odd = (
        sem(n) for n in ("s_done", "s_reduced", "p_ready", "p_turned", "pT_even", "pT_odd"))
    rec_ready, rec_turned, recT_ready, pv_done, hs1_ready, hs_ready = (
        sem(n) for n in ("rec_ready", "rec_turned", "recT_ready", "pv_done", "hs1_ready", "hs_ready"))
    s2_done, max2_ready, e2_ready, sum2_ready, p2_ready, p2_turned, p2T_ready, ca2_done = (
        sem(n) for n in ("s2_done", "max2_ready", "e2_ready", "sum2_ready", "p2_ready", "p2_turned", "p2T_ready",
                         "ca2_done"))
    aT_ready, out_done, y_ready = sem("aT_ready"), sem("out_done"), sem("y_ready")
    stored = [sem("stored0"), sem("stored1")]

    S, PT = M.ps[0:2], M.ps[2:4]
    PV, PV1, TR, PRJ = M.ps[4:8]
    num, recT_ps, ca2_ps = PV[:, 0:S2 * T2], PV[:, 256:512], PV[:, 256:512]
    num1, recT1_ps = PV1[:, 0:S2 * C], PV1[:, 256:256 + S2 * C]
    s2_ps, p2T_ps = PV1[0:C, 0:32], PV1[0:32, 128:256]
    xT_ps, k2_ps, wk2_ps = TR[:, 0:2 * N], TR[0:LA, 256:264], TR[:, 320:320 + S2 * 32]
    scale = DL ** -0.5

    def pipeline(eng, stage):
        stage(0, 0, True, True)
        stage(1, 1, True, True)
        with eng.Fori(1, (B - 2) // 2) as half:
            for u in range(2):
                stage(2 * half + u, u, True, True)
        stage(B - 2, 0, False, True)
        stage(B - 1, 1, False, False)

    def first(j, n=1):
        return isinstance(j, int) and j < n

    def wait_pT(eng, i, t):
        eng.wait_ge(pT_odd if t % 2 else pT_even, 2 * i + t // 2 + 1)

    def copy_quad(copy, t):
        rows, cols = (N, C) if t < 2 else (NE, N)
        return copy(pT[0:rows, t, :].rearrange("p (k n) -> p k n", k=4)[:, :, 0:cols],
                    PT[t % 2][0:rows, :].rearrange("p (k n) -> p k n", k=4)[:, :, 0:cols])

    def loads_until(j, u):
        return 80 * ((j - u) // 2 + 1) if isinstance(j, int) else 40 * j + 80 - 40 * u

    block = ctx.enter_context(nc.Block())

    @block.sync
    def _(sp):
        loads = [(wqa_a, "wqa", 0, LA), (wqa_b, "wqa", LA, D), (wk, "l_wk", 0, C), (wv, "l_wv", 0, C),
                 (wvca, "l_wvca", 0, C), (wkca, "L1_xattn_Wk_ca", 0, C), (wqT_a, "l_wqT", 0, LA),
                 (wqT_b, "l_wqT", LA, D), (E, "spread", 0, C), (vmask, "vmask", 0, 32)]
        for to, name, r0, r1 in loads:
            sp.dma_start(to[:, :], d[name][r0:r1]).then_inc(w_loaded, 16)
        sp.dma_start(wout[:, :, :], d["l_wout"]).then_inc(w_loaded, 16)
        sp.dma_start(kmask[:, 0, :], d["kmask"][0:LA]).then_inc(w_loaded, 16)
        sp.dma_start(kmask[0:LB, 1, :], d["kmask"][LA:D]).then_inc(w_loaded, 16)

        def load_context(j, u):
            sp.dma_start(M.ctxT[:, u, :], d["ctxT"][j]).then_inc(ctx_loaded[u], 16)
            for r in range(4):
                sp.dma_start(caq[32 * r + DL:32 * r + DL + CA, u, :], d["ctx_768"][j, NE:NC_, :])\
                  .then_inc(ctx_loaded[u], 16)

        def write(i, u):
            sp.wait_ge(y_ready, i + 1)
            sp.dma_start(out[i], yt[:, u, :]).then_inc(stored[u], 16)

        sp.wait_ge(zeroed, 2)
        load_context(0, 0)
        load_context(1, 1)

        def stage(i, u, more):
            sp.wait_ge(v_done, i + 1)
            sp.wait_ge(s_done, NCH * i + 4)
            load_context(i + 2, u)
            if more:
                write(i - 1, 1 - u)

        stage(0, 0, False)
        stage(1, 1, True)
        with sp.Fori(1, (B - 2) // 2) as half:
            for u in range(2):
                stage(2 * half + u, u, True)
        write(B - 3, 1)
        write(B - 2, 0)
        write(B - 1, 1)
        for u in range(2):
            sp.wait_ge(stored[u], 8 * B)

    @block.gpsimd
    def _(pool):
        pool.memset(caq[:, :, :], 0.0).then_inc(zeroed, 1)
        pool.memset(xpad[:, :, :, :], 0.0).then_inc(zeroed, 1)
        pool.memset(k2b[:, :, :], 0.0).then_inc(zeroed, 1)
        pool.wait_ge(zeroed, 3)
        pool.wait_ge(w_loaded, 16 * 13)

        def copy_x1(j, u):
            if not first(j, 2):
                pool.wait_ge(turned, j - 1)
            hold(pool, M)
            pool.tensor_copy(x1[:, u, :], M.X[:, j, :]).then_inc(x1_copied, 1)

        def copy_xpad(j, u):
            if not first(j, 2):
                pool.wait_ge(pv_done, 4 * (j - 2) + 2)
            hold(pool, M)
            pool.tensor_copy(xpad[:, u, :, 0:DL], M.X[:, j, :].rearrange("p (n d) -> p n d", d=DL))\
                .then_inc(xpad_copied, 1)
            pool.wait_ge(x1_copied, j + 1)
            pool.wait_ge(xpad_copied, j + 1)
            hold(pool, M)
            pool.tensor_tensor(M.X[:, j, :], M.X[:, j, :], M.BIAS[:, 3, :], ALU.add).then_inc(bias_added, 1)

        def repeat_ca(j, u):
            pool.wait_ge(ctx_loaded[u], loads_until(j, u))
            if not first(j):
                pool.wait_ge(v_done, j)
            hold(pool, M)
            pool.tensor_copy(ca32[:, :].rearrange("p (n t) -> p n t", t=CA),
                             M.ctxT[:, u, NE:NC_].unsqueeze(1).broadcast_to([C, HL, CA])).then_inc(ca32_ready, 1)

        def block_keys(j):
            pool.wait_ge(xT_ready, 4 * (j + 1))
            if not first(j):
                pool.wait_ge(wk2_done, j)
            for s, rows in ((0, LA), (1, LB)):
                pool.tensor_tensor(k2b[0:rows, s, :].rearrange("p (n t) -> p n t", t=CA),
                                   k2[0:rows, s, :].unsqueeze(1).broadcast_to([rows, HL, CA]),
                                   kmask[0:rows, s, :].rearrange("p (n t) -> p n t", t=CA), ALU.mult)\
                    .then_inc(k2b_ready, 1)

        def ahead(j, u, more=True):
            copy_xpad(j, u)
            repeat_ca(j, u)
            block_keys(j)
            if more:
                copy_x1(j + 1, 1 - u)

        copy_x1(0, 0)
        ahead(0, 0)
        ahead(1, 1)
        with pool.Fori(1, B // 2 - 1) as half:
            for u in range(2):
                ahead(2 * half + u, u)
        ahead(B - 2, 0)
        ahead(B - 1, 1, False)

    @block.scalar
    def _(act):
        def copy_xT(j):
            act.wait_ge(turned, j + 1)
            if not first(j):
                act.wait_ge(qk_done, j)
                act.wait_ge(k2b_ready, 2 * j)
            act.activation(xT[:, 0:N], xT_ps[0:LA, 0:N], ACT.Copy).then_inc(xT_ready, 1)
            act.activation(xT[0:LB, N:2 * N], xT_ps[0:LB, N:2 * N], ACT.Copy).then_inc(xT_ready, 1)
            act.activation(k2[:, 0, :], k2_ps[:, 0:CA], ACT.Copy).then_inc(xT_ready, 1)
            act.activation(k2[0:LB, 1, :], k2_ps[0:LB, CA:2 * CA], ACT.Copy).then_inc(xT_ready, 1)

        def copy_qk(j, u):
            act.wait_ge(qk_done, j + 1)
            if not first(j, 2):
                act.wait_ge(s_done, NCH * (j - 1))
            act.activation(qk[:, u, 0:S2 * T2], PRJ[:, 0:S2 * T2], ACT.Copy, scale=scale)
            act.activation(qk[:, u, S2 * T2:], PRJ[:, S2 * T2:S2 * T2 + S2 * NE], ACT.Copy).then_inc(qk_ready, 1)

        def copy_v(j, u):
            act.wait_ge(v_done, j + 1)
            if not first(j, 2):
                act.wait_ge(pv_done, 4 * (j - 1))
            act.activation(v[:, u, :], PRJ[0:NE, 0:S2 * T2], ACT.Copy).then_inc(v_ready, 1)

        def copy_wk2(j, u):
            act.wait_ge(wk2_done, j + 1)
            if not first(j, 2):
                act.wait_ge(s2_done, j - 1)
            act.activation(wk2[:, u, :], wk2_ps, ACT.Copy).then_inc(wk2_ready, 1)

        def exps(j, u, c):
            act.wait_ge(s_reduced, NCH * j + c + 1)
            if not first(j, 2):
                act.wait_ge(p_turned, 4 * (j - 2) + c // 2 + 1)
                if c == 0:
                    act.wait_ge(rec_ready, 4 * (j - 1))
            rows, cols = (C, N) if c < 4 else (N, NE)
            for m in (2 * c, 2 * c + 1):
                at = 128 * (m % 2)
                last = act.activation(p[0:rows, u, c, at:at + cols], S[c % 2][0:rows, at:at + cols], ACT.Exp,
                                      bias=M.negmax[0:rows, m:m + 1], accum_out=sums[0:rows, u, m:m + 1])
            last.then_inc(p_ready, 1)

        def copy_even(i, t):
            act.wait_ge(p_turned, 4 * i + t + 1)
            if not first(i):
                act.wait_ge(pv_done, 4 * (i - 1) + t + 1)
            copy_quad(lambda to, src: act.activation(to, src, ACT.Copy), t).then_inc(pT_even, 1)

        def copy_recT1(i):
            act.wait_ge(rec_turned, 2 * i + 1)
            if not first(i):
                act.wait_ge(hs1_ready, i)
            act.activation(recT1[:, :], recT1_ps, ACT.Copy).then_inc(recT_ready, 1)

        def copy_recT(i):
            act.wait_ge(rec_turned, 2 * i + 2)
            if not first(i):
                act.wait_ge(hs_ready, 2 * i - 1)
            act.activation(recT[:, :], recT_ps, ACT.Copy).then_inc(recT_ready, 1)

        def exp2(i):
            act.wait_ge(max2_ready, 2 * (i + 1))
            act.activation(p2[:, 1, :], p2[:, 0, :], ACT.Exp, scale=scale).then_inc(e2_ready, 1)

        def copy_p2T(i):
            act.wait_ge(p2_turned, i + 1)
            if not first(i):
                act.wait_ge(ca2_done, i)
            act.activation(p2T[:, :], p2T_ps, ACT.Copy).then_inc(p2T_ready, 1)

        for j in range(2):
            copy_xT(j)
            copy_qk(j, j)
            copy_v(j, j)
            copy_wk2(j, j)
        for c in range(NCH):
            exps(0, 0, c)

        def stage(i, u, a, b):
            def exps_next(c):
                if b:
                    exps(i + 1, 1 - u, c)

            copy_even(i, 0)
            exps_next(0)
            if not first(i):
                copy_p2T(i - 1)
            exps_next(1)
            exps_next(2)
            copy_recT1(i)
            if a:
                copy_xT(i + 2)
            exps_next(3)
            copy_even(i, 2)
            exps_next(4)
            copy_recT(i)
            exps_next(5)
            exps_next(6)
            exp2(i)
            if a:
                copy_qk(i + 2, u)
            exps_next(7)
            if a:
                copy_wk2(i + 2, u)
                copy_v(i + 2, u)

        pipeline(act, stage)
        copy_p2T(B - 1)

    @block.vector
    def _(dve):
        dve.wait_ge(w_loaded, 16 * 13)

        def block_values(j, u):
            dve.wait_ge(v_ready, j + 1)
            if not first(j, 2):
                dve.wait_ge(ca2_done, j - 1)
            dve.tensor_tensor(v2[:, u, :], PRJ[0:32, S2 * T2:2 * S2 * T2], vmask[:, :], ALU.mult).then_inc(v2_ready, 1)

        def reduce_max(j, c):
            dve.wait_ge(s_done, NCH * j + c + 1)
            rows, cols = (C, N) if c < 4 else (N, NE)
            src = S[c % 2][0:rows, 0:256].rearrange("p (k n) -> p k n", k=2)[:, :, 0:cols]
            dve.tensor_reduce(M.negmax[0:rows, 2 * c:2 * c + 2], src, AX.X, ALU.max, negate=True).then_inc(s_reduced, 1)

        def copy_odd(i, t):
            dve.wait_ge(p_turned, 4 * i + t + 1)
            if not first(i):
                dve.wait_ge(pv_done, 4 * (i - 1) + t + 1)
            copy_quad(dve.tensor_copy, t).then_inc(pT_odd, 1)

        def reciprocals(i, u, main):
            dve.wait_ge(p_ready, NCH * i + 4 + 4 * main)
            if not first(i):
                dve.wait_ge(rec_turned, 2 * (i - 1) + main + 1)
            rows, mine = (N if main else C), slice(HL * main, HL * main + HL)
            dve.reciprocal(rec[0:rows, mine], sums[0:rows, u, mine]).then_inc(rec_ready, 1)
            dve.wait_ge(rec_ready, 4 * i + 2 * main + 1)
            dve.tensor_copy(rec32[0:rows, main, :].rearrange("p (n e) -> p n e", n=HL),
                            rec[0:rows, mine].unsqueeze(2).broadcast_to([rows, HL, 32])).then_inc(rec_ready, 1)

        def divide1(i):
            dve.wait_ge(pv_done, 4 * i + 2)
            dve.wait_ge(recT_ready, 2 * i + 1)
            if not first(i):
                dve.wait_ge(s2_done, i)
            dve.tensor_tensor(hs1[:, :], num1, recT1[:, :], ALU.mult).then_inc(hs1_ready, 1)

        def divide(i):
            dve.wait_ge(pv_done, 4 * (i + 1))
            dve.wait_ge(recT_ready, 2 * i + 2)
            if not first(i):
                dve.wait_ge(hs_ready, 2 * i)
            dve.tensor_tensor(hs[:, :], num, recT[:, :], ALU.mult).then_inc(hs_ready, 1)

        def less_max2(i):
            dve.wait_ge(s2_done, i + 1)
            if not first(i):
                dve.wait_ge(max2_ready, 2 * i)
            s2 = s2_ps.rearrange("p (n t) -> p n t", t=CA)
            dve.tensor_reduce(max2[:, :], s2, AX.X, ALU.max).then_inc(max2_ready, 1)
            dve.wait_ge(max2_ready, 2 * i + 1)
            dve.tensor_tensor(p2[:, 0, :].rearrange("p (n t) -> p n t", t=CA), s2,
                              max2[:, :].unsqueeze(2).broadcast_to([C, HL, CA]), ALU.subtract).then_inc(max2_ready, 1)

        def divide2(i):
            dve.wait_ge(e2_ready, i + 1)
            if not first(i):
                dve.wait_ge(p2_ready, i)
                dve.wait_ge(p2_turned, i)
            e2 = p2[:, 1, :].rearrange("p (n t) -> p n t", t=CA)
            dve.tensor_reduce(sum2[:, 0, :], e2, AX.X, ALU.add).then_inc(sum2_ready, 1)
            dve.wait_ge(sum2_ready, 2 * i + 1)
            dve.reciprocal(sum2[:, 1, :], sum2[:, 0, :]).then_inc(sum2_ready, 1)
            dve.wait_ge(sum2_ready, 2 * i + 2)
            dve.tensor_tensor(p2[:, 2, :].rearrange("p (n t) -> p n t", t=CA), e2,
                              sum2[:, 1, :].unsqueeze(2).broadcast_to([C, HL, CA]), ALU.mult).then_inc(p2_ready, 1)

        def add_branch(i):
            dve.wait_ge(ca2_done, i + 1)
            dve.wait_ge(hs_ready, 2 * i + 1)
            if not first(i):
                dve.wait_ge(out_done, i)
            dve.tensor_tensor(res[:, :], ca2_ps, hs[:, :], ALU.add).then_inc(hs_ready, 1)

        def result(i, u):
            dve.wait_ge(out_done, i + 1)
            dve.wait_ge(bias_added, i + 1)
            if not first(i, 2):
                dve.wait_ge(stored[u], 16 * ((i - u) // 2) if isinstance(i, int) else 8 * i - 8 * u)
            dve.tensor_tensor(yt[:, u, :], PRJ[:, 0:D], M.X[:, i, :], ALU.add).then_inc(y_ready, 1)

        block_values(0, 0)
        for c in range(NCH):
            reduce_max(0, c)

        def stage(i, u, a, b):
            def reduce_next(*chunks):
                for c in chunks if b else ():
                    reduce_max(i + 1, c)

            reciprocals(i, u, 0)
            reduce_next(0)
            reciprocals(i, u, 1)
            reduce_next(1)
            copy_odd(i, 1)
            reduce_next(2)
            if not first(i):
                add_branch(i - 1)
            if b:
                block_values(i + 1, 1 - u)
            reduce_next(3, 4)
            divide1(i)
            copy_odd(i, 3)
            reduce_next(5)
            if not first(i):
                result(i - 1, 1 - u)
            less_max2(i)
            reduce_next(6)
            divide(i)
            divide2(i)
            reduce_next(7)

        pipeline(dve, stage)
        add_branch(B - 1)
        result(B - 1, 1)

    @block.tensor
    def _(pe):
        def q_of(u, s, j):
            return qk[32 * j:32 * j + 32, u, T2 * s:T2 * s + N]

        def k_of(u, s, j):
            return qk[32 * j:32 * j + 32, u, S2 * T2 + NE * s:S2 * T2 + NE * s + NE]

        def turn(j, u):
            pe.wait_ge(x1_copied, j + 1)
            pe.wait_ge(ctx_loaded[u], loads_until(j, u))
            if not first(j):
                pe.wait_ge(wk2_ready, j)
            pe.transpose(TR[0:LA, 0:N], x1[:, u, 0:LA], M.ident[:, :])
            pe.transpose(TR[0:LB, N:2 * N], x1[:, u, LA:D], M.ident[:, :])
            ca = M.ctxT[:, u, NE:NC_]
            pe.matmul(k2_ps[:, 0:CA], wkca[:, 0:LA], ca, start=True, stop=True)
            pe.matmul(k2_ps[0:LB, CA:2 * CA], wkca[:, LA:D], ca, start=True, stop=True).then_inc(turned, 1)

        def project_qk(j, u):
            pe.wait_ge(xT_ready, 4 * (j + 1))
            if not first(j):
                pe.wait_ge(v2_ready, j)
            if not first(j, 3):
                pe.wait_ge(y_ready, j - 2)
            for s in range(S2):
                cols = slice(T2 * s, T2 * s + T2)
                pe.matmul(PRJ[:, cols], wqa_a[:, cols], xT[:, 0:N], start=True, stop=False)
                pe.matmul(PRJ[:, cols], wqa_b[:, cols], xT[0:LB, N:2 * N], start=False, stop=True)
            for s in range(S2):
                last = pe.matmul(PRJ[:, S2 * T2 + NE * s:S2 * T2 + NE * s + NE], wk[:, T2 * s:T2 * s + T2],
                                 M.ctxT[:, u, 0:NE], start=True, stop=True)
            last.then_inc(qk_done, 1)

        def project_v(j, u):
            pe.wait_ge(qk_ready, j + 1)
            pe.wait_ge(ca32_ready, j + 1)
            pe.matmul(PRJ[0:NE, 0:S2 * T2], M.ctxT[:, u, 0:NE], wv[:, :], start=True, stop=True)
            pe.matmul(PRJ[0:32, S2 * T2:2 * S2 * T2], ca32[:, :], wvca[:, :], start=True, stop=True).then_inc(v_done, 1)

        def fold_keys(j, u):
            pe.wait_ge(k2b_ready, 2 * (j + 1))
            for s in range(S2):
                out = wk2_ps[:, 32 * s:32 * s + 32]
                pe.matmul(out, wqT_a[:, T2 * s:T2 * s + T2], k2b[:, 0, :], start=True, stop=False)
                last = pe.matmul(out, wqT_b[:, T2 * s:T2 * s + T2], k2b[0:LB, 1, :], start=False, stop=True)
            last.then_inc(wk2_done, 1)

        def scores(j, u, c):
            if not (isinstance(j, int) and NCH * j + c < 2):
                pe.wait_ge(p_ready, NCH * j + c - 1)
            bank, r = S[c % 2], c % 4
            if c < 4:
                last = pe.matmul(bank[0:C, 0:256], caq[32 * r:32 * r + 32, u, :], qk[32 * r:32 * r + 32, u, 0:256],
                                 start=True, stop=True, tile_position=(32 * r, 0))
            else:
                for s in range(S2):
                    last = pe.matmul(bank[:, 128 * s:128 * s + NE], q_of(u, s, r), k_of(u, s, r),
                                     start=True, stop=True, tile_position=(32 * r, 0))
            last.then_inc(s_done, 1)

        def turn_p(i, u, t):
            pe.wait_ge(p_ready, NCH * i + 2 * t + 2)
            if t >= 2:
                wait_pT(pe, i, t - 2)
            elif not first(i):
                wait_pT(pe, i - 1, t + 2)
            rows, cols = (N, C) if t < 2 else (NE, N)
            for k in range(4):
                at = 128 * (k % 2)
                last = pe.transpose(PT[t % 2][0:rows, 128 * k:128 * k + cols], p[0:cols, u, 2 * t + k // 2, at:at + rows],
                                    M.ident[0:cols, 0:cols])
            last.then_inc(p_turned, 1)

        def turn_rec1(i):
            pe.wait_ge(rec_ready, 4 * i + 2)
            if not first(i):
                pe.wait_ge(p2T_ready, i)
            for t in range(S2):
                last = pe.transpose(recT1_ps[:, C * t:C * t + C], rec32[0:C, 0, 128 * t:128 * t + 128], M.ident[0:C, 0:C])
            last.then_inc(rec_turned, 1)

        def turn_rec(i):
            pe.wait_ge(rec_ready, 4 * i + 4)
            if not first(i):
                pe.wait_ge(hs_ready, 2 * i)
            for t in range(S2):
                last = pe.transpose(recT_ps[:, T2 * t:T2 * t + T2], rec32[:, 1, 128 * t:128 * t + 128], M.ident[:, :])
            last.then_inc(rec_turned, 1)

        def weighted(i, u, t):
            wait_pT(pe, i, t)
            if t == 0:
                pe.wait_ge(xpad_copied, i + 1)
            if t % 2 == 0:
                pe.wait_ge(recT_ready, 2 * i + t // 2 + 1)
            branch, slot = t < 2, t % 2
            rows, cols = (N, C) if branch else (NE, N)
            out = num1 if branch else num
            for k in range(4):
                values = xpad[:, u, 4 * slot + k, :] if branch else v[:, u, T2 * slot + 32 * k:T2 * slot + 32 * k + 32]
                last = pe.matmul(out[32 * k:32 * k + 32, cols * slot:cols * slot + cols], values,
                                 pT[0:rows, t, 128 * k:128 * k + cols], start=True, stop=True)
            last.then_inc(pv_done, 1)

        def scores2(i, u):
            pe.wait_ge(hs1_ready, i + 1)
            for t in range(S2):
                last = pe.matmul(s2_ps, hs1[:, C * t:C * t + C], wk2[:, u, 32 * t:32 * t + 32], start=(t == 0),
                                 stop=(t == 1))
            last.then_inc(s2_done, 1)

        def turn_p2(i):
            pe.wait_ge(p2_ready, i + 1)
            pe.matmul(p2T_ps, p2[:, 2, :], E[:, :], start=True, stop=True).then_inc(p2_turned, 1)

        def weighted2(i, u):
            pe.wait_ge(p2T_ready, i + 1)
            pe.wait_ge(hs_ready, 2 * i + 1)
            for t in range(S2):
                last = pe.matmul(ca2_ps[:, T2 * t:T2 * t + T2], v2[:, u, T2 * t:T2 * t + T2], p2T[:, :], start=True,
                                 stop=True)
            last.then_inc(ca2_done, 1)

        def project_out(i, j):
            pe.wait_ge(hs_ready, 2 * (i + 1))
            pe.wait_ge(v2_ready, j)
            for t in range(S2):
                last = pe.matmul(PRJ[:, 0:D], res[:, T2 * t:T2 * t + T2], wout[:, t, :], start=(t == 0), stop=(t == 1))
            last.then_inc(out_done, 1)

        pe.wait_ge(w_loaded, 16 * 13)
        for j in range(2):
            turn(j, j)
            project_qk(j, j)
            project_v(j, j)
            fold_keys(j, j)
        for c in range(NCH):
            scores(0, 0, c)

        def stage(i, u, a, b):
            def scores_next(c):
                if b:
                    scores(i + 1, 1 - u, c)

            turn_p(i, u, 0)
            scores_next(0)
            scores_next(1)
            if not first(i):
                turn_p2(i - 1)
            turn_p(i, u, 1)
            scores_next(2)
            if not first(i):
                weighted2(i - 1, 1 - u)
            turn_rec1(i)
            if a:
                turn(i + 2, u)
            scores_next(3)
            turn_p(i, u, 2)
            weighted(i, u, 0)
            weighted(i, u, 1)
            scores_next(4)
            turn_rec(i)
            turn_p(i, u, 3)
            if not first(i):
                project_out(i - 1, min(i + 2, B) if isinstance(i, int) else i + 2)
            scores_next(5)
            weighted(i, u, 2)
            scores2(i, u)
            scores_next(6)
            if a:
                project_qk(i + 2, u)
            weighted(i, u, 3)
            scores_next(7)
            if a:
                fold_keys(i + 2, u)
                project_v(i + 2, u)

        pipeline(pe, stage)
        turn_p2(B - 1)
        weighted2(B - 1, 1)
        project_out(B - 1, B)

    ctx.close()


def layouts(given):
    import numpy as np

    def pairs(n):
        return 128 * (n % 2) + 32 * (n // 2)

    def fours(n):
        return 128 * (n // 4) + 32 * (n % 4)

    def padded(w, place):
        to = np.zeros((w.shape[0], 256), w.dtype)
        for n in range(HL):
            to[:, place(n):place(n) + DL] = w[:, DL * n:DL * n + DL]
        return to

    wqa = padded(given["L1_xattn_Wq"], pairs)
    spread = np.zeros((C, N), np.float32)
    kmask = np.zeros((D, HL * CA), np.float32)
    vmask = np.zeros((HL * CA, 256), np.float32)
    for n in range(HL):
        mine = slice(DL * n, DL * n + DL)
        wqa[mine, pairs(n) + DL:pairs(n) + DL + CA] = given["L1_xattn_Wq_ca"][:, mine].T
        kmask[mine, CA * n:CA * n + CA] = 1
        vmask[CA * n:CA * n + CA, fours(n):fours(n) + DL] = 1
    spread[np.linspace(0, C - 1, N).astype(np.int64), np.arange(N)] = 1
    return {
        "ctxT": given["ctx_768"].transpose(0, 2, 1),
        "ff_b1T": given["L0_xattn_ff_b1"].reshape(2 * FT, 128).T,
        "wqa": wqa,
        "l_wk": padded(given["L1_xattn_Wk"], pairs),
        "l_wv": padded(given["L1_xattn_Wv"], fours),
        "l_wvca": padded(given["L1_xattn_Wv_ca"], fours),
        "l_wqT": padded(given["L1_xattn_Wq"].T, fours),
        "l_wout": padded(given["L1_xattn_Wout"].T, fours).T.reshape(2, 128, D).transpose(1, 0, 2),
        "spread": spread, "kmask": kmask, "vmask": vmask,
    }


def build(nc, d, out):
    ctx = ExitStack()
    with ctx:
        M = Memory(nc, ctx)
        with ExitStack() as scope:
            setup(nc, scope, M, d)
        attention(nc, ctx, M, d, False)
        attention(nc, ctx, M, d, True)
        feed_forward(nc, ctx, M, d)
        second_block(nc, ctx, M, d, out)


def kernel(**inputs):
    import numpy as np
    import concourse.bacc as bacc
    from concourse.bass_utils import run_bass_kernel_spmd

    nc = bacc.Bacc("TRN2", target_bir_lowering=False, num_devices=1)
    given = {name: np.ascontiguousarray(a) for name, a in inputs.items()}
    laid = layouts(given)
    arrays = {"in_" + name: np.ascontiguousarray(a) for name, a in {**given, **laid}.items()}
    d = {name[3:]: nc.dram_tensor(name, a.shape, mybir.dt.from_np(a.dtype), kind="ExternalInput").ap()
         for name, a in arrays.items()}
    out = nc.dram_tensor("out_0", (B, N, D), F32, kind="ExternalOutput").ap()
    build(nc, d, out)
    return run_bass_kernel_spmd(nc, [arrays], core_ids=[0]).results[0]["out_0"]
```

```python
import concourse.bass as bass
from concourse import mybir
from contextlib import ExitStack

F32 = mybir.dt.float32
F32R = mybir.dt.float32r
ALU = mybir.AluOpType
ACT = mybir.ActivationFunctionType
AX = mybir.AxisListType

B, N, D = 64, 128, 160
NC_, C = 120, 96
H, DH = 20, 8
D0, D1 = 128, 32
GROUPS = H // 4
FF = 4 * D
FT = FF // 128
EPS = 1e-5
HL, DL = 8, 20
CA = 4
NE = NC_ - CA
LA, LB = 100, 60


def hold(eng, M):
    eng.sem_inc(M.held, 1)


def split_stack(ap, slots):
    v = ap.rearrange("p (n k d) -> p n k d", k=4, d=DH)
    return v[:, :, slots, :]


class Memory:

    def __init__(self, nc, ctx):
        def sb(name, shape, dt=F32):
            return ctx.enter_context(nc.sbuf_tensor(name, shape, dt))

        self.held = ctx.enter_context(nc.semaphore("held"))
        self.X = sb("X", [N, B, D])
        self.MV = sb("MV", [N, B, 2])
        self.veps, self.rstd = sb("veps", [N, 1]), sb("rstd", [N, 1])
        self.eps, self.half = sb("eps", [N, 1]), sb("half", [N, 1])
        self.LN = sb("LN", [N, 6, D])
        self.BIAS = sb("BIAS", [N, 4, D])
        self.ident = sb("ident", [128, 128])
        self.quad = sb("quad", [128, 4])
        self.negmax = sb("negmax", [128, H])
        self.stats = sb("stats", [N, 4, 6])
        self.mv1 = sb("mv1", [N, 4, 2])
        self.h = sb("h", [N, 2, D])
        self.hs = sb("hs", [N, 2, 4, D1], F32R)
        self.hT = sb("hT", [128, N])
        self.hsT = sb("hsT", [128, N], F32R)
        self.xc = sb("xc", [N, D])
        self.aT = sb("aT", [128, 256])
        self.ctxT = sb("ctxT", [C, 2, NC_])
        self.ps = [ctx.enter_context(nc.psum_tensor(f"bank{i}", [128, 512], F32)) for i in range(8)]


class AttentionWeights:

    def __init__(self, nc, ctx, cross):
        tag = "c" if cross else "s"

        def sb(name, shape):
            return ctx.enter_context(nc.sbuf_tensor(f"{name}_{tag}", shape, F32))

        self.cross, self.loaded = cross, ctx.enter_context(nc.semaphore(f"w_loaded_{tag}"))
        self.nq = D if cross else 3 * D
        self.wq0, self.wq_raw = sb("wq0", [D0, self.nq]), sb("wq_raw", [128, self.nq])
        self.wkv = sb("wkv", [C, 2 * D])
        self.wo0, self.wo1 = sb("wo0", [D0, D]), sb("wo1", [D1, D])
        self.count = 16 * (2 + 5 * (1 if cross else 3) + (2 if cross else 0))

    def load(self, sp, d):
        n = "2" if self.cross else "1"
        q, k, v, o = (d[f"L0_xattn_{name}"] for name in ("q" + n, "k" + n, "v" + n, f"o{n}_w"))
        loads = [(self.wo0[:, :], o[0:D0]), (self.wo1[:, :], o[D0:D])]
        for n, w in enumerate([q] if self.cross else [q, k, v]):
            loads.append((self.wq0[:, n * D:n * D + D], w[0:D0]))
            loads += [(self.wq_raw[32 * r:32 * r + 32, n * D:n * D + D], w[D0:D]) for r in range(4)]
        if self.cross:
            loads += [(self.wkv[:, 0:D], k), (self.wkv[:, D:2 * D], v)]
        for to, src in loads:
            sp.dma_start(to, src).then_inc(self.loaded, 16)


class FeedForwardWeights:

    def __init__(self, nc, ctx):
        def sb(name, shape):
            return ctx.enter_context(nc.sbuf_tensor(f"{name}_f", shape, F32))

        self.loaded, self.count = ctx.enter_context(nc.semaphore("w_loaded_f")), 16 * 7
        self.w1, self.w1_raw = sb("w1", [D0, 2 * FF]), sb("w1_raw", [128, 2 * FF])
        self.w2, self.b1 = sb("w2", [128, FT, D]), sb("b1", [128, 2 * FT])

    def load(self, sp, d):
        sp.dma_start(self.w1[:, :], d["L0_xattn_ff_w1"][0:D0]).then_inc(self.loaded, 16)
        for r in range(4):
            sp.dma_start(self.w1_raw[32 * r:32 * r + 32, :], d["L0_xattn_ff_w1"][D0:D]).then_inc(self.loaded, 16)
        sp.dma_start(self.w2[:, :, :], d["L0_xattn_ff_w2"].rearrange("(t p) n -> p t n", p=128))\
          .then_inc(self.loaded, 16)
        sp.dma_start(self.b1[:, :], d["ff_b1T"]).then_inc(self.loaded, 16)


class SecondWeights:

    def __init__(self, nc, ctx):
        def sb(name, shape):
            return ctx.enter_context(nc.sbuf_tensor(f"{name}_l", shape, F32))

        self.loaded, self.count = ctx.enter_context(nc.semaphore("w_loaded_l")), 16 * 8
        self.wqa_a, self.wqa_b = sb("wqa_a", [LA, 256]), sb("wqa_b", [LB, 256])
        self.wk, self.wv, self.wvca = sb("wk", [C, 256]), sb("wv", [C, 256]), sb("wvca", [C, 256])
        self.wout, self.E = sb("wout", [128, 2, D]), sb("E", [C, N])
        self.vmask = sb("vmask", [32, 256])
        self.wk2 = sb("wk2", [128, B, 64])

    def load(self, sp, d):
        loads = [(self.wqa_a, "wqa", 0, LA), (self.wqa_b, "wqa", LA, D), (self.wk, "l_wk", 0, C),
                 (self.wv, "l_wv", 0, C), (self.wvca, "l_wvca", 0, C), (self.E, "spread", 0, C),
                 (self.vmask, "vmask", 0, 32)]
        for to, name, r0, r1 in loads:
            sp.dma_start(to[:, :], d[name][r0:r1]).then_inc(self.loaded, 16)
        sp.dma_start(self.wout[:, :, :], d["l_wout"]).then_inc(self.loaded, 16)


def setup(nc, ctx, M, d, all_weights, wk2):
    def sb(name, shape):
        return ctx.enter_context(nc.sbuf_tensor(f"{name}_k", shape, F32))

    sem = lambda n: ctx.enter_context(nc.semaphore(n))
    x_loaded = [sem(f"x_loaded{k}") for k in range(8)]
    vectors_loaded, zeroed, placed, stats_done, means_done = (
        sem(n) for n in ("vectors_loaded", "zeroed", "placed", "stats_done0", "means_done0"))
    Q = 16
    parts = ((0, 0, LA), (1, LA, D))
    wkca, caT, kmask = sb("wkca", [C, D]), sb("caT", [C, B * CA]), sb("kmask", [LA, 2, HL * CA])
    wqT = sb("wqT", [LA, 2, 256])
    k2, k2b = sb("k2", [LA, 2, B * CA]), sb("k2b", [LA, 2, 2, Q * HL * CA])
    fold_loaded, k2_done, k2_ready, k2b_ready, folded, wk2_ready = (
        sem(n) for n in ("fold_loaded", "k2_done", "k2_ready", "k2b_ready", "folded", "wk2_ready"))
    k2_ps, fold_ps = M.ps[0:2], M.ps[2:6]
    block = ctx.enter_context(nc.Block())

    @block.sync
    def _(sp):
        for k in range(8):
            sp.dma_start(M.X[:, 8 * k:8 * k + 8, :], d["x"][8 * k:8 * k + 8].rearrange("b n d -> n b d"))\
              .then_inc(x_loaded[k], 16)
        for weights in all_weights:
            weights.load(sp, d)

    @block.tensor
    def _(pe):
        pe.wait_ge(fold_loaded, 16 * 6)
        for s, r0, r1 in parts:
            pe.matmul(k2_ps[s][0:r1 - r0, 0:B * CA], wkca[:, r0:r1], caT[:, :], start=True, stop=True)\
              .then_inc(k2_done, 1)
        for g in range(B // Q):
            pe.wait_ge(k2b_ready, 2 * (g + 1))
            if g >= 2:
                pe.wait_ge(wk2_ready, 2 * (g - 1))
            for t in range(2):
                for s, r0, r1 in parts:
                    last = pe.matmul(fold_ps[2 * (g % 2) + t][:, :], wqT[0:r1 - r0, s, 128 * t:128 * t + 128],
                                     k2b[0:r1 - r0, g % 2, s, :], start=(s == 0), stop=(s == 1))
                last.then_inc(folded, 1)

    @block.scalar
    def _(act):
        act.dma_start(wkca[:, :], d["L1_xattn_Wk_ca"]).then_inc(fold_loaded, 16)
        act.dma_start(caT[:, :], d["caT"]).then_inc(fold_loaded, 16)
        for s, r0, r1 in parts:
            act.dma_start(kmask[0:r1 - r0, s, :], d["kmask"][r0:r1]).then_inc(fold_loaded, 16)
            act.dma_start(wqT[0:r1 - r0, s, :], d["l_wqT"][r0:r1]).then_inc(fold_loaded, 16)
        names = ["n1_g", "n1_b", "n2_g", "n2_b", "n3_g", "n3_b"]
        for k, n in enumerate(names):
            act.dma_start(M.LN[:, k, :], d["L0_xattn_" + n].partition_broadcast(N)).then_inc(vectors_loaded, 16)
        names = ["L0_xattn_o1_b", "L0_xattn_o2_b", "L0_xattn_ff_b2", "L1_xattn_b_out"]
        for k, n in enumerate(names):
            act.dma_start(M.BIAS[:, k, :], d[n].partition_broadcast(N)).then_inc(vectors_loaded, 16)
        for s, r0, r1 in parts:
            act.wait_ge(k2_done, s + 1)
            act.activation(k2[0:r1 - r0, s, :], k2_ps[s][0:r1 - r0, 0:B * CA], ACT.Copy).then_inc(k2_ready, 1)
        for g in range(B // Q):
            for t in range(2):
                act.wait_ge(folded, 2 * g + t + 1)
                act.activation(wk2[:, Q * g:Q * g + Q, 32 * t:32 * t + 32],
                               fold_ps[2 * (g % 2) + t][:, :].rearrange("p (b n) -> p b n", b=Q), ACT.Copy)\
                   .then_inc(wk2_ready, 1)
        act.wait_ge(vectors_loaded, 160)

    @block.gpsimd
    def _(pool):
        pool.memset(M.ident[:, :], 0.0).then_inc(zeroed, 1)
        pool.memset(M.quad[:, :], 1.0).then_inc(zeroed, 1)
        pool.memset(M.half[:, :], -0.5).then_inc(zeroed, 1)
        pool.memset(M.eps[:, :], EPS).then_inc(zeroed, 1)
        pool.wait_ge(zeroed, 4)
        pool.affine_select(out=M.ident[:, :], in_=M.ident[:, :], compare_op=ALU.not_equal, fill=1.0, base=0,
                           pattern=[[-1, 128]], channel_multiplier=1).then_inc(placed, 1)
        pool.affine_select(out=M.quad[:, :], in_=M.quad[:, :], compare_op=ALU.is_ge, fill=0.0, base=0,
                           pattern=[[-32, 4]], channel_multiplier=1).then_inc(placed, 1)
        pool.wait_ge(placed, 2)
        pool.affine_select(out=M.quad[:, :], in_=M.quad[:, :], compare_op=ALU.is_ge, fill=0.0, base=31,
                           pattern=[[32, 4]], channel_multiplier=-1).then_inc(placed, 1)
        pool.wait_ge(placed, 3)
        pool.wait_ge(fold_loaded, 16 * 6)
        pool.wait_ge(k2_ready, 2)
        for g in range(B // Q):
            if g >= 2:
                pool.wait_ge(folded, 2 * (g - 1))
            for s, r0, r1 in parts:
                shape = [r1 - r0, Q, HL, CA]
                keys = k2[0:r1 - r0, s, Q * CA * g:Q * CA * (g + 1)].rearrange("p (b t) -> p b t", t=CA)
                mask = kmask[0:r1 - r0, s, :].rearrange("p (n t) -> p n t", t=CA)
                pool.tensor_tensor(k2b[0:r1 - r0, g % 2, s, :].rearrange("p (b n t) -> p b n t", b=Q, t=CA),
                                   keys.unsqueeze(2).broadcast_to(shape), mask.unsqueeze(1).broadcast_to(shape),
                                   ALU.mult).then_inc(k2b_ready, 1)

    @block.vector
    def _(dve):
        for k in range(8):
            dve.wait_ge(x_loaded[k], 16)
            with dve.Fori(2 * k, 2 * k + 2) as four:
                for e in range(4):
                    hold(dve, M)
                    dve.bn_stats(M.stats[:, e, :], M.X[:, 4 * four + e, :]).then_inc(stats_done, 1)
                dve.wait_ge(stats_done, 4 * (four + 1))
                hold(dve, M)
                for e in range(4):
                    dve.bn_aggr(M.mv1[:, e, :], M.stats[:, e, :]).then_inc(means_done, 1)
                dve.wait_ge(means_done, 5 * four + 4)
                dve.tensor_copy(M.MV[:, bass.ds(4 * four, 4), :], M.mv1[:, :, :]).then_inc(means_done, 1)
                dve.wait_ge(means_done, 5 * four + 5)


NORM_STEPS = 8


def normalise(pool, M, j, u, ln, step, h_free):
    base = NORM_STEPS * j
    h, hs, X = M.h[:, u, :], M.hs[:, u], M.X[:, j, :]
    h_free(pool, j)
    hold(pool, M)
    pool.tensor_tensor(M.veps[:, :], M.MV[:, j, 1:2], M.eps[:, :], ALU.add).then_inc(step, 1)
    hold(pool, M)
    pool.tensor_tensor(M.xc[:, :], X, M.MV[:, j, 0:1].broadcast_to([N, D]), ALU.subtract).then_inc(step, 1)
    pool.wait_ge(step, base + 2)
    hold(pool, M)
    pool.tensor_tensor(M.rstd[:, :], M.veps[:, :], M.half[:, :], ALU.pow).then_inc(step, 1)
    pool.wait_ge(step, base + 3)
    hold(pool, M)
    pool.tensor_tensor(h, M.xc[:, :], M.rstd[:, :].broadcast_to([N, D]), ALU.mult).then_inc(step, 1)
    pool.wait_ge(step, base + 4)
    pool.tensor_tensor(M.xc[:, :], h, M.LN[:, ln, :], ALU.mult).then_inc(step, 1)
    pool.wait_ge(step, base + 5)
    pool.tensor_tensor(h, M.xc[:, :], M.LN[:, ln + 1, :], ALU.add).then_inc(step, 1)
    pool.wait_ge(step, base + 6)
    hold(pool, M)
    tail = h[:, D0:D].unsqueeze(1).broadcast_to([N, 2, D1])
    pool.tensor_copy(hs[:, 0::2, :], tail).then_inc(step, 1)
    pool.wait_ge(step, base + 7)
    high = hs[:, 0:1, :].bitcast(F32).broadcast_to([N, 2, D1])
    pool.tensor_tensor(hs[:, 1::2, :], tail, high, ALU.subtract).then_inc(step, 1)


def stack_weight(dve, raw, out, n, done, base):
    dve.tensor_copy(out[:, :], raw[:, :]).then_inc(done, 1)
    dve.wait_ge(done, base + 1)
    dve.tensor_tensor(out[64:128, :], raw[64:128, :], out[64:128, :].bitcast(F32), ALU.subtract).then_inc(done, 1)
    dve.wait_ge(done, base + 2)


def attention(nc, ctx, M, d, weights):
    cross = weights.cross
    tag = "c" if cross else "s"
    nk = NC_ if cross else N
    ctx = ctx.enter_context(ExitStack())

    def sb(name, shape, dt=F32):
        return ctx.enter_context(nc.sbuf_tensor(f"{name}_{tag}", shape, dt))

    def sem(name):
        return ctx.enter_context(nc.semaphore(f"{name}_{tag}"))

    nq, wq0, wq_raw, wkv, wo0, wo1 = (
        weights.nq, weights.wq0, weights.wq_raw, weights.wkv, weights.wo0, weights.wo1)
    wqs = sb("wqs", [128, nq], F32R)
    qs, ks = sb("qs", [N, H * 32], F32R), sb("ks", [N, H * 32], F32R)
    qT, kT = sb("qT", [128, 2, GROUPS, N], F32R), sb("kT", [128, 2, GROUPS, N], F32R)
    kB = sb("kB", [128, 2, 4, N], F32R)
    p, pT = sb("p", [N, 2, 5, 512]), sb("pT", [128, 5, 512])
    sums = sb("sums", [N, 2, H])
    rec, rec8 = sb("rec", [N, H]), sb("rec8", [N, D])
    recT = sb("recT", [128, 256])
    v = sb("v", [128, 2, D])
    vpad = sb("vpad", [128, 2, H, 32])

    w_split, vpad_zero = sem("w_split"), sem("vpad_zero")
    blocks_ready = sem("blocks_ready")
    ctx_loaded = [sem("ctx_loaded0"), sem("ctx_loaded1")]
    norm_step, h_used = sem("norm_step"), sem("h_used")
    hT_ready, qkv_done, high_ready, v_copied, low_ready, v_ready = (
        sem(n) for n in ("hT_ready", "qkv_done", "high_ready", "v_copied", "low_ready", "v_ready"))
    turned, turned_copied, s_done, s_reduced = (sem(n) for n in ("turned", "turned_copied", "s_done", "s_reduced"))
    p_ready, p_turned, pT_even, pT_odd, pv_done = (
        sem(n) for n in ("p_ready", "p_turned", "pT_even", "pT_odd", "pv_done"))
    rec_ready, rec_turned, recT_ready = (sem(n) for n in ("rec_ready", "rec_turned", "recT_ready"))
    aT_ready, o_done, x_ready = (sem(n) for n in ("aT_ready", "o_done", "x_ready"))
    bias_added, stats_done, means_done = (sem(n) for n in ("bias_added", "stats_done", "means_done"))

    S, PT = M.ps[0:2], M.ps[2:4]
    PV, TR, QKV, TURN = M.ps[4:8]
    numA, numB = PV[:, 0:128], PV[0:32, 256:384]
    scale = DH ** -0.5

    def heads(c):
        return [4 * g + c for g in range(4)] if c < 4 else [16 + j for j in range(4)]

    def wait_pT(eng, i, c):
        if c % 2:
            eng.wait_ge(pT_odd, 2 * i + c // 2 + 1)
        else:
            eng.wait_ge(pT_even, 3 * i + c // 2 + 1)

    def pipeline(eng, stage):
        stage(0, 0, True, True, True)
        stage(1, 1, True, True, True)
        with eng.Fori(1, B // 2 - 2) as half:
            for u in range(2):
                stage(2 * half + u, u, True, True, True)
        stage(B - 4, 0, True, True, True)
        stage(B - 3, 1, False, True, True)
        stage(B - 2, 0, False, False, True)
        stage(B - 1, 1, False, False, False)

    block = ctx.enter_context(nc.Block())

    @block.sync
    def _(sp):
        if cross:
            for u in range(2):
                sp.dma_start(M.ctxT[:, u, :], d["ctxT"][u]).then_inc(ctx_loaded[u], 16)
            with sp.Fori(0, (B - 2) // 2) as half:
                for u in range(2):
                    sp.wait_ge(qkv_done, 2 * half + u + 1)
                    sp.dma_start(M.ctxT[:, u, :], d["ctxT"][2 * half + u + 2]).then_inc(ctx_loaded[u], 16)

    @block.gpsimd
    def _(pool):
        pool.memset(vpad[:, :, :, :], 0.0).then_inc(vpad_zero, 1)
        pool.memset(kB[:, :, :, :].bitcast(F32), 0.0).then_inc(vpad_zero, 1)

        def h_free(pool, j):
            if isinstance(j, int) and j < 2:
                return
            pool.wait_ge(h_used, j - 1)

        def place_blocks(j, u):
            pool.wait_ge(turned_copied, 3 * (j + 1))
            if not (isinstance(j, int) and j < 2):
                pool.wait_ge(s_done, 5 * (j - 1))
            hold(pool, M)
            pool.tensor_tensor(kB[:, u, :, 0:nk], kT[:, u, 4:5, 0:nk].bitcast(F32).broadcast_to([128, 4, nk]),
                               M.quad[:, :].unsqueeze(2).broadcast_to([128, 4, nk]), ALU.mult).then_inc(blocks_ready, 1)

        def place_v(j, u):
            pool.wait_ge(v_copied, j + 1)
            if not (isinstance(j, int) and j < 2):
                pool.wait_ge(pv_done, 5 * (j - 1))
            hold(pool, M)
            to = bass.AP(vpad, u * H * 32, [[2 * H * 32, nk], [128, GROUPS], [32 + DH, 4], [1, DH]])
            pool.tensor_copy(to, v[0:nk, u, :].rearrange("p (g i e) -> p g i e", g=GROUPS, e=DH)).then_inc(v_ready, 1)

        def add_bias(j):
            pool.wait_ge(norm_step, NORM_STEPS * (j + 1))
            hold(pool, M)
            pool.tensor_tensor(M.X[:, j, :], M.X[:, j, :], M.BIAS[:, int(cross), :], ALU.add)\
                .then_inc(bias_added, 1)

        def ahead(j, u):
            normalise(pool, M, j, u, 2 * int(cross), norm_step, h_free)
            add_bias(j)

        pool.wait_ge(vpad_zero, 2)
        for j in range(3):
            ahead(j, j % 2)
        place_v(0, 0)
        place_blocks(0, 0)
        ahead(3, 1)
        place_v(1, 1)
        place_blocks(1, 1)
        with pool.Fori(1, (B - 2) // 2) as half:
            for u in range(2):
                j = 2 * half + u
                ahead(j + 2, u)
                place_v(j, u)
                place_blocks(j, u)
        place_v(B - 2, 0)
        place_blocks(B - 2, 0)
        place_v(B - 1, 1)
        place_blocks(B - 1, 1)

    @block.scalar
    def _(act):
        def high_halves(j, u):
            act.wait_ge(qkv_done, j + 1)
            if not (isinstance(j, int) and j < 1):
                act.wait_ge(turned, 3 * j)
            if not (isinstance(j, int) and j < 2):
                act.wait_ge(v_ready, j - 1)
            q4 = QKV[:, 0:D].rearrange("p (n d) -> p n d", d=DH).unsqueeze(2).broadcast_to([N, H, 2, DH])
            k4 = QKV[0:nk, D:2 * D].rearrange("p (n d) -> p n d", d=DH).unsqueeze(2).broadcast_to([nk, H, 2, DH])
            act.activation(split_stack(qs[:, :], slice(0, None, 2)), q4, ACT.Copy).then_inc(high_ready, 1)
            act.activation(split_stack(ks[0:nk, :], slice(0, 2)), k4, ACT.Copy).then_inc(high_ready, 1)
            act.activation(v[0:nk, u, :], QKV[0:nk, 2 * D:3 * D], ACT.Copy).then_inc(v_copied, 1)

        def exps(j, u, c):
            act.wait_ge(s_reduced, 5 * j + c + 1)
            if not (isinstance(j, int) and j < 2):
                act.wait_ge(p_turned, 5 * (j - 2) + c + 1)
            if c == 0 and not (isinstance(j, int) and j < 2):
                act.wait_ge(rec_ready, 2 * (j - 1))
            for k, n in enumerate(heads(c)):
                last = act.activation(p[:, u, c, 128 * k:128 * k + nk], S[(u + c) % 2][:, 128 * k:128 * k + nk], ACT.Exp,
                                      bias=M.negmax[:, 4 * c + k:4 * c + k + 1], accum_out=sums[:, u, n:n + 1])
            last.then_inc(p_ready, 1)

        def copy_even(i, u, c):
            act.wait_ge(p_turned, 5 * i + c + 1)
            if not (isinstance(i, int) and i < 1):
                act.wait_ge(pv_done, 5 * (i - 1) + c + 1)
            act.activation(pT[0:nk, c, :], PT[(u + c) % 2][0:nk, :], ACT.Copy).then_inc(pT_even, 1)

        def copy_recT(i):
            act.wait_ge(rec_turned, i + 1)
            if not (isinstance(i, int) and i < 1):
                act.wait_ge(aT_ready, 2 * i)
            act.activation(recT[:, 0:128], TR[:, 256:384], ACT.Copy).then_inc(recT_ready, 1)
            act.activation(recT[0:32, 128:256], TR[0:32, 384:512], ACT.Copy).then_inc(recT_ready, 1)

        high_halves(0, 0)
        high_halves(1, 1)
        for c in range(5):
            exps(0, 0, c)

        def stage(i, u, h, a, b):
            for c in range(5):
                if c % 2 == 0:
                    copy_even(i, u, c)
                if b:
                    exps(i + 1, 1 - u, c)
                if a and c == 0:
                    high_halves(i + 2, u)
                if c == 2:
                    copy_recT(i)

        pipeline(act, stage)

    @block.vector
    def _(dve):
        dve.wait_ge(weights.loaded, weights.count)
        for w in (wq0, wq_raw):
            dve.tensor_scalar(w[:, 0:D], w[:, 0:D], scale, None, op0=ALU.mult).then_inc(w_split, 1)
        dve.wait_ge(w_split, 2)
        stack_weight(dve, wq_raw, wqs, nq, w_split, 2)

        def copy_hT(j):
            dve.wait_ge(h_used, j + 1)
            if not (isinstance(j, int) and j < 1):
                dve.wait_ge(qkv_done, j)
            dve.tensor_copy(M.hT[:, :], TR[:, 0:128]).then_inc(hT_ready, 1)
            dve.tensor_copy(M.hsT[:, :], TR[:, 128:256]).then_inc(hT_ready, 1)

        def low_halves(j):
            dve.wait_ge(high_ready, 2 * (j + 1))
            dve.wait_ge(v_copied, j + 1)
            q4 = QKV[:, 0:D].rearrange("p (n d) -> p n d", d=DH).unsqueeze(2).broadcast_to([N, H, 2, DH])
            k4 = QKV[0:nk, D:2 * D].rearrange("p (n d) -> p n d", d=DH).unsqueeze(2).broadcast_to([nk, H, 2, DH])
            qh = split_stack(qs[:, :], slice(0, 1)).bitcast(F32).broadcast_to([N, H, 2, DH])
            kh = split_stack(ks[0:nk, :], slice(0, 1)).bitcast(F32).broadcast_to([nk, H, 2, DH])
            dve.tensor_tensor(split_stack(qs[:, :], slice(1, None, 2)), q4, qh, ALU.subtract).then_inc(low_ready, 1)
            dve.tensor_tensor(split_stack(ks[0:nk, :], slice(2, 4)), k4, kh, ALU.subtract).then_inc(low_ready, 1)

        def copy_turned(j, u, part):
            dve.wait_ge(turned, 3 * j + part + 1)
            if part == 0 and not (isinstance(j, int) and j < 2):
                dve.wait_ge(s_done, 5 * (j - 1))
            if part == 0:
                out, src = qT[:, u, 0:4, :], TURN[:, :].rearrange("p (g n) -> p g n", g=4)
                dve.tensor_copy(out, src).then_inc(turned_copied, 1)
            elif part == 1:
                src = TURN[:, :].rearrange("p (g n) -> p g n", g=4)[:, :, 0:nk]
                dve.tensor_copy(kT[:, u, 0:4, 0:nk], src).then_inc(turned_copied, 1)
            else:
                dve.tensor_copy(qT[:, u, 4, :], TURN[:, 0:128])
                dve.tensor_copy(kT[:, u, 4, 0:nk], TURN[:, 128:128 + nk]).then_inc(turned_copied, 1)

        def reduce_max(j, u, c):
            dve.wait_ge(s_done, 5 * j + c + 1)
            src = S[(u + c) % 2][:, :].rearrange("p (g n) -> p g n", g=4)[:, :, 0:nk]
            dve.tensor_reduce(M.negmax[:, 4 * c:4 * c + 4], src, AX.X, ALU.max, negate=True).then_inc(s_reduced, 1)

        def copy_odd(i, u, c):
            dve.wait_ge(p_turned, 5 * i + c + 1)
            if not (isinstance(i, int) and i < 1):
                dve.wait_ge(pv_done, 5 * (i - 1) + c + 1)
            dve.tensor_copy(pT[0:nk, c, :], PT[(u + c) % 2][0:nk, :]).then_inc(pT_odd, 1)

        def reciprocals(i, u):
            dve.wait_ge(p_ready, 5 * (i + 1))
            if not (isinstance(i, int) and i < 1):
                dve.wait_ge(rec_turned, i)
            dve.reciprocal(rec[:, :], sums[:, u, :]).then_inc(rec_ready, 1)
            dve.wait_ge(rec_ready, 2 * i + 1)
            dve.tensor_copy(rec8[:, :].rearrange("p (n d) -> p n d", d=DH),
                            rec[:, :].unsqueeze(2).broadcast_to([N, H, DH])).then_inc(rec_ready, 1)

        def divide(i):
            dve.wait_ge(pv_done, 5 * (i + 1))
            dve.wait_ge(recT_ready, 2 * (i + 1))
            if not (isinstance(i, int) and i < 1):
                dve.wait_ge(o_done, i)
            dve.tensor_tensor(M.aT[:, 0:128], numA, recT[:, 0:128], ALU.mult).then_inc(aT_ready, 1)
            dve.tensor_tensor(M.aT[0:32, 128:256], numB, recT[0:32, 128:256], ALU.mult).then_inc(aT_ready, 1)

        def residual(i):
            dve.wait_ge(o_done, i + 1)
            dve.wait_ge(bias_added, i + 1)
            dve.tensor_tensor(M.X[:, i, :], QKV[:, 0:D], M.X[:, i, :], ALU.add).then_inc(x_ready, 1)

        def statistics(i, step):
            if step == 0:
                dve.wait_ge(x_ready, i + 1)
                hold(dve, M)
                dve.bn_stats(M.stats[:, 0, :], M.X[:, i, :]).then_inc(stats_done, 1)
            elif step == 1:
                dve.wait_ge(stats_done, i + 1)
                hold(dve, M)
                dve.bn_aggr(M.mv1[:, 0, :], M.stats[:, 0, :]).then_inc(means_done, 1)
            else:
                dve.wait_ge(means_done, 2 * i + 1)
                dve.tensor_copy(M.MV[:, i, :], M.mv1[:, 0, :]).then_inc(means_done, 1)

        for j in range(2):
            copy_hT(j)
            low_halves(j)
            for part in range(3):
                copy_turned(j, j, part)
        copy_hT(2)
        for c in range(5):
            reduce_max(0, 0, c)

        def stage(i, u, h, a, b):
            before = not (isinstance(i, int) and i < 1)
            for c in range(5):
                if c % 2:
                    copy_odd(i, u, c)
                if b:
                    reduce_max(i + 1, 1 - u, c)
                if c == 0:
                    reciprocals(i, u)
                if a and c == 1:
                    low_halves(i + 2)
                if before and c == 1:
                    divide(i - 1)
                if before and c == 4:
                    statistics(i - 1, 0)
                if a and c >= 2:
                    copy_turned(i + 2, u, c - 2)
                if before and c == 3:
                    residual(i - 1)
                if before and c == 4:
                    statistics(i - 1, 1)
                if h and c == 4:
                    copy_hT(i + 3)
                if before and c == 4:
                    statistics(i - 1, 2)

        pipeline(dve, stage)
        divide(B - 1)
        residual(B - 1)
        for step in range(3):
            statistics(B - 1, step)
        dve.wait_ge(means_done, 2 * B)

    @block.tensor
    def _(pe):
        def turn_h(j, u):
            pe.wait_ge(norm_step, NORM_STEPS * (j + 1))
            if not (isinstance(j, int) and j < 1):
                pe.wait_ge(hT_ready, 2 * j)
            if not (isinstance(j, int) and j < 3):
                pe.wait_ge(recT_ready, 2 * (j - 2))
            pe.transpose(TR[:, 0:128], M.h[:, u, 0:D0], M.ident[:, :])
            pe.transpose(TR[:, 128:256], M.hs[:, u].rearrange("p k d -> p (k d)").bitcast(F32), M.ident[:, :])\
              .then_inc(h_used, 1)

        def project(j, u):
            pe.wait_ge(hT_ready, 2 * (j + 1))
            if cross:
                pe.wait_ge(ctx_loaded[u], 16 * ((j - u) // 2 + 1) if isinstance(j, int) else ctx_count(j, u))
            if not (isinstance(j, int) and j < 1):
                pe.wait_ge(low_ready, 2 * j)
            if not (isinstance(j, int) and j < 4):
                pe.wait_ge(x_ready, j - 3)
            pe.matmul(QKV[:, 0:nq], M.hT[:, :], wq0[:, :], start=True, stop=False)
            last = pe.matmul(QKV[:, 0:nq], M.hsT[:, :], wqs[:, :], start=False, stop=True)
            if cross:
                last = pe.matmul(QKV[0:NC_, D:3 * D], M.ctxT[:, u, :], wkv[:, :], start=True, stop=True)
            last.then_inc(qkv_done, 1)

        def ctx_count(j, u):
            return 8 * j + (16 - 8 * u)

        def turn_stack(j, part):
            pe.wait_ge(low_ready, 2 * (j + 1))
            if part > 0 or not (isinstance(j, int) and j < 1):
                pe.wait_ge(turned_copied, 3 * j + part)
            blocks = [[(qs, g, g) for g in range(4)], [(ks, g, g) for g in range(4)], [(qs, 4, 0), (ks, 4, 1)]][part]
            for src, g, at in blocks:
                rows = N if src is qs else nk
                last = pe.transpose(TURN[:, 128 * at:128 * at + rows], src[0:rows, 128 * g:128 * g + 128].bitcast(F32),
                                    M.ident[0:rows, 0:rows])
            last.then_inc(turned, 1)

        def scores(j, u, c):
            if not (isinstance(j, int) and 5 * j + c < 2):
                pe.wait_ge(p_ready, 5 * j + c - 1)
            bank = S[(u + c) % 2]
            if c == 4:
                pe.wait_ge(blocks_ready, j + 1)
                last = pe.matmul(bank[:, :], qT[:, u, 4, :], kB[:, u].rearrange("p k n -> p (k n)"),
                                 start=True, stop=True)
            else:
                for g in range(4):
                    r = 32 * c
                    last = pe.matmul(bank[:, 128 * g:128 * g + nk], qT[r:r + 32, u, g, :], kT[r:r + 32, u, g, 0:nk],
                                     start=True, stop=True, tile_position=(r, 0))
            last.then_inc(s_done, 1)

        def turn_p(i, u, c):
            pe.wait_ge(p_ready, 5 * i + c + 1)
            if c >= 2:
                wait_pT(pe, i, c - 2)
            elif not (isinstance(i, int) and i < 1):
                wait_pT(pe, i - 1, c + 3)
            for k in range(4):
                last = pe.transpose(PT[(u + c) % 2][0:nk, 128 * k:128 * k + N], p[:, u, c, 128 * k:128 * k + nk],
                                    M.ident[:, :])
            last.then_inc(p_turned, 1)

        def turn_rec(i, j):
            pe.wait_ge(rec_ready, 2 * (i + 1))
            pe.wait_ge(hT_ready, 2 * j)
            pe.transpose(TR[:, 256:384], rec8[:, 0:D0], M.ident[:, :])
            pe.transpose(TR[0:32, 384:512], rec8[:, D0:D], M.ident[:, :]).then_inc(rec_turned, 1)

        def weighted(i, u, c):
            wait_pT(pe, i, c)
            if c == 0:
                pe.wait_ge(v_ready, i + 1)
                if not (isinstance(i, int) and i < 1):
                    pe.wait_ge(aT_ready, 2 * i)
            for k, n in enumerate(heads(c)):
                out = numA[32 * k:32 * k + 32, :] if c < 4 else numB
                last = pe.matmul(out, vpad[0:nk, u, n, :], pT[0:nk, c, 128 * k:128 * k + 128], start=(c == 0),
                                 stop=(c == 3 or (c == 4 and k == 3)), skip_group_check=True)
            last.then_inc(pv_done, 1)

        def project_out(i, j):
            pe.wait_ge(aT_ready, 2 * (i + 1))
            pe.wait_ge(low_ready, 2 * j)
            pe.matmul(QKV[:, 0:D], M.aT[:, 0:128], wo0[:, :], start=True, stop=False)
            pe.matmul(QKV[:, 0:D], M.aT[0:32, 128:256], wo1[:, :], start=False, stop=True).then_inc(o_done, 1)

        pe.wait_ge(w_split, 4)
        pe.wait_ge(weights.loaded, weights.count)
        for j in range(2):
            turn_h(j, j)
            project(j, j)
            for part in range(3):
                turn_stack(j, part)
        turn_h(2, 0)
        pe.wait_ge(turned_copied, 3)
        for c in range(5):
            scores(0, 0, c)

        def stage(i, u, h, a, b):
            for c in range(5):
                turn_p(i, u, c)
                if b and c == 0:
                    pe.wait_ge(turned_copied, 3 * (i + 1) + 2)
                if b and c == 4:
                    pe.wait_ge(turned_copied, 3 * (i + 2))
                if b:
                    scores(i + 1, 1 - u, c)
                if a and c == 0:
                    project(i + 2, u)
                if c == 1:
                    turn_rec(i, min(i + 3, B) if isinstance(i, int) else i + 3)
                if a and c >= 2:
                    turn_stack(i + 2, c - 2)
                if c >= 2:
                    weighted(i, u, c - 2)
                elif not (isinstance(i, int) and i < 1):
                    weighted(i - 1, 1 - u, c + 3)
                if c == 3 and not (isinstance(i, int) and i < 1):
                    project_out(i - 1, min(i + 3, B) if isinstance(i, int) else i + 3)
                if h and c == 3:
                    turn_h(i + 3, 1 - u)

        pipeline(pe, stage)
        weighted(B - 1, 1, 3)
        weighted(B - 1, 1, 4)
        project_out(B - 1, B)

    ctx.close()


def feed_forward(nc, ctx, M, weights):
    ctx = ctx.enter_context(ExitStack())
    G, Q = B // 4, 4

    def sb(name, shape, dt=F32):
        return ctx.enter_context(nc.sbuf_tensor(f"{name}_f", shape, dt))

    def sem(name):
        return ctx.enter_context(nc.semaphore(f"{name}_f"))

    w1, w1_raw, w2, b1 = weights.w1, weights.w1_raw, weights.w2, weights.b1
    w1s = sb("w1s", [128, 2 * FF], F32R)
    hT, hsT = sb("hT4", [128, 2, Q * N]), sb("hsT4", [128, 2, Q * N], F32R)
    gate, f = sb("gate", [128, 2, Q * N]), sb("f", [128, 2, FT, Q * N])
    w_split, norm_step, h_used, hT_ready, bias_added = (
        sem(n) for n in ("w_split", "norm_step", "h_used", "hT_ready", "bias_added"))
    up_done, gate_ready, f_ready, down_done, x_ready = (
        sem(n) for n in ("up_done", "gate_ready", "f_ready", "down_done", "x_ready"))
    A, GP, DOWN = M.ps[0:2], M.ps[2:4], M.ps[4:6]
    TR = M.ps[6]
    block = ctx.enter_context(nc.Block())

    def pipeline(eng, stage, last):
        stage(0, 0, True, True, False)
        stage(1, 1, True, True, True)
        with eng.Fori(1, G // 2 - 1) as half:
            for u in range(2):
                stage(2 * half + u, u, True, True, True)
        stage(G - 2, 0, True, True, True)
        stage(G - 1, 1, True, False, True)
        if last:
            stage(G, 0, False, False, True)

    @block.gpsimd
    def _(pool):

        def h_free(pool, j):
            if isinstance(j, int) and j < 2:
                return
            pool.wait_ge(h_used, j - 1)

        def ahead(j, u):
            normalise(pool, M, j, u, 4, norm_step, h_free)
            pool.wait_ge(norm_step, NORM_STEPS * (j + 1))
            hold(pool, M)
            pool.tensor_tensor(M.X[:, j, :], M.X[:, j, :], M.BIAS[:, 2, :], ALU.add).then_inc(bias_added, 1)

        ahead(0, 0)
        ahead(1, 1)
        with pool.Fori(1, B // 2) as half:
            for u in range(2):
                ahead(2 * half + u, u)

    @block.scalar
    def _(act):
        def copy_hT(k, u, q):
            act.wait_ge(h_used, Q * k + q + 1)
            if q == 0 and not (isinstance(k, int) and k < 2):
                act.wait_ge(up_done, FT * (k - 1))
            act.activation(hT[:, u, N * q:N * q + N], TR[:, 0:128], ACT.Copy).then_inc(hT_ready, 1)
            act.activation(hsT[:, u, N * q:N * q + N], TR[:, 128:256], ACT.Copy).then_inc(hT_ready, 1)

        def gelu(k, u, t):
            act.wait_ge(up_done, FT * k + t + 1)
            if not (isinstance(k, int) and FT * k + t < 2):
                act.wait_ge(f_ready, FT * k + t - 1)
            act.activation(gate[:, (u + t) % 2, :], GP[(u + t) % 2][:, :], ACT.Gelu, bias=b1[:, FT + t:FT + t + 1])\
               .then_inc(gate_ready, 1)

        act.wait_ge(weights.loaded, weights.count)
        for q in range(Q):
            copy_hT(0, 0, q)

        def stage(k, u, up, ahead, down):
            for t in range(FT):
                gelu(k, u, t)
                if ahead and t < Q:
                    copy_hT(k + 1, 1 - u, t)

        pipeline(act, stage, False)

    @block.vector
    def _(dve):
        dve.wait_ge(weights.loaded, weights.count)
        stack_weight(dve, w1_raw, w1s, 2 * FF, w_split, 0)

        def gated(k, u, t):
            dve.wait_ge(gate_ready, FT * k + t + 1)
            if t == 0 and not (isinstance(k, int) and k < 2):
                dve.wait_ge(down_done, Q * (k - 1))
            dve.scalar_tensor_tensor(f[:, u, t, :], A[(u + t) % 2][:, :], b1[:, t:t + 1], gate[:, (u + t) % 2, :],
                                     ALU.add, ALU.mult).then_inc(f_ready, 1)

        def residual(k, q):
            j = Q * k + q
            dve.wait_ge(down_done, j + 1)
            dve.wait_ge(bias_added, j + 1)
            dve.tensor_tensor(M.X[:, j, :], DOWN[q % 2][:, 0:D], M.X[:, j, :], ALU.add).then_inc(x_ready, 1)

        def stage(k, u, up, ahead, down):
            for t in range(FT):
                if up:
                    gated(k, u, t)
                if down and t < Q:
                    residual(k - 1, t)

        pipeline(dve, stage, True)

    @block.tensor
    def _(pe):
        def turn_h(k, q):
            j = Q * k + q
            pe.wait_ge(norm_step, NORM_STEPS * (j + 1))
            if not (isinstance(j, int) and j < 1):
                pe.wait_ge(hT_ready, 2 * j)
            pe.transpose(TR[:, 0:128], M.h[:, q % 2, 0:D0], M.ident[:, :])
            pe.transpose(TR[:, 128:256], M.hs[:, q % 2].rearrange("p k d -> p (k d)").bitcast(F32), M.ident[:, :])\
              .then_inc(h_used, 1)

        def up_tile(k, u, t):
            if t == 0:
                pe.wait_ge(hT_ready, 2 * Q * (k + 1))
            if not (isinstance(k, int) and FT * k + t < 2):
                pe.wait_ge(f_ready, FT * k + t - 1)
            for bank, at in ((GP, FF), (A, 0)):
                out, cols = bank[(u + t) % 2][:, :], slice(at + 128 * t, at + 128 * t + 128)
                pe.matmul(out, w1[:, cols], hT[:, u, :], start=True, stop=False)
                last = pe.matmul(out, w1s[:, cols], hsT[:, u, :], start=False, stop=True)
            last.then_inc(up_done, 1)

        def down(k, u, q):
            j = Q * k + q
            pe.wait_ge(f_ready, FT * (k + 1))
            if not (isinstance(j, int) and j < 2):
                pe.wait_ge(x_ready, j - 1)
            for t in range(FT):
                last = pe.matmul(DOWN[q % 2][:, 0:D], f[:, u, t, N * q:N * q + N], w2[:, t, :], start=(t == 0),
                                 stop=(t == FT - 1))
            last.then_inc(down_done, 1)

        pe.wait_ge(weights.loaded, weights.count)
        pe.wait_ge(w_split, 2)
        for q in range(Q):
            turn_h(0, q)

        def stage(k, u, up, ahead, down_):
            for t in range(FT):
                if up:
                    up_tile(k, u, t)
                if ahead and t < Q:
                    turn_h(k + 1, t)
                if down_ and t < Q:
                    down(k - 1, 1 - u, t)

        pipeline(pe, stage, True)

    ctx.close()


def second_block(nc, ctx, M, d, weights, out):
    ctx = ctx.enter_context(ExitStack())

    def sb(name, shape, dt=F32):
        return ctx.enter_context(nc.sbuf_tensor(f"{name}_l", shape, dt))

    def sem(name):
        return ctx.enter_context(nc.semaphore(f"{name}_l"))

    S2, T2 = 2, 128
    NCH = 8
    wqa_a, wqa_b, wk, wv, wvca = weights.wqa_a, weights.wqa_b, weights.wk, weights.wv, weights.wvca
    wout, E, vmask, wk2 = weights.wout, weights.E, weights.vmask, weights.wk2
    caq = sb("caq", [128, 2, C])
    ca32 = sb("ca32", [C, 32])
    p, pT = sb("p", [128, 2, NCH, 256]), sb("pT", [128, 4, 512])
    sums = sb("sums", [128, 2, 2 * HL])
    rec, rec32 = sb("rec", [128, 2 * HL]), sb("rec32", [128, 2, HL * 32])
    recT1, recT = sb("recT1", [128, S2 * C]), sb("recT", [128, S2 * T2])
    x1, xpad = sb("x1", [N, 2, D]), sb("xpad", [N, 2, HL, 32])
    xT = sb("xT", [LA, 2 * N])
    qk = sb("qk", [128, 2, S2 * T2 + S2 * NE])
    v, v2 = sb("v", [NE, 2, S2 * T2]), sb("v2", [32, 2, S2 * T2])
    p2, sum2, max2 = sb("p2", [C, 3, 32]), sb("sum2", [C, 2, HL]), sb("max2", [C, HL])
    p2T, hs1, hs, yt = sb("p2T", [32, N]), sb("hs1", [128, S2 * C]), sb("hs", [128, S2 * T2]), sb("yt", [N, 2, D])
    res = sb("res", [128, S2 * T2])

    zeroed = sem("zeroed")
    ctx_loaded = [sem("ctx_loaded0"), sem("ctx_loaded1")]
    x1_copied, xpad_copied, bias_added, ca32_ready = (
        sem(n) for n in ("x1_copied", "xpad_copied", "bias_added", "ca32_ready"))
    turned, xT_ready, qk_done, qk_ready, v_done, v_ready, v2_ready = (
        sem(n) for n in ("turned", "xT_ready", "qk_done", "qk_ready", "v_done", "v_ready", "v2_ready"))
    s_done, s_reduced, p_ready, p_turned, pT_even, pT_odd = (
        sem(n) for n in ("s_done", "s_reduced", "p_ready", "p_turned", "pT_even", "pT_odd"))
    rec_ready, rec_turned, recT_ready, pv_done, hs1_ready, hs_ready = (
        sem(n) for n in ("rec_ready", "rec_turned", "recT_ready", "pv_done", "hs1_ready", "hs_ready"))
    s2_done, max2_ready, e2_ready, sum2_ready, p2_ready, p2_turned, p2T_ready, ca2_done = (
        sem(n) for n in ("s2_done", "max2_ready", "e2_ready", "sum2_ready", "p2_ready", "p2_turned", "p2T_ready",
                         "ca2_done"))
    aT_ready, out_done, y_ready = sem("aT_ready"), sem("out_done"), sem("y_ready")
    stored = [sem("stored0"), sem("stored1")]

    S, PT = M.ps[0:2], M.ps[2:4]
    PV, PV1, TR, PRJ = M.ps[4:8]
    num, recT_ps, ca2_ps = PV[:, 0:S2 * T2], PV[:, 256:512], PV[:, 256:512]
    num1, recT1_ps = PV1[:, 0:S2 * C], PV1[:, 256:256 + S2 * C]
    s2_ps, p2T_ps = PV1[0:C, 0:32], PV1[0:32, 128:256]
    xT_ps = TR[:, 0:2 * N]
    scale = DL ** -0.5

    def pipeline(eng, stage):
        stage(0, 0, True, True)
        stage(1, 1, True, True)
        with eng.Fori(1, (B - 2) // 2) as half:
            for u in range(2):
                stage(2 * half + u, u, True, True)
        stage(B - 2, 0, False, True)
        stage(B - 1, 1, False, False)

    def first(j, n=1):
        return isinstance(j, int) and j < n

    def wait_pT(eng, i, t):
        eng.wait_ge(pT_odd if t % 2 else pT_even, 2 * i + t // 2 + 1)

    def copy_quad(copy, t):
        rows, cols = (N, C) if t < 2 else (NE, N)
        return copy(pT[0:rows, t, :].rearrange("p (k n) -> p k n", k=4)[:, :, 0:cols],
                    PT[t % 2][0:rows, :].rearrange("p (k n) -> p k n", k=4)[:, :, 0:cols])

    def loads_until(j, u):
        return 80 * ((j - u) // 2 + 1) if isinstance(j, int) else 40 * j + 80 - 40 * u

    block = ctx.enter_context(nc.Block())

    @block.sync
    def _(sp):
        def load_context(j, u):
            sp.dma_start(M.ctxT[:, u, :], d["ctxT"][j]).then_inc(ctx_loaded[u], 16)
            for r in range(4):
                sp.dma_start(caq[32 * r + DL:32 * r + DL + CA, u, :], d["ctx_768"][j, NE:NC_, :])\
                  .then_inc(ctx_loaded[u], 16)

        def write(i, u):
            sp.wait_ge(y_ready, i + 1)
            sp.dma_start(out[i], yt[:, u, :]).then_inc(stored[u], 16)

        sp.wait_ge(zeroed, 2)
        load_context(0, 0)
        load_context(1, 1)

        def stage(i, u, more):
            sp.wait_ge(v_done, i + 1)
            sp.wait_ge(s_done, NCH * i + 4)
            load_context(i + 2, u)
            if more:
                write(i - 1, 1 - u)

        stage(0, 0, False)
        stage(1, 1, True)
        with sp.Fori(1, (B - 2) // 2) as half:
            for u in range(2):
                stage(2 * half + u, u, True)
        write(B - 3, 1)
        write(B - 2, 0)
        write(B - 1, 1)
        for u in range(2):
            sp.wait_ge(stored[u], 8 * B)

    @block.gpsimd
    def _(pool):
        pool.memset(caq[:, :, :], 0.0).then_inc(zeroed, 1)
        pool.memset(xpad[:, :, :, :], 0.0).then_inc(zeroed, 1)
        pool.wait_ge(zeroed, 2)

        def copy_x1(j, u):
            if not first(j, 2):
                pool.wait_ge(turned, j - 1)
            hold(pool, M)
            pool.tensor_copy(x1[:, u, :], M.X[:, j, :]).then_inc(x1_copied, 1)

        def copy_xpad(j, u):
            if not first(j, 2):
                pool.wait_ge(pv_done, 4 * (j - 2) + 2)
            hold(pool, M)
            pool.tensor_copy(xpad[:, u, :, 0:DL], M.X[:, j, :].rearrange("p (n d) -> p n d", d=DL))\
                .then_inc(xpad_copied, 1)
            pool.wait_ge(x1_copied, j + 1)
            pool.wait_ge(xpad_copied, j + 1)
            hold(pool, M)
            pool.tensor_tensor(M.X[:, j, :], M.X[:, j, :], M.BIAS[:, 3, :], ALU.add).then_inc(bias_added, 1)

        def repeat_ca(j, u):
            pool.wait_ge(ctx_loaded[u], loads_until(j, u))
            if not first(j):
                pool.wait_ge(v_done, j)
            hold(pool, M)
            pool.tensor_copy(ca32[:, :].rearrange("p (n t) -> p n t", t=CA),
                             M.ctxT[:, u, NE:NC_].unsqueeze(1).broadcast_to([C, HL, CA])).then_inc(ca32_ready, 1)

        def ahead(j, u, more=True):
            copy_xpad(j, u)
            repeat_ca(j, u)
            if more:
                copy_x1(j + 1, 1 - u)

        copy_x1(0, 0)
        ahead(0, 0)
        ahead(1, 1)
        with pool.Fori(1, B // 2 - 1) as half:
            for u in range(2):
                ahead(2 * half + u, u)
        ahead(B - 2, 0)
        ahead(B - 1, 1, False)

    @block.scalar
    def _(act):
        def copy_qk(j, u):
            act.wait_ge(qk_done, j + 1)
            if not first(j, 2):
                act.wait_ge(s_done, NCH * (j - 1))
            act.activation(qk[:, u, 0:S2 * T2], PRJ[:, 0:S2 * T2], ACT.Copy, scale=scale)
            act.activation(qk[:, u, S2 * T2:], PRJ[:, S2 * T2:S2 * T2 + S2 * NE], ACT.Copy).then_inc(qk_ready, 1)

        def copy_v(j, u):
            act.wait_ge(v_done, j + 1)
            if not first(j, 2):
                act.wait_ge(pv_done, 4 * (j - 1))
            act.activation(v[:, u, :], PRJ[0:NE, 0:S2 * T2], ACT.Copy).then_inc(v_ready, 1)

        def exps(j, u, c):
            act.wait_ge(s_reduced, NCH * j + c + 1)
            if not first(j, 2):
                act.wait_ge(p_turned, 4 * (j - 2) + c // 2 + 1)
                if c == 0:
                    act.wait_ge(rec_ready, 4 * (j - 1))
            rows, cols = (C, N) if c < 4 else (N, NE)
            for m in (2 * c, 2 * c + 1):
                at = 128 * (m % 2)
                last = act.activation(p[0:rows, u, c, at:at + cols], S[c % 2][0:rows, at:at + cols], ACT.Exp,
                                      bias=M.negmax[0:rows, m:m + 1], accum_out=sums[0:rows, u, m:m + 1])
            last.then_inc(p_ready, 1)

        def copy_even(i, t):
            act.wait_ge(p_turned, 4 * i + t + 1)
            if not first(i):
                act.wait_ge(pv_done, 4 * (i - 1) + t + 1)
            copy_quad(lambda to, src: act.activation(to, src, ACT.Copy), t).then_inc(pT_even, 1)

        def copy_recT1(i):
            act.wait_ge(rec_turned, 2 * i + 1)
            if not first(i):
                act.wait_ge(hs1_ready, i)
            act.activation(recT1[:, :], recT1_ps, ACT.Copy).then_inc(recT_ready, 1)

        def copy_recT(i):
            act.wait_ge(rec_turned, 2 * i + 2)
            if not first(i):
                act.wait_ge(hs_ready, 2 * i - 1)
            act.activation(recT[:, :], recT_ps, ACT.Copy).then_inc(recT_ready, 1)

        def exp2(i):
            act.wait_ge(max2_ready, 2 * (i + 1))
            act.activation(p2[:, 1, :], p2[:, 0, :], ACT.Exp, scale=scale).then_inc(e2_ready, 1)

        def copy_p2T(i):
            act.wait_ge(p2_turned, i + 1)
            if not first(i):
                act.wait_ge(ca2_done, i)
            act.activation(p2T[:, :], p2T_ps, ACT.Copy).then_inc(p2T_ready, 1)

        for j in range(2):
            copy_qk(j, j)
            copy_v(j, j)
        for c in range(NCH):
            exps(0, 0, c)

        def stage(i, u, a, b):
            def exps_next(c):
                if b:
                    exps(i + 1, 1 - u, c)

            copy_even(i, 0)
            exps_next(0)
            if not first(i):
                copy_p2T(i - 1)
            exps_next(1)
            exps_next(2)
            copy_recT1(i)
            exps_next(3)
            copy_even(i, 2)
            exps_next(4)
            copy_recT(i)
            exps_next(5)
            exps_next(6)
            exp2(i)
            if a:
                copy_qk(i + 2, u)
            exps_next(7)
            if a:
                copy_v(i + 2, u)

        pipeline(act, stage)
        copy_p2T(B - 1)

    @block.vector
    def _(dve):
        dve.wait_ge(weights.loaded, weights.count)

        def copy_xT(j):
            dve.wait_ge(turned, j + 1)
            if not first(j):
                dve.wait_ge(qk_done, j)
            dve.tensor_copy(xT[:, 0:N], xT_ps[0:LA, 0:N]).then_inc(xT_ready, 1)
            dve.tensor_copy(xT[0:LB, N:2 * N], xT_ps[0:LB, N:2 * N]).then_inc(xT_ready, 1)

        def block_values(j, u):
            dve.wait_ge(v_ready, j + 1)
            if not first(j, 2):
                dve.wait_ge(ca2_done, j - 1)
            dve.tensor_tensor(v2[:, u, :], PRJ[0:32, S2 * T2:2 * S2 * T2], vmask[:, :], ALU.mult).then_inc(v2_ready, 1)

        def reduce_max(j, c):
            dve.wait_ge(s_done, NCH * j + c + 1)
            rows, cols = (C, N) if c < 4 else (N, NE)
            src = S[c % 2][0:rows, 0:256].rearrange("p (k n) -> p k n", k=2)[:, :, 0:cols]
            dve.tensor_reduce(M.negmax[0:rows, 2 * c:2 * c + 2], src, AX.X, ALU.max, negate=True).then_inc(s_reduced, 1)

        def copy_odd(i, t):
            dve.wait_ge(p_turned, 4 * i + t + 1)
            if not first(i):
                dve.wait_ge(pv_done, 4 * (i - 1) + t + 1)
            copy_quad(dve.tensor_copy, t).then_inc(pT_odd, 1)

        def reciprocals(i, u, main):
            dve.wait_ge(p_ready, NCH * i + 4 + 4 * main)
            if not first(i):
                dve.wait_ge(rec_turned, 2 * (i - 1) + main + 1)
            rows, mine = (N if main else C), slice(HL * main, HL * main + HL)
            dve.reciprocal(rec[0:rows, mine], sums[0:rows, u, mine]).then_inc(rec_ready, 1)
            dve.wait_ge(rec_ready, 4 * i + 2 * main + 1)
            dve.tensor_copy(rec32[0:rows, main, :].rearrange("p (n e) -> p n e", n=HL),
                            rec[0:rows, mine].unsqueeze(2).broadcast_to([rows, HL, 32])).then_inc(rec_ready, 1)

        def divide1(i):
            dve.wait_ge(pv_done, 4 * i + 2)
            dve.wait_ge(recT_ready, 2 * i + 1)
            if not first(i):
                dve.wait_ge(s2_done, i)
            dve.tensor_tensor(hs1[:, :], num1, recT1[:, :], ALU.mult).then_inc(hs1_ready, 1)

        def divide(i):
            dve.wait_ge(pv_done, 4 * (i + 1))
            dve.wait_ge(recT_ready, 2 * i + 2)
            if not first(i):
                dve.wait_ge(hs_ready, 2 * i)
            dve.tensor_tensor(hs[:, :], num, recT[:, :], ALU.mult).then_inc(hs_ready, 1)

        def less_max2(i):
            dve.wait_ge(s2_done, i + 1)
            if not first(i):
                dve.wait_ge(max2_ready, 2 * i)
            s2 = s2_ps.rearrange("p (n t) -> p n t", t=CA)
            dve.tensor_reduce(max2[:, :], s2, AX.X, ALU.max).then_inc(max2_ready, 1)
            dve.wait_ge(max2_ready, 2 * i + 1)
            dve.tensor_tensor(p2[:, 0, :].rearrange("p (n t) -> p n t", t=CA), s2,
                              max2[:, :].unsqueeze(2).broadcast_to([C, HL, CA]), ALU.subtract).then_inc(max2_ready, 1)

        def divide2(i):
            dve.wait_ge(e2_ready, i + 1)
            if not first(i):
                dve.wait_ge(p2_ready, i)
                dve.wait_ge(p2_turned, i)
            e2 = p2[:, 1, :].rearrange("p (n t) -> p n t", t=CA)
            dve.tensor_reduce(sum2[:, 0, :], e2, AX.X, ALU.add).then_inc(sum2_ready, 1)
            dve.wait_ge(sum2_ready, 2 * i + 1)
            dve.reciprocal(sum2[:, 1, :], sum2[:, 0, :]).then_inc(sum2_ready, 1)
            dve.wait_ge(sum2_ready, 2 * i + 2)
            dve.tensor_tensor(p2[:, 2, :].rearrange("p (n t) -> p n t", t=CA), e2,
                              sum2[:, 1, :].unsqueeze(2).broadcast_to([C, HL, CA]), ALU.mult).then_inc(p2_ready, 1)

        def add_branch(i):
            dve.wait_ge(ca2_done, i + 1)
            dve.wait_ge(hs_ready, 2 * i + 1)
            if not first(i):
                dve.wait_ge(out_done, i)
            dve.tensor_tensor(res[:, :], ca2_ps, hs[:, :], ALU.add).then_inc(hs_ready, 1)

        def result(i, u):
            dve.wait_ge(out_done, i + 1)
            dve.wait_ge(bias_added, i + 1)
            if not first(i, 2):
                dve.wait_ge(stored[u], 16 * ((i - u) // 2) if isinstance(i, int) else 8 * i - 8 * u)
            dve.tensor_tensor(yt[:, u, :], PRJ[:, 0:D], M.X[:, i, :], ALU.add).then_inc(y_ready, 1)

        copy_xT(0)
        block_values(0, 0)
        copy_xT(1)
        for c in range(NCH):
            reduce_max(0, c)

        def stage(i, u, a, b):
            def reduce_next(*chunks):
                for c in chunks if b else ():
                    reduce_max(i + 1, c)

            reciprocals(i, u, 0)
            reduce_next(0)
            reciprocals(i, u, 1)
            reduce_next(1)
            copy_odd(i, 1)
            reduce_next(2)
            if not first(i):
                add_branch(i - 1)
            if b:
                block_values(i + 1, 1 - u)
            if a:
                copy_xT(i + 2)
            reduce_next(3, 4)
            divide1(i)
            copy_odd(i, 3)
            reduce_next(5)
            if not first(i):
                result(i - 1, 1 - u)
            less_max2(i)
            reduce_next(6)
            divide(i)
            divide2(i)
            reduce_next(7)

        pipeline(dve, stage)
        add_branch(B - 1)
        result(B - 1, 1)

    @block.tensor
    def _(pe):
        def q_of(u, s, j):
            return qk[32 * j:32 * j + 32, u, T2 * s:T2 * s + N]

        def k_of(u, s, j):
            return qk[32 * j:32 * j + 32, u, S2 * T2 + NE * s:S2 * T2 + NE * s + NE]

        def turn(j, u):
            pe.wait_ge(x1_copied, j + 1)
            if not first(j):
                pe.wait_ge(xT_ready, 2 * j)
            pe.transpose(TR[0:LA, 0:N], x1[:, u, 0:LA], M.ident[:, :])
            pe.transpose(TR[0:LB, N:2 * N], x1[:, u, LA:D], M.ident[:, :]).then_inc(turned, 1)

        def project_qk(j, u):
            pe.wait_ge(xT_ready, 2 * (j + 1))
            pe.wait_ge(ctx_loaded[u], loads_until(j, u))
            if not first(j):
                pe.wait_ge(v2_ready, j)
            if not first(j, 3):
                pe.wait_ge(y_ready, j - 2)
            for s in range(S2):
                cols = slice(T2 * s, T2 * s + T2)
                pe.matmul(PRJ[:, cols], wqa_a[:, cols], xT[:, 0:N], start=True, stop=False)
                pe.matmul(PRJ[:, cols], wqa_b[:, cols], xT[0:LB, N:2 * N], start=False, stop=True)
            for s in range(S2):
                last = pe.matmul(PRJ[:, S2 * T2 + NE * s:S2 * T2 + NE * s + NE], wk[:, T2 * s:T2 * s + T2],
                                 M.ctxT[:, u, 0:NE], start=True, stop=True)
            last.then_inc(qk_done, 1)

        def project_v(j, u):
            pe.wait_ge(qk_ready, j + 1)
            pe.wait_ge(ca32_ready, j + 1)
            pe.matmul(PRJ[0:NE, 0:S2 * T2], M.ctxT[:, u, 0:NE], wv[:, :], start=True, stop=True)
            pe.matmul(PRJ[0:32, S2 * T2:2 * S2 * T2], ca32[:, :], wvca[:, :], start=True, stop=True).then_inc(v_done, 1)

        def scores(j, u, c):
            if not (isinstance(j, int) and NCH * j + c < 2):
                pe.wait_ge(p_ready, NCH * j + c - 1)
            bank, r = S[c % 2], c % 4
            if c < 4:
                last = pe.matmul(bank[0:C, 0:256], caq[32 * r:32 * r + 32, u, :], qk[32 * r:32 * r + 32, u, 0:256],
                                 start=True, stop=True, tile_position=(32 * r, 0))
            else:
                for s in range(S2):
                    last = pe.matmul(bank[:, 128 * s:128 * s + NE], q_of(u, s, r), k_of(u, s, r),
                                     start=True, stop=True, tile_position=(32 * r, 0))
            last.then_inc(s_done, 1)

        def turn_p(i, u, t):
            pe.wait_ge(p_ready, NCH * i + 2 * t + 2)
            if t >= 2:
                wait_pT(pe, i, t - 2)
            elif not first(i):
                wait_pT(pe, i - 1, t + 2)
            rows, cols = (N, C) if t < 2 else (NE, N)
            for k in range(4):
                at = 128 * (k % 2)
                last = pe.transpose(PT[t % 2][0:rows, 128 * k:128 * k + cols], p[0:cols, u, 2 * t + k // 2, at:at + rows],
                                    M.ident[0:cols, 0:cols])
            last.then_inc(p_turned, 1)

        def turn_rec1(i):
            pe.wait_ge(rec_ready, 4 * i + 2)
            if not first(i):
                pe.wait_ge(p2T_ready, i)
            for t in range(S2):
                last = pe.transpose(recT1_ps[:, C * t:C * t + C], rec32[0:C, 0, 128 * t:128 * t + 128], M.ident[0:C, 0:C])
            last.then_inc(rec_turned, 1)

        def turn_rec(i):
            pe.wait_ge(rec_ready, 4 * i + 4)
            if not first(i):
                pe.wait_ge(hs_ready, 2 * i)
            for t in range(S2):
                last = pe.transpose(recT_ps[:, T2 * t:T2 * t + T2], rec32[:, 1, 128 * t:128 * t + 128], M.ident[:, :])
            last.then_inc(rec_turned, 1)

        def weighted(i, u, t):
            wait_pT(pe, i, t)
            if t == 0:
                pe.wait_ge(xpad_copied, i + 1)
            if t % 2 == 0:
                pe.wait_ge(recT_ready, 2 * i + t // 2 + 1)
            branch, slot = t < 2, t % 2
            rows, cols = (N, C) if branch else (NE, N)
            out = num1 if branch else num
            for k in range(4):
                values = xpad[:, u, 4 * slot + k, :] if branch else v[:, u, T2 * slot + 32 * k:T2 * slot + 32 * k + 32]
                last = pe.matmul(out[32 * k:32 * k + 32, cols * slot:cols * slot + cols], values,
                                 pT[0:rows, t, 128 * k:128 * k + cols], start=True, stop=True)
            last.then_inc(pv_done, 1)

        def scores2(i):
            pe.wait_ge(hs1_ready, i + 1)
            for t in range(S2):
                last = pe.matmul(s2_ps, hs1[:, C * t:C * t + C], wk2[:, i, 32 * t:32 * t + 32], start=(t == 0),
                                 stop=(t == 1))
            last.then_inc(s2_done, 1)

        def turn_p2(i):
            pe.wait_ge(p2_ready, i + 1)
            pe.matmul(p2T_ps, p2[:, 2, :], E[:, :], start=True, stop=True).then_inc(p2_turned, 1)

        def weighted2(i, u):
            pe.wait_ge(p2T_ready, i + 1)
            pe.wait_ge(hs_ready, 2 * i + 1)
            for t in range(S2):
                last = pe.matmul(ca2_ps[:, T2 * t:T2 * t + T2], v2[:, u, T2 * t:T2 * t + T2], p2T[:, :], start=True,
                                 stop=True)
            last.then_inc(ca2_done, 1)

        def project_out(i, j):
            pe.wait_ge(hs_ready, 2 * (i + 1))
            pe.wait_ge(v2_ready, j)
            for t in range(S2):
                last = pe.matmul(PRJ[:, 0:D], res[:, T2 * t:T2 * t + T2], wout[:, t, :], start=(t == 0), stop=(t == 1))
            last.then_inc(out_done, 1)

        pe.wait_ge(weights.loaded, weights.count)
        for j in range(2):
            turn(j, j)
            project_qk(j, j)
            project_v(j, j)
        for c in range(NCH):
            scores(0, 0, c)

        def stage(i, u, a, b):
            def scores_next(c):
                if b:
                    scores(i + 1, 1 - u, c)

            turn_p(i, u, 0)
            scores_next(0)
            scores_next(1)
            if not first(i):
                turn_p2(i - 1)
            turn_p(i, u, 1)
            scores_next(2)
            if not first(i):
                weighted2(i - 1, 1 - u)
            turn_rec1(i)
            if a:
                turn(i + 2, u)
            scores_next(3)
            turn_p(i, u, 2)
            weighted(i, u, 0)
            weighted(i, u, 1)
            scores_next(4)
            turn_rec(i)
            turn_p(i, u, 3)
            if not first(i):
                project_out(i - 1, min(i + 2, B) if isinstance(i, int) else i + 2)
            scores_next(5)
            weighted(i, u, 2)
            scores2(i)
            scores_next(6)
            if a:
                project_qk(i + 2, u)
            weighted(i, u, 3)
            scores_next(7)
            if a:
                project_v(i + 2, u)

        pipeline(pe, stage)
        turn_p2(B - 1)
        weighted2(B - 1, 1)
        project_out(B - 1, B)

    ctx.close()


def layouts(given):
    import numpy as np

    def pairs(n):
        return 128 * (n % 2) + 32 * (n // 2)

    def fours(n):
        return 128 * (n // 4) + 32 * (n % 4)

    def padded(w, place):
        to = np.zeros((w.shape[0], 256), w.dtype)
        for n in range(HL):
            to[:, place(n):place(n) + DL] = w[:, DL * n:DL * n + DL]
        return to

    wqa = padded(given["L1_xattn_Wq"], pairs)
    spread = np.zeros((C, N), np.float32)
    kmask = np.zeros((D, HL * CA), np.float32)
    vmask = np.zeros((HL * CA, 256), np.float32)
    for n in range(HL):
        mine = slice(DL * n, DL * n + DL)
        wqa[mine, pairs(n) + DL:pairs(n) + DL + CA] = given["L1_xattn_Wq_ca"][:, mine].T
        kmask[mine, CA * n:CA * n + CA] = 1
        vmask[CA * n:CA * n + CA, fours(n):fours(n) + DL] = 1
    spread[np.linspace(0, C - 1, N).astype(np.int64), np.arange(N)] = 1
    return {
        "ctxT": given["ctx_768"].transpose(0, 2, 1),
        "caT": given["ctx_768"][:, NE:].transpose(2, 0, 1).reshape(C, B * CA),
        "ff_b1T": given["L0_xattn_ff_b1"].reshape(2 * FT, 128).T,
        "wqa": wqa,
        "l_wk": padded(given["L1_xattn_Wk"], pairs),
        "l_wv": padded(given["L1_xattn_Wv"], fours),
        "l_wvca": padded(given["L1_xattn_Wv_ca"], fours),
        "l_wqT": padded(given["L1_xattn_Wq"].T, fours),
        "l_wout": padded(given["L1_xattn_Wout"].T, fours).T.reshape(2, 128, D).transpose(1, 0, 2),
        "spread": spread, "kmask": kmask, "vmask": vmask,
    }


def build(nc, d, out):
    ctx = ExitStack()
    with ctx:
        M = Memory(nc, ctx)
        first, second = AttentionWeights(nc, ctx, False), AttentionWeights(nc, ctx, True)
        ff, last = FeedForwardWeights(nc, ctx), SecondWeights(nc, ctx)
        with ExitStack() as scope:
            setup(nc, scope, M, d, (first, second, ff, last), last.wk2)
        attention(nc, ctx, M, d, first)
        attention(nc, ctx, M, d, second)
        feed_forward(nc, ctx, M, ff)
        second_block(nc, ctx, M, d, last, out)


def kernel(**inputs):
    import numpy as np
    import concourse.bacc as bacc
    from concourse.bass_utils import run_bass_kernel_spmd

    nc = bacc.Bacc("TRN2", target_bir_lowering=False, num_devices=1)
    given = {name: np.ascontiguousarray(a) for name, a in inputs.items()}
    laid = layouts(given)
    arrays = {"in_" + name: np.ascontiguousarray(a) for name, a in {**given, **laid}.items()}
    d = {name[3:]: nc.dram_tensor(name, a.shape, mybir.dt.from_np(a.dtype), kind="ExternalInput").ap()
         for name, a in arrays.items()}
    out = nc.dram_tensor("out_0", (B, N, D), F32, kind="ExternalOutput").ap()
    build(nc, d, out)
    return run_bass_kernel_spmd(nc, [arrays], core_ids=[0]).results[0]["out_0"]
```
